# Optimizing a Trainium2 kernel written in Bass

```python
import numpy as np
import jax
import jax.numpy as jnp

def _softmax(x, axis=-1):
    return jax.nn.softmax(x, axis=axis)

def _gelu(x):
    return jax.nn.gelu(x, approximate=True)

def _silu(x):
    return jax.nn.silu(x)

def _sigmoid(x):
    return jax.nn.sigmoid(x)

def _layernorm(x, axis=-1, eps=1e-05):
    m = jnp.mean(x, axis=axis, keepdims=True)
    v = jnp.var(x, axis=axis, keepdims=True)
    return (x - m) / jnp.sqrt(v + eps)

def _scatter_add(tgt, idx, src, axis=0):
    return tgt.at[idx].add(src)

def _segment_sum(src, seg, n):
    return jax.ops.segment_sum(src, seg, n)
kernel_name = 'mk_early_fusion_d1_tok_img256_r4_9b449a'

def setup_inputs(seed: int=0):
    np.random.seed(seed)
    _w = jnp.asarray

    def _rec_inputs():
        import jax
        import jax.numpy as jnp
        _rk = jax.random.key(seed)
        x = -0.000928989 + 1.00043 * jax.random.normal(jax.random.fold_in(_rk, 1), (128, 64, 64, 1), jnp.float32)
        txt = -0.0645857 + 1.41221 * jax.random.normal(jax.random.fold_in(_rk, 2), (128, 32, 64), jnp.float32)
        return (x, txt)
    x, txt = _rec_inputs()

    def _L0_tok_setup():
        import jax, jax.numpy as jnp
        import numpy as np
        L = 4
        M1 = 12
        M2 = 12
        BN_EPS = 1e-05

        def _fourier_layer(v, W1, W2):
            B, C, Sx, Sy = v.shape
            x_ft = jnp.fft.rfft2(v)
            out1 = jnp.einsum('bixy,ioxy->boxy', x_ft[:, :, :M1, :M2], W1)
            out2 = jnp.einsum('bixy,ioxy->boxy', x_ft[:, :, -M1:, :M2], W2)
            out_ft = jnp.zeros((B, C, Sx, Sy // 2 + 1), jnp.complex64)
            out_ft = out_ft.at[:, :, :M1, :M2].set(out1)
            out_ft = out_ft.at[:, :, Sx - M1:, :M2].set(out2)
            return jnp.fft.irfft2(out_ft, s=(Sx, Sy))
        key = jax.random.key(seed)
        ks = jax.random.split(key, 10)
        B, S, d_a, d_v, d_u = (16, 64, 3, 32, 1)
        return {'x': jax.random.normal(ks[0], (B, S, S, 1), jnp.float32), 'p_w': jax.random.normal(ks[1], (d_a, d_v), jnp.float32) * 0.3, 'p_b': jax.random.normal(ks[2], (d_v,), jnp.float32) * 0.1, 'fw1': jax.random.normal(ks[3], (L, d_v, d_v, M1, M2, 2), jnp.float32) * (1.0 / d_v), 'fw2': jax.random.normal(ks[4], (L, d_v, d_v, M1, M2, 2), jnp.float32) * (1.0 / d_v), 'w_w': jax.random.normal(ks[5], (L, d_v, d_v), jnp.float32) * (1.0 / np.sqrt(d_v)), 'w_b': jax.random.normal(ks[6], (L, d_v), jnp.float32) * 0.1, 'bn_g': jnp.ones((L, d_v), jnp.float32), 'bn_b': jnp.zeros((L, d_v), jnp.float32), 'q_w': jax.random.normal(ks[7], (d_v, d_u), jnp.float32) * 0.3, 'q_b': jax.random.normal(ks[8], (d_u,), jnp.float32) * 0.1}
    _L0_tok_all = _L0_tok_setup()
    _L0_tok_in = {k: v for k, v in _L0_tok_all.items() if k in ('p_w', 'p_b', 'fw1', 'fw2', 'w_w', 'w_b', 'bn_g', 'bn_b', 'q_w', 'q_b')}
    del _L0_tok_all

    def _L0_attn_setup():
        import jax, jax.numpy as jnp
        import numpy as np
        U_DECAY = 0.97
        X_DECAY = 0.97
        LN_EPS = 1e-05
        L1_EPS = 1e-12

        def _ln(x):
            m = jnp.mean(x, axis=-1, keepdims=True)
            v = jnp.mean((x - m) ** 2, axis=-1, keepdims=True)
            return (x - m) * jax.lax.rsqrt(v + LN_EPS)
        key = jax.random.key(seed)
        k0, k1, k2, k3 = jax.random.split(key, 4)
        B, T, d, n = (8, 64, 64, 256)
        embeddings = jax.random.normal(k0, (B, T, d), dtype=jnp.float32)
        E = jax.random.normal(k1, (d, n), dtype=jnp.float32) / n ** 0.5
        Dx = jax.random.normal(k2, (n, d), dtype=jnp.float32) / d ** 0.5
        Dy = jax.random.normal(k3, (n, d), dtype=jnp.float32) / d ** 0.5
        return {'embeddings': embeddings, 'E': E, 'Dx': Dx, 'Dy': Dy}
    _L0_attn_all = _L0_attn_setup()
    _L0_attn_in = {k: v for k, v in _L0_attn_all.items() if k in ('E', 'Dx', 'Dy')}
    del _L0_attn_all

    def _L0_ffn_setup():
        import jax, jax.numpy as jnp
        import numpy as np
        B, S, D, F, E, K = (8, 512, 64, 256, 8, 2)
        key = jax.random.key(seed)
        ks = jax.random.split(key, 10)
        s = 0.02
        return {'x': jax.random.normal(ks[0], (B, S, D), dtype=jnp.float32), 'Wr': jax.random.normal(ks[1], (D, E), dtype=jnp.float32) * s, 'W1s': jax.random.normal(ks[2], (D, F), dtype=jnp.float32) * s, 'b1s': jnp.zeros((F,), dtype=jnp.float32), 'W2s': jax.random.normal(ks[3], (F, D), dtype=jnp.float32) * s, 'b2s': jnp.zeros((D,), dtype=jnp.float32), 'W1p': jax.random.normal(ks[4], (E, D, F), dtype=jnp.float32) * s, 'b1p': jnp.zeros((E, F), dtype=jnp.float32), 'W2p': jax.random.normal(ks[5], (E, F, D), dtype=jnp.float32) * s, 'b2p': jnp.zeros((E, D), dtype=jnp.float32)}
    _L0_ffn_all = _L0_ffn_setup()
    _L0_ffn_in = {k: v for k, v in _L0_ffn_all.items() if k in ('Wr', 'W1s', 'b1s', 'W2s', 'b2s', 'W1p', 'b1p', 'W2p', 'b2p')}
    del _L0_ffn_all
    return {'x': x, 'txt': txt, 'L0_tok_p_w': _L0_tok_in['p_w'], 'L0_tok_p_b': _L0_tok_in['p_b'], 'L0_tok_fw1': _L0_tok_in['fw1'], 'L0_tok_fw2': _L0_tok_in['fw2'], 'L0_tok_w_w': _L0_tok_in['w_w'], 'L0_tok_w_b': _L0_tok_in['w_b'], 'L0_tok_bn_g': _L0_tok_in['bn_g'], 'L0_tok_bn_b': _L0_tok_in['bn_b'], 'L0_tok_q_w': _L0_tok_in['q_w'], 'L0_tok_q_b': _L0_tok_in['q_b'], 'L0_attn_E': _L0_attn_in['E'], 'L0_attn_Dx': _L0_attn_in['Dx'], 'L0_attn_Dy': _L0_attn_in['Dy'], 'L0_ffn_Wr': _L0_ffn_in['Wr'], 'L0_ffn_W1s': _L0_ffn_in['W1s'], 'L0_ffn_b1s': _L0_ffn_in['b1s'], 'L0_ffn_W2s': _L0_ffn_in['W2s'], 'L0_ffn_b2s': _L0_ffn_in['b2s'], 'L0_ffn_W1p': _L0_ffn_in['W1p'], 'L0_ffn_b1p': _L0_ffn_in['b1p'], 'L0_ffn_W2p': _L0_ffn_in['W2p'], 'L0_ffn_b2p': _L0_ffn_in['b2p']}

def reference(x, txt, L0_tok_p_w, L0_tok_p_b, L0_tok_fw1, L0_tok_fw2, L0_tok_w_w, L0_tok_w_b, L0_tok_bn_g, L0_tok_bn_b, L0_tok_q_w, L0_tok_q_b, L0_attn_E, L0_attn_Dx, L0_attn_Dy, L0_ffn_Wr, L0_ffn_W1s, L0_ffn_b1s, L0_ffn_W2s, L0_ffn_b2s, L0_ffn_W1p, L0_ffn_b1p, L0_ffn_W2p, L0_ffn_b2p):
    import jax
    import jax.numpy as jnp

    def _L0_tok_ref(x, p_w, p_b, fw1, fw2, w_w, w_b, bn_g, bn_b, q_w, q_b):
        import jax, jax.numpy as jnp
        import numpy as np
        L = 4
        M1 = 12
        M2 = 12
        BN_EPS = 1e-05

        def _fourier_layer(v, W1, W2):
            B, C, Sx, Sy = v.shape
            x_ft = jnp.fft.rfft2(v)
            out1 = jnp.einsum('bixy,ioxy->boxy', x_ft[:, :, :M1, :M2], W1)
            out2 = jnp.einsum('bixy,ioxy->boxy', x_ft[:, :, -M1:, :M2], W2)
            out_ft = jnp.zeros((B, C, Sx, Sy // 2 + 1), jnp.complex64)
            out_ft = out_ft.at[:, :, :M1, :M2].set(out1)
            out_ft = out_ft.at[:, :, Sx - M1:, :M2].set(out2)
            return jnp.fft.irfft2(out_ft, s=(Sx, Sy))
        B, Sx, Sy, _ = x.shape
        gx = jnp.broadcast_to(jnp.linspace(0.0, 1.0, Sx, dtype=jnp.float32)[None, :, None, None], (B, Sx, Sy, 1))
        gy = jnp.broadcast_to(jnp.linspace(0.0, 1.0, Sy, dtype=jnp.float32)[None, None, :, None], (B, Sx, Sy, 1))
        h = jnp.concatenate([x, gx, gy], axis=-1)
        v = h @ p_w + p_b
        v = jnp.transpose(v, (0, 3, 1, 2))
        for i in range(L):
            W1 = fw1[i, ..., 0] + 1j * fw1[i, ..., 1]
            W2 = fw2[i, ..., 0] + 1j * fw2[i, ..., 1]
            x1 = _fourier_layer(v, W1, W2)
            x2 = jnp.einsum('bcxy,cd->bdxy', v, w_w[i]) + w_b[i][None, :, None, None]
            v = x1 + x2
            mean = jnp.mean(v, axis=(0, 2, 3), keepdims=True)
            var = jnp.var(v, axis=(0, 2, 3), keepdims=True)
            v = (v - mean) * jax.lax.rsqrt(var + BN_EPS)
            v = v * bn_g[i][None, :, None, None] + bn_b[i][None, :, None, None]
            if i < L - 1:
                v = jax.nn.relu(v)
        out = jnp.einsum('bcxy,cu->bxyu', v, q_w) + q_b
        return jnp.squeeze(out)

    def _L0_attn_ref(embeddings, E, Dx, Dy):
        import jax, jax.numpy as jnp
        import numpy as np
        U_DECAY = 0.97
        X_DECAY = 0.97
        LN_EPS = 1e-05
        L1_EPS = 1e-12

        def _ln(x):
            m = jnp.mean(x, axis=-1, keepdims=True)
            v = jnp.mean((x - m) ** 2, axis=-1, keepdims=True)
            return (x - m) * jax.lax.rsqrt(v + LN_EPS)
        B, T, d = embeddings.shape
        n = E.shape[1]

        def step(carry, v_prev):
            x_state, rho = carry
            x_update = jax.nn.relu(v_prev @ Dx.T)
            x_t = X_DECAY * x_state + x_update
            x_t = x_t / jnp.maximum(jnp.sum(jnp.abs(x_t), axis=-1, keepdims=True), L1_EPS)
            a_star = jnp.einsum('bdn,bn->bd', rho, x_t)
            y_core = _ln(a_star) @ Dy.T
            y_t = jax.nn.relu(y_core) * jax.nn.relu(x_t)
            v_star = _ln(y_t @ E.T)
            rho_t = U_DECAY * rho + _ln(v_prev)[:, :, None] * x_t[:, None, :]
            return ((x_t, rho_t), v_star)
        x0 = jnp.zeros((B, n), dtype=embeddings.dtype)
        rho0 = jnp.zeros((B, d, n), dtype=embeddings.dtype)
        _, vs = jax.lax.scan(step, (x0, rho0), jnp.swapaxes(embeddings, 0, 1))
        return jnp.swapaxes(vs, 0, 1)

    def _L0_ffn_ref(x, Wr, W1s, b1s, W2s, b2s, W1p, b1p, W2p, b2p):
        import jax, jax.numpy as jnp
        import numpy as np
        B, S, D, F, E, K = (8, 512, 64, 256, 8, 2)
        gelu = lambda t: jax.nn.gelu(t, approximate=False)
        shared = gelu(x @ W1s + b1s) @ W2s + b2s
        rw = jax.nn.softmax(x @ Wr, axis=-1)
        topw, topi = jax.lax.top_k(rw, K)
        topw = topw / jnp.sum(topw, axis=-1, keepdims=True)
        mask = jnp.sum(jax.nn.one_hot(topi, E, dtype=topw.dtype) * topw[..., None], axis=-2)
        h = gelu(jnp.einsum('bsd,edf->bsef', x, W1p) + b1p)
        priv = jnp.einsum('bsef,efd->bsed', h, W2p) + b2p
        routed = jnp.einsum('bsed,bse->bsd', priv, mask)
        return shared + routed
    h = _L0_tok_ref(x, L0_tok_p_w, L0_tok_p_b, L0_tok_fw1, L0_tok_fw2, L0_tok_w_w, L0_tok_w_b, L0_tok_bn_g, L0_tok_bn_b, L0_tok_q_w, L0_tok_q_b)
    h = jnp.concatenate([h, txt], axis=1)
    h = h + _L0_attn_ref(_layernorm(h, axis=-1), L0_attn_E, L0_attn_Dx, L0_attn_Dy)
    h = h + _L0_ffn_ref(_layernorm(h, axis=-1), L0_ffn_Wr, L0_ffn_W1s, L0_ffn_b1s, L0_ffn_W2s, L0_ffn_b2s, L0_ffn_W1p, L0_ffn_b1p, L0_ffn_W2p, L0_ffn_b2p)
    return h

_drawn_inputs = setup_inputs


def setup_inputs(seed=0):
    import zlib

    import numpy as np

    out = dict(_drawn_inputs(seed))
    spreads = {'L0_tok_bn_g': (1.0, 0.2),
     'L0_tok_bn_b': (0.0, 0.1),
     'L0_ffn_b1s': (0.0, 0.8),
     'L0_ffn_b2s': (0.0, 0.1),
     'L0_ffn_b1p': (0.0, 0.8),
     'L0_ffn_b2p': (0.0, 0.1)}
    factors = {'L0_tok_p_b': 8.0,
     'L0_tok_w_b': 8.0,
     'L0_ffn_W1s': 3.651,
     'L0_ffn_W2s': 2.992,
     'L0_ffn_W1p': 5.174,
     'L0_ffn_W2p': 4.398}
    for name, (base, spread) in spreads.items():
        noise = np.random.default_rng([zlib.crc32(name.encode()), seed]).standard_normal(out[name].shape)
        drawn = base * np.exp(spread * noise) if base else spread * noise
        out[name] = jnp.asarray(drawn.astype(out[name].dtype))
    for name, factor in factors.items():
        out[name] = (out[name] * factor).astype(out[name].dtype)
    return out
```

```python
from contextlib import ExitStack

import numpy as np

import concourse.bass as bass
from concourse import mybir

F32 = mybir.dt.float32
ALU = mybir.AluOpType
ACT = mybir.ActivationFunctionType
AX = mybir.AxisListType

P = 128
S = 64
C = 32
G = P // C
PX = S * S
M1 = M2 = 12
KX = 2 * M1
MODES = M1 * M2
SPEC = 2 * 2 * MODES
CH = 512
NCH = PX // CH
EPS = 1e-5
DECAY = 0.97


def shape_constants():
    f = np.float64
    ang = 2 * np.pi / S
    y = np.arange(S, dtype=f)
    ky = np.arange(M2, dtype=f)
    kx = np.concatenate([np.arange(M1), np.arange(S - M1, S)]).astype(f).reshape(2, M1)
    row = np.stack([np.cos(ang * np.outer(y, ky)), -np.sin(ang * np.outer(y, ky))], -1)
    dfty = np.kron(np.eye(2), row.reshape(S, 2 * M2))
    x = np.arange(S, dtype=f)
    th = ang * x[:, None, None] * kx[None]
    c, s = np.cos(th), np.sin(th)
    dftx = np.zeros((S, 2, 2, 2, M1))
    dftx[:, 0, :, 0], dftx[:, 1, :, 0] = c, s
    dftx[:, 0, :, 1], dftx[:, 1, :, 1] = -s, c
    idftx = np.zeros((2, 2, M1, S, 2))
    ct, st = c.transpose(1, 2, 0) / S, s.transpose(1, 2, 0) / S
    idftx[:, 0, :, :, 0], idftx[:, 1, :, :, 0] = ct, -st
    idftx[:, 0, :, :, 1], idftx[:, 1, :, :, 1] = st, ct
    wt = np.where(ky == 0, 1.0, 2.0)[:, None] / S
    inv = np.stack([wt * np.cos(ang * np.outer(ky, y)), -wt * np.sin(ang * np.outer(ky, y))], 1)
    inv[0, 1] = 0.0
    idfty = np.kron(np.eye(4), inv.reshape(2 * M2, S))
    lin = np.linspace(0.0, 1.0, S, dtype=np.float32)
    planes = np.stack([np.broadcast_to(lin[:, None], (S, S)), np.broadcast_to(lin[None], (S, S)), np.ones((S, S))])
    ft = np.fft.fft2(planes.astype(f))[:, kx.astype(int)][..., :M2]
    ft = np.stack([ft.real, ft.imag], 2).transpose(1, 2, 0, 4, 3)
    out = {
        "dfty": dfty, "dftx": dftx.reshape(2 * S, 2 * KX), "idftx": idftx.reshape(2 * KX, 2 * S), "idfty": idfty,
        "eye": np.eye(P), "groupmean": np.tile(np.eye(C), (G, G)) / G,
        "grid_px": np.repeat(planes.reshape(3, PX), G, 0),
        "grid_ft": ft.reshape(2, 2, 3, MODES),
    }
    return {k: np.ascontiguousarray(v, dtype=np.float32) for k, v in out.items()}


def at_least(eng, sem, value):
    if isinstance(value, int) and value <= 0:
        return
    eng.wait_ge(sem, value)


def walk(eng, n, body):
    if n == 1:
        body(0, 0, 0, True)
        return
    body(0, 0, 0, False)
    body(1, 1, 0, n == 2)
    if n > 4:
        with eng.Fori(1, n // 2 - 1) as m:
            body(2 * m, 0, m, False)
            body(2 * m + 1, 1, m, False)
    if n > 2:
        body(n - 2, 0, n // 2 - 1, False)
        body(n - 1, 1, n // 2 - 1, True)


class Semaphores:

    def __init__(self, ctx, nc):
        def sem(name):
            return ctx.enter_context(nc.semaphore(name))

        self.in_a = sem("in_a")
        self.par_in = sem("par_in")
        self.const_in = sem("const_in")
        self.u_in0 = sem("u_in0")
        self.u_in1 = sem("u_in1")
        self.y_in0 = sem("y_in0")
        self.y_in1 = sem("y_in1")
        self.bn_done = sem("bn_done")
        self.tr_done = sem("tr_done")
        self.vt_ready = sem("vt_ready")
        self.fy_done = sem("fy_done")
        self.a_ready = sem("a_ready")
        self.t2_done = sem("t2_done")
        self.a2_ready = sem("a2_ready")
        self.fx_done = sem("fx_done")
        self.sp_ready = sem("sp_ready")
        self.sp_out0 = sem("sp_out0")
        self.sp_out1 = sem("sp_out1")
        self.w_in = sem("w_in")
        self.w_fix = sem("w_fix")
        self.mix_done = sem("mix_done")
        self.mix_low = sem("mix_low")
        self.mix_high = sem("mix_high")
        self.y_out0 = sem("y_out0")
        self.y_out1 = sem("y_out1")
        self.ix_done = sem("ix_done")
        self.s_ready = sem("s_ready")
        self.tt_done = sem("tt_done")
        self.t_ready = sem("t_ready")
        self.um_done = sem("um_done")
        self.uo_ready = sem("uo_ready")
        self.st_done = sem("st_done")
        self.u_out0 = sem("u_out0")
        self.u_out1 = sem("u_out1")
        self.step = sem("step")
        self.aggr = sem("aggr")
        self.pe_step = sem("pe_step")
        self.act_step = sem("act_step")
        self.hq_done = sem("hq_done")
        self.hq_ready = sem("hq_ready")
        self.hq_out0 = sem("hq_out0")
        self.hq_out1 = sem("hq_out1")
        self.pw_done = sem("pw_done")
        self.pw_ready = sem("pw_ready")
        self.range = range(self.in_a.num, self.pw_ready.num + 1)


def end_phase(nc, sems):
    nc.gpsimd.sem_clear(sems.range)
    nc.all_engine_barrier()


def forward_phase(nc, sems, tag, K, source, n, spectrum, scale_bias, load_weights):
    s = sems
    with ExitStack() as ctx:
        u = ctx.enter_context(nc.sbuf_tensor(f"f_u{tag}", [P, 2, PX], F32))
        vt = ctx.enter_context(nc.sbuf_tensor(f"f_vt{tag}", [P, 2, CH], F32))
        ya = ctx.enter_context(nc.sbuf_tensor(f"f_ya{tag}", [P, 2, M2, S, 2], F32))
        yt = ctx.enter_context(nc.sbuf_tensor(f"f_yt{tag}", [P, 2, M2, P], F32))
        sp = ctx.enter_context(nc.sbuf_tensor(f"f_sp{tag}", [P, 2, SPEC], F32))
        ps_tr = [ctx.enter_context(nc.psum_tensor(f"f_tr{b}{tag}", [P, CH], F32)) for b in range(2)]
        ps_a = [ctx.enter_context(nc.psum_tensor(f"f_a{b}{tag}", [P, CH], F32)) for b in range(2)]
        ps_t = [ctx.enter_context(nc.psum_tensor(f"f_t{b}{tag}", [P, CH], F32)) for b in range(2)]
        ps_s = [ctx.enter_context(nc.psum_tensor(f"f_s{b}{tag}", [P, CH], F32)) for b in range(2)]
        u_in, sp_out = [s.u_in0, s.u_in1], [s.sp_out0, s.sp_out1]
        block = ctx.enter_context(nc.Block())

        @block.sync
        def _(sp_eng):
            load_weights(sp_eng)

            def store(i, par):
                at_least(sp_eng, s.sp_ready, 2 * i + 2)
                sp_eng.dma_start(spectrum(i), sp[:, par]).then_inc(sp_out[par], 16)

            def body(i, par, r, last):
                at_least(sp_eng, s.tr_done, NCH * (i - 1))
                sp_eng.dma_start(u[:, par], source(i)).then_inc(u_in[par], 16)
                if not (isinstance(i, int) and i < 2):
                    store(i - 2, par)

            walk(sp_eng, n, body)
            sp_eng.wait_ge(s.w_in, 64)
            for i in range(max(n - 2, 0), n):
                store(i, i % 2)
            sp_eng.wait_ge(s.sp_out0, 16 * ((n + 1) // 2))
            if n > 1:
                sp_eng.wait_ge(s.sp_out1, 16 * (n // 2))

        @block.gpsimd
        def _(pool):
            turn_weights(pool, nc, s, K)

        def spectrum_out(act, i, par, r):
            if isinstance(r, int) and r == 0:
                pass
            else:
                act.wait_ge(sp_out[par], 16 * r)
            for hh in range(2):
                act.wait_ge(s.fx_done, 2 * i + hh + 1)
                src = ps_s[hh][:, 0:6 * 48].rearrange("p (k c x) -> p c k x", k=6, c=4)
                dst = sp[:, par].rearrange("p (c k x) -> p c k x", c=4, k=M2)[:, :, 6 * hh:6 * hh + 6, :]
                for c in range(4):
                    ins = nc.scalar.copy(dst[:, c], src[:, c])
                ins.then_inc(s.sp_ready, 1)

        @block.scalar
        def _(act):
            def body(i, par, r, last):
                act.wait_ge(u_in[par], 16 * r + 16)
                for k in range(4):
                    px = u[:, par, 1024 * k:1024 * k + 1024]
                    if scale_bias is None:
                        nc.scalar.copy(px, px).then_inc(s.bn_done, 1)
                    else:
                        nc.scalar.activation(px, px, ACT.Relu, bias=scale_bias[1], scale=scale_bias[0])\
                            .then_inc(s.bn_done, 1)
                for q in range(NCH // 2):
                    if q == 2 and not (isinstance(i, int) and i == 0):
                        spectrum_out(act, i - 1, 1 - par, r - 1 if par == 0 else r)
                    act.wait_ge(s.fy_done, NCH * i + 2 * q + 2)
                    at_least(act, s.t2_done, 3 * (i - 1))
                    dst = ya[:, par, :, 16 * q:16 * q + 16, :].rearrange("p k x r -> p x k r")
                    src = ps_a[q % 2][:, 0:384].rearrange("p (x k r) -> p x k r", x=16, r=2)
                    nc.scalar.copy(dst, src).then_inc(s.a_ready, 1)
                if last:
                    spectrum_out(act, i, par, r)

            walk(act, n, body)

        def second_turn(dve, i, par):
            for j in range(3):
                b = (3 * par + j) % 2
                dve.wait_ge(s.t2_done, 3 * i + j + 1)
                at_least(dve, s.fx_done, 2 * (i - 1))
                nc.vector.tensor_copy(yt[:, par, 4 * j:4 * j + 4, :], ps_t[b][:, :]).then_inc(s.a2_ready, 1)

        @block.vector
        def _(dve):
            def body(i, par, r, last):
                for k in range(NCH):
                    c = NCH * i + k
                    dve.wait_ge(s.tr_done, c + 1)
                    at_least(dve, s.fy_done, c - 1)
                    nc.vector.tensor_copy(vt[:, k % 2, :], ps_tr[k % 2][:, :]).then_inc(s.vt_ready, 1)
                    if k == 1 and not (isinstance(i, int) and i == 0):
                        second_turn(dve, i - 1, 1 - par)
                if last:
                    second_turn(dve, i, par)

            walk(dve, n, body)

        @block.tensor
        def _(pe):
            def turn_chunk(i, par, k):
                c = NCH * i + k
                pe.wait_ge(s.bn_done, 4 * i + k // 2 + 1)
                at_least(pe, s.vt_ready, c - 1)
                for b in range(4):
                    ins = nc.tensor.transpose(ps_tr[k % 2][:, P * b:P * b + P],
                                              u[:, par, CH * k + P * b:CH * k + P * b + P], K["eye"][:, :])
                ins.then_inc(s.tr_done, 1)

            def transform_y(i, k):
                c = NCH * i + k
                pe.wait_ge(s.vt_ready, c + 1)
                if k % 2 == 0:
                    at_least(pe, s.a_ready, 4 * i + k // 2 - 1)
                for b in range(4):
                    o = 192 * (k % 2) + 48 * b
                    ins = nc.tensor.matmul(ps_a[k // 2 % 2][:, o:o + 48], vt[:, k % 2, P * b:P * b + P],
                                           K["dfty"][:, :], start=True, stop=True)
                ins.then_inc(s.fy_done, 1)

            def turn_again(i, par):
                pe.wait_ge(s.a_ready, 4 * i + 4)
                for j in range(3):
                    b = (3 * par + j) % 2
                    at_least(pe, s.a2_ready, 3 * i + j - 1)
                    for t in range(4):
                        k = 4 * j + t
                        ins = nc.tensor.transpose(ps_t[b][:, P * t:P * t + P],
                                                  ya[:, par, k].rearrange("p x r -> p (x r)"), K["eye"][:, :])
                    ins.then_inc(s.t2_done, 1)

            def transform_x(i, par):
                pe.wait_ge(s.a2_ready, 3 * i + 3)
                for hh in range(2):
                    at_least(pe, s.sp_ready, 2 * i + hh - 1)
                    for t in range(6):
                        ins = nc.tensor.matmul(ps_s[hh][:, 48 * t:48 * t + 48], yt[:, par, 6 * hh + t, :],
                                               K["dftx"][:, :], start=True, stop=True)
                    ins.then_inc(s.fx_done, 1)

            def body(i, par, r, last):
                for k in range(NCH):
                    turn_chunk(i, par, k)
                    if k >= 1:
                        transform_y(i, k - 1)
                    if not (isinstance(i, int) and i == 0):
                        if k == 1:
                            turn_again(i - 1, 1 - par)
                        if k == 3:
                            transform_x(i - 1, 1 - par)
                transform_y(i, NCH - 1)
                if last:
                    turn_again(i, par)
                    transform_x(i, par)

            walk(pe, n, body)


def turn_weights(pool, nc, s, K):
    w, tmp = K["mixw"], K["mixtmp"]
    pool.wait_ge(s.w_in, 64)
    steps = 0
    for h in range(2):
        rows = slice(2 * h * C + C, 2 * h * C + 2 * C)
        re, im = w[rows, :, 0], w[rows, :, 1]
        if h:
            pool.wait_ge(s.w_fix, 3)
        nc.gpsimd.tensor_copy(tmp[rows, :], re).then_inc(s.w_fix, 1)
        pool.wait_ge(s.w_fix, 3 * h + 1)
        nc.gpsimd.tensor_scalar(re, im, -1.0, None, ALU.mult).then_inc(s.w_fix, 1)
        pool.wait_ge(s.w_fix, 3 * h + 2)
        nc.gpsimd.tensor_copy(im, tmp[rows, :]).then_inc(s.w_fix, 1)
    pool.wait_ge(s.w_fix, 6)


def weight_loader(s, K, fw1, fw2, layer):
    def load(eng):
        for h, fw in enumerate((fw1, fw2)):
            src = fw[layer].rearrange("i o x y r -> i (o x y) r")
            for ri in range(2):
                a = (2 * h + ri) * C
                eng.dma_start(K["mixw"][a:a + C], src).then_inc(s.w_in, 16)
    return load


def mix_phase(nc, sems, tag, K, B, xsp, ysp, par, layer, first, consts):
    s = sems
    with ExitStack() as ctx:
        xm = ctx.enter_context(nc.sbuf_tensor(f"m_x{tag}", [P, B, MODES], F32))
        ys = ctx.enter_context(nc.sbuf_tensor(f"m_y{tag}", [B, 2, 2 * M1 * C], F32))
        bank = [ctx.enter_context(nc.psum_tensor(f"m_p{b}{tag}", [P, CH], F32)) for b in range(4)]
        pp = ctx.enter_context(nc.psum_tensor(f"m_pp{tag}", [P, CH], F32))
        pp2 = ctx.enter_context(nc.psum_tensor(f"m_pp2{tag}", [P, CH], F32))
        wv = K["mixw"][:, :, :].rearrange("p (o x y) r -> p o x y r", o=C, x=M1)
        y_out = [s.y_out0, s.y_out1]
        block = ctx.enter_context(nc.Block())

        @block.sync
        def _(eng):
            for h in range(2):
                for ri in range(2):
                    if first:
                        a = 64 * h + 4 * ri
                        eng.dma_start(xm[a:a + 1], xsp[:, SPEC // 4 * (2 * h + ri):SPEC // 4 * (2 * h + ri + 1)]
                                      .rearrange("(o b) m -> o b m", o=1)).then_inc(s.in_a, 16)
                        eng.dma_start(xm[a + 1:a + 4], consts["grid_ft"][h, ri].rearrange("j (o m) -> j o m", o=1)
                                      .broadcast_to([3, B, MODES])).then_inc(s.in_a, 16)
                    else:
                        a = (2 * h + ri) * C
                        eng.dma_start(xm[a:a + C], xsp.rearrange("(b c) (q m) -> q c b m", c=C, q=4)[2 * h + ri])\
                            .then_inc(s.in_a, 16)
            for q in range(2 * M2):
                h, k = q // M2, q % M2
                eng.wait_ge(s.mix_low, q + 1)
                eng.wait_ge(s.mix_high, q + 1)
                eng.dma_start(ysp[k, 2 * M1 * h:2 * M1 * (h + 1)].rearrange("r b c -> b r c"),
                              ys[:, q % 2].rearrange("b (r c) -> b r c", c=C)).then_inc(y_out[q % 2], 16)
            eng.wait_ge(s.y_out0, 16 * M2)
            eng.wait_ge(s.y_out1, 16 * M2)

        @block.scalar
        def _(act):
            for g in range(G):
                rows = slice(C * g, C * g + C)
                act.dma_start(K["wbd"][rows, rows], par["w_w"][layer]).then_inc(s.par_in, 16)
                for name in ("w_b", "bn_g", "bn_b"):
                    act.dma_start(K[name][rows, :], par[name][layer].rearrange("(c o) -> c o", o=1)).then_inc(s.par_in, 16)
            for q in range(2 * M2):
                act.wait_ge(s.mix_done, 2 * q + 2)
                if q >= 2:
                    act.wait_ge(y_out[q % 2], 16 * (q // 2))
                out = ys[:, q % 2].rearrange("b (r x c) -> b r x c", r=2, x=M1)[:, :, 6:12, :]
                nc.scalar.copy(out, bank[(2 * q + 1) % 4][0:B, 0:384]).then_inc(s.mix_high, 1)
            act.wait_ge(s.par_in, 16 * 4 * G)

        @block.vector
        def _(dve):
            if first:
                for n in range(2 * C * MODES // CH):
                    dve.wait_ge(s.pw_done, n + 1)
                    nc.vector.tensor_copy(K["mixw"][:, :, :].rearrange("p a r -> p (a r)")[:, CH * n:CH * n + CH],
                                          (pp, pp2)[n % 2][:, :]).then_inc(s.pw_ready, 1)
                dve.wait_ge(s.pw_done, 19)
                nc.vector.tensor_copy(K["pwbd"][:, :], pp2[0:4 * G, 0:P]).then_inc(s.pw_ready, 1)
            for q in range(2 * M2):
                dve.wait_ge(s.mix_done, 2 * q + 1)
                if q >= 2:
                    dve.wait_ge(y_out[q % 2], 16 * (q // 2))
                out = ys[:, q % 2].rearrange("b (r x c) -> b r x c", r=2, x=M1)[:, :, 0:6, :]
                nc.vector.tensor_copy(out, bank[2 * q % 4][0:B, 0:384]).then_inc(s.mix_low, 1)

        @block.tensor
        def _(pe):
            if first:
                for n in range(2 * C * MODES // CH):
                    at_least(pe, s.pw_ready, n - 1)
                    nc.tensor.matmul((pp, pp2)[n % 2][:, :], K["lift_mix"][:, :],
                                     K["mixw"][:, :, :].rearrange("p a r -> p (a r)")[:, CH * n:CH * n + CH],
                                     start=True, stop=True).then_inc(s.pw_done, 1)
                pe.wait_ge(s.par_in, 16 * 4 * G)
                pe.wait_ge(s.pw_ready, 18)
                nc.tensor.matmul(pp2[0:4 * G, 0:P], K["lift_px"][:, :], K["wbd"][:, :],
                                 start=True, stop=True).then_inc(s.pw_done, 1)
            pe.wait_ge(s.in_a, 128 if first else 64)
            depth = 8 if first else 2 * C
            for q in range(2 * M2):
                h, k = q // M2, q % M2
                rows = slice(64 * h, 64 * h + depth)
                for half in range(2):
                    n = 2 * q + half
                    at_least(pe, s.mix_high if half else s.mix_low, q - 1)
                    for t in range(6):
                        x = 6 * half + t
                        out = bank[n % 4][0:B, 0:384].rearrange("b (r x c) -> b x c r", r=2, x=6)[:, t]
                        ins = nc.tensor.matmul(out, xm[rows, :, M1 * k + x], wv[rows, :, x, k, :],
                                               start=True, stop=True)
                    ins.then_inc(s.mix_done, 1)


def inverse_phase(nc, sems, tag, K, U, ysp, n, images, scale_bias, stats):
    s = sems
    first = images is not None
    with ExitStack() as ctx:
        rows_in = 4 * G if first else P
        v = ctx.enter_context(nc.sbuf_tensor(f"i_v{tag}", [rows_in, 2, PX], F32))
        ysb = ctx.enter_context(nc.sbuf_tensor(f"i_y{tag}", [2 * KX, 2, M2, P], F32))
        sx = ctx.enter_context(nc.sbuf_tensor(f"i_s{tag}", [P, 2, S, M2, 2], F32))
        st = ctx.enter_context(nc.sbuf_tensor(f"i_t{tag}", [4 * 2 * M2, 2, 16, P], F32))
        uo = ctx.enter_context(nc.sbuf_tensor(f"i_u{tag}", [P, 2, PX], F32))
        ps_s = [ctx.enter_context(nc.psum_tensor(f"i_ps{b}{tag}", [P, CH], F32)) for b in range(2)]
        ps_t = [ctx.enter_context(nc.psum_tensor(f"i_pt{b}{tag}", [4 * 2 * M2, CH], F32)) for b in range(2)]
        ps_u = [ctx.enter_context(nc.psum_tensor(f"i_pu{b}{tag}", [P, CH], F32)) for b in range(4)]
        u_in, y_in, u_out = [s.u_in0, s.u_in1], [s.y_in0, s.y_in1], [s.u_out0, s.u_out1]
        block = ctx.enter_context(nc.Block())

        @block.sync
        def _(eng):
            if first:
                for par in range(2):
                    eng.dma_start(v[G:4 * G, par], K["grid_px"]).then_inc(s.const_in, 16)

            def store(i, par):
                eng.wait_ge(s.uo_ready, NCH * i + NCH)
                eng.dma_start(U[i], uo[:, par]).then_inc(u_out[par], 16)

            def body(i, par, r, last):
                at_least(eng, s.ix_done, 3 * (i - 1))
                eng.dma_start(ysb[:, par], ysp[:, :, bass.ds(G * i, G), :].rearrange("k r b c -> r k (b c)"))\
                    .then_inc(y_in[par], 16)
                at_least(eng, s.um_done, NCH * (i - 1))
                if first:
                    eng.dma_start(v[0:G, par], images[bass.ds(G * i, G), :]).then_inc(u_in[par], 16)
                else:
                    eng.dma_start(v[:, par], U[i]).then_inc(u_in[par], 16)
                if not (isinstance(i, int) and i < 2):
                    store(i - 2, par)

            walk(eng, n, body)
            store(n - 2, 0)
            store(n - 1, 1)
            eng.wait_ge(s.u_out0, 8 * n)
            eng.wait_ge(s.u_out1, 8 * n)

        @block.scalar
        def _(act):
            def norm(i, par, r):
                act.wait_ge(u_in[par], 16 * r + 16)
                for k in range(4):
                    px = v[:, par, 1024 * k:1024 * k + 1024]
                    nc.scalar.activation(px, px, ACT.Relu, bias=scale_bias[1], scale=scale_bias[0])\
                        .then_inc(s.bn_done, 1)

            def body(i, par, r, last):
                if not first and isinstance(i, int) and i == 0:
                    norm(0, 0, 0)
                for k in range(NCH):
                    c = NCH * i + k
                    act.wait_ge(s.um_done, c + 1)
                    if k == 0 and not (isinstance(i, int) and i < 2):
                        act.wait_ge(u_out[par], 16 * r)
                        act.wait_ge(s.st_done, NCH * (i - 1))
                    nc.scalar.activation(uo[:, par, CH * k:CH * k + CH], ps_u[k % 4][:, :], ACT.Identity,
                                         bias=K["w_b"][:, 0:1]).then_inc(s.uo_ready, 1)
                    if k == 3 and not first and not last:
                        norm(i + 1, 1 - par, r if par == 0 else r + 1)

            walk(act, n, body)

        def spread(dve, i, par):
            for j in range(3):
                dve.wait_ge(s.ix_done, 3 * i + j + 1)
                at_least(dve, s.tt_done, 4 * (i - 1))
                dst = sx[:, par, :, 4 * j:4 * j + 4, :].rearrange("p x k r -> p k x r")
                nc.vector.tensor_copy(dst, ps_s[(3 * par + j) % 2][:, :].rearrange("p (k x r) -> p k x r", k=4, r=2))\
                    .then_inc(s.s_ready, 1)

        def turned(dve, i, par):
            for j in range(4):
                dve.wait_ge(s.tt_done, 4 * i + j + 1)
                at_least(dve, s.um_done, NCH * (i - 1))
                nc.vector.tensor_copy(st[:, par, 4 * j:4 * j + 4, :], ps_t[j % 2][:, :]).then_inc(s.t_ready, 1)

        @block.vector
        def _(dve):
            spread(dve, 0, 0)
            turned(dve, 0, 0)

            def body(i, par, r, last):
                for k in range(NCH):
                    c = NCH * i + k
                    dve.wait_ge(s.uo_ready, c + 1)
                    nc.vector.bn_stats(stats[:, bass.ds(6 * c, 6)], uo[:, par, CH * k:CH * k + CH])\
                        .then_inc(s.st_done, 1)
                    if not last and k == 0:
                        spread(dve, i + 1, 1 - par)
                    if not last and k == 4:
                        turned(dve, i + 1, 1 - par)

            walk(dve, n, body)

        @block.tensor
        def _(pe):
            def inverse_x(i, par, r):
                pe.wait_ge(y_in[par], 16 * r + 16)
                for j in range(3):
                    at_least(pe, s.s_ready, 3 * i + j - 1)
                    for t in range(4):
                        ins = nc.tensor.matmul(ps_s[(3 * par + j) % 2][:, P * t:P * t + P], ysb[:, par, 4 * j + t, :],
                                               K["idftx"][:, :], start=True, stop=True)
                    ins.then_inc(s.ix_done, 1)

            def turn(i, par):
                pe.wait_ge(s.s_ready, 3 * i + 3)
                for j in range(4):
                    at_least(pe, s.t_ready, 4 * i + j - 1)
                    for t in range(4):
                        x = 4 * (4 * j + t)
                        ins = nc.tensor.transpose(ps_t[j % 2][:, P * t:P * t + P],
                                                  sx[:, par, x:x + 4].rearrange("p x k r -> p (x k r)"), K["eye"][:, :])
                    ins.then_inc(s.tt_done, 1)

            def pixels(i, par, r, k):
                c = NCH * i + k
                if first:
                    if k == 0:
                        pe.wait_ge(s.const_in, 32)
                        pe.wait_ge(u_in[par], 16 * r + 16)
                else:
                    pe.wait_ge(s.bn_done, 4 * i + k // 2 + 1)
                pe.wait_ge(s.t_ready, 4 * i + k // 2 + 1)
                at_least(pe, s.uo_ready, c - 3)
                weights = K["pwbd"] if first else K["wbd"]
                nc.tensor.matmul(ps_u[k % 4][:, :], weights[:, :], v[:, par, CH * k:CH * k + CH], start=True, stop=False,
                                 skip_group_check=True)
                for hh in range(2):
                    ins = nc.tensor.matmul(ps_u[k % 4][:, 256 * hh:256 * hh + 256], st[:, par, 2 * k + hh, :],
                                           K["idfty"][:, :], start=False, stop=True, skip_group_check=True)
                ins.then_inc(s.um_done, 1)

            inverse_x(0, 0, 0)
            turn(0, 0)

            def body(i, par, r, last):
                for k in range(NCH):
                    pixels(i, par, r, k)
                    if not last and k == 1:
                        inverse_x(i + 1, 1 - par, r if par == 0 else r + 1)
                    if not last and k == 4:
                        turn(i + 1, 1 - par)

            walk(pe, n, body)


def norm_phase(nc, sems, tag, K, n, stats, scale_bias):
    s = sems
    scale, bias = scale_bias
    with ExitStack() as ctx:
        mv = ctx.enter_context(nc.sbuf_tensor(f"n_mv{tag}", [P, 2], F32))
        avg = ctx.enter_context(nc.sbuf_tensor(f"n_avg{tag}", [P, 2], F32))
        dm = ctx.enter_context(nc.sbuf_tensor(f"n_dm{tag}", [P, 2], F32))
        sd = ctx.enter_context(nc.sbuf_tensor(f"n_sd{tag}", [P, 4], F32))
        ps = ctx.enter_context(nc.psum_tensor(f"n_ps{tag}", [P, CH], F32))
        block = ctx.enter_context(nc.Block())

        @block.vector
        def _(dve):
            count = 0

            def then(ins):
                nonlocal count
                count += 1
                ins.then_inc(s.step, 1)
                dve.wait_ge(s.step, count)

            then(nc.vector.bn_aggr(mv[:, :], stats[:, 0:6 * NCH * n]))
            dve.sem_inc(s.aggr, 1)
            dve.wait_ge(s.pe_step, 1)
            then(nc.vector.tensor_copy(avg[:, :], ps[:, 0:2]))
            then(nc.vector.tensor_tensor(dm[:, 0:1], mv[:, 0:1], avg[:, 0:1], ALU.subtract))
            then(nc.vector.tensor_tensor(dm[:, 1:2], dm[:, 0:1], dm[:, 0:1], ALU.mult))
            dve.sem_inc(s.aggr, 1)
            dve.wait_ge(s.pe_step, 2)
            then(nc.vector.tensor_tensor(sd[:, 0:1], avg[:, 1:2], ps[:, 2:3], ALU.add))
            then(nc.vector.tensor_scalar(sd[:, 1:2], sd[:, 0:1], EPS, None, ALU.add))
            dve.sem_inc(s.aggr, 1)
            dve.wait_ge(s.act_step, 1)
            then(nc.vector.reciprocal(sd[:, 3:4], sd[:, 2:3]))
            then(nc.vector.tensor_tensor(scale, sd[:, 3:4], K["bn_g"][:, 0:1], ALU.mult))
            then(nc.vector.tensor_tensor(sd[:, 0:1], avg[:, 0:1], scale, ALU.mult))
            then(nc.vector.tensor_tensor(bias, K["bn_b"][:, 0:1], sd[:, 0:1], ALU.subtract))

        @block.scalar
        def _(act):
            act.wait_ge(s.aggr, 3)
            nc.scalar.activation(sd[:, 2:3], sd[:, 1:2], ACT.Sqrt).then_inc(s.act_step, 1)

        @block.tensor
        def _(pe):
            pe.wait_ge(s.aggr, 1)
            nc.tensor.matmul(ps[:, 0:2], K["groupmean"][:, :], mv[:, :], start=True, stop=True).then_inc(s.pe_step, 1)
            pe.wait_ge(s.aggr, 2)
            nc.tensor.matmul(ps[:, 2:3], K["groupmean"][:, :], dm[:, 1:2], start=True, stop=True).then_inc(s.pe_step, 1)


def project_phase(nc, sems, K, U, n, h_img, scale_bias, q_w, q_b):
    s = sems
    scale, bias = scale_bias
    with ExitStack() as ctx:
        u = ctx.enter_context(nc.sbuf_tensor("proj_u", [P, 2, PX], F32))
        hb = ctx.enter_context(nc.sbuf_tensor("proj_h", [P, 2, 2, CH], F32))
        qbd = ctx.enter_context(nc.sbuf_tensor("proj_w", [P, P], F32))
        qc = ctx.enter_context(nc.sbuf_tensor("proj_c", [P, 4], F32))
        qbias = ctx.enter_context(nc.sbuf_tensor("proj_b", [P, 1], F32))
        ones = ctx.enter_context(nc.sbuf_tensor("proj_1", [P, P], F32))
        bank = [ctx.enter_context(nc.psum_tensor(f"proj_p{b}", [P, CH], F32)) for b in range(4)]
        pc = ctx.enter_context(nc.psum_tensor("proj_pc", [P, CH], F32))
        u_in, out = [s.u_in0, s.u_in1], [s.hq_out0, s.hq_out1]
        block = ctx.enter_context(nc.Block())

        @block.sync
        def _(eng):
            for g in range(G):
                eng.dma_start(qc[C * g:C * g + C, 0:1], q_w).then_inc(s.const_in, 16)
            eng.dma_start(qc[:, 1:2], q_b.rearrange("(a o) -> a o", o=1).broadcast_to([P, 1])).then_inc(s.const_in, 16)

            def store(i, par):
                eng.wait_ge(s.hq_ready, 2 * i + 2)
                for j in range(4):
                    eng.dma_start(h_img[i].rearrange("g (k j c) -> j g k c", j=4, k=2)[j],
                                  hb[32 * j:32 * j + G, par]).then_inc(out[par], 16)

            def body(i, par, r, last):
                at_least(eng, s.hq_done, 2 * (i - 1))
                eng.dma_start(u[:, par], U[i]).then_inc(u_in[par], 16)
                if not (isinstance(i, int) and i < 2):
                    store(i - 2, par)

            walk(eng, n, body)
            store(n - 2, 0)
            store(n - 1, 1)
            eng.wait_ge(s.hq_out0, 32 * n)
            eng.wait_ge(s.hq_out1, 32 * n)

        @block.vector
        def _(dve):
            nc.vector.memset(qbd[:, :], 0.0).then_inc(s.step, 1)
            nc.vector.memset(ones[:, :], 1.0 / G).then_inc(s.step, 1)
            for b in range(4):
                nc.vector.memset(bank[b][:, :], 0.0).then_inc(s.step, 1)
            dve.wait_ge(s.const_in, 16 * (G + 1))
            dve.wait_ge(s.step, 6)
            for g in range(G):
                rows = slice(C * g, C * g + C)
                nc.vector.tensor_tensor(qbd[rows, g:g + 1], qc[rows, 0:1], scale[rows, :], ALU.mult).then_inc(s.step, 1)
            nc.vector.tensor_tensor(qc[:, 2:3], qc[:, 0:1], bias, ALU.mult).then_inc(s.step, 1)
            dve.wait_ge(s.pe_step, 1)
            nc.vector.tensor_tensor(qbias[:, :], pc[:, 0:1], qc[:, 1:2], ALU.add).then_inc(s.step, 1)

        @block.scalar
        def _(act):
            act.wait_ge(s.step, 12)

            def body(i, par, r, last):
                for kk in range(2):
                    act.wait_ge(s.hq_done, 2 * i + kk + 1)
                    if kk == 0 and not (isinstance(i, int) and i < 2):
                        act.wait_ge(out[par], 64 * r)
                    nc.scalar.activation(hb[:, par, kk, :], bank[2 * par + kk][:, :], ACT.Identity,
                                         bias=qbias[:, 0:1]).then_inc(s.hq_ready, 1)

            walk(act, n, body)

        @block.tensor
        def _(pe):
            pe.wait_ge(s.step, 11)
            nc.tensor.matmul(pc[:, 0:1], ones[:, :], qc[:, 2:3], start=True, stop=True).then_inc(s.pe_step, 1)

            def body(i, par, r, last):
                pe.wait_ge(u_in[par], 16 * r + 16)
                for kk in range(2):
                    at_least(pe, s.hq_ready, 2 * i + kk - 3)
                    for j in range(4):
                        k = 4 * kk + j
                        ins = nc.tensor.matmul(bank[2 * par + kk][32 * j:32 * j + G, :], qbd[:, 0:G],
                                               u[:, par, CH * k:CH * k + CH], start=True, stop=True)
                    ins.then_inc(s.hq_done, 1)

            walk(pe, n, body)


def operator(nc, ctx, sems, d, h_img):
    B = d["x"].shape[0]
    n = B // G
    layers = d["w_w"].shape[0]

    def sb(name, shape):
        return ctx.enter_context(nc.sbuf_tensor("k_" + name, shape, F32))

    K = {
        "mixw": sb("mixw", [P, C * MODES, 2]), "mixtmp": sb("mixtmp", [P, C * MODES]),
        "wbd": sb("wbd", [P, P]), "pwbd": sb("pwbd", [4 * G, P]), "lift_mix": sb("lift_mix", [P, P]),
        "lift_px": sb("lift_px", [P, 4 * G]), "w_b": sb("w_b", [P, 1]), "bn_g": sb("bn_g", [P, 1]), "bn_b": sb("bn_b", [P, 1]),
    }
    for name in ("dfty", "dftx", "idftx", "idfty", "eye", "groupmean"):
        K[name] = sb(name, list(d[name].shape))
    K["grid_px"] = d["grid_px"]
    stats = sb("stats", [P, 6 * NCH * n])
    sb_t = sb("scale_bias", [P, 2])
    scale_bias = (sb_t[:, 0:1], sb_t[:, 1:2])
    U = nc.dram_tensor("u_scratch", (n, P, PX), F32).ap()
    xsp = nc.dram_tensor("x_spectrum", (n, P, SPEC), F32).ap()
    isp = nc.dram_tensor("image_spectrum", (B, SPEC), F32).ap()
    ysp = nc.dram_tensor("y_spectrum", (M2, 2 * KX, B, C), F32).ap()
    par = {"w_w": d["w_w"], "w_b": d["w_b"], "bn_g": d["bn_g"], "bn_b": d["bn_b"]}
    images = d["x"].rearrange("b x y o -> b (x y o)")
    s = sems

    with nc.Block() as block:
        names = ("dfty", "dftx", "idftx", "idfty", "eye", "groupmean")

        @block.vector
        def _(dve):
            for t in ("wbd", "lift_mix", "lift_px"):
                nc.vector.memset(K[t][:, :], 0.0).then_inc(s.step, 1)

        @block.sync
        def _(eng):
            for name in names:
                eng.dma_start(K[name][:, :], d[name]).then_inc(s.const_in, 16)
            eng.wait_ge(s.step, 3)
            with nc.allow_non_contiguous_dma("lifting weights, 128 words a piece"):
                for q in range(4):
                    rows, col = slice(C * q, C * q + C), 64 * (q // 2) + 4 * (q % 2)
                    eng.dma_start(K["lift_mix"][rows, col:col + 3], d["p_w"].rearrange("j c -> c j")).then_inc(s.const_in, 16)
                    eng.dma_start(K["lift_mix"][rows, col + 3:col + 4], d["p_b"].rearrange("(c o) -> c o", o=1)).then_inc(s.const_in, 16)
                    eng.dma_start(K["lift_px"][rows, q:3 * G:G], d["p_w"].rearrange("j c -> c j")).then_inc(s.const_in, 16)
                    eng.dma_start(K["lift_px"][rows, 3 * G + q:3 * G + q + 1], d["p_b"].rearrange("(c o) -> c o", o=1)).then_inc(s.const_in, 16)
            eng.wait_ge(s.const_in, 16 * (len(names) + 16))
    end_phase(nc, s)

    fw1, fw2 = d["fw1"], d["fw2"]
    forward_phase(nc, s, "_0", K, lambda i: images, 1, lambda i: isp, None, weight_loader(s, K, fw1, fw2, 0))
    end_phase(nc, s)
    mix_phase(nc, s, "_0", K, B, isp, ysp, par, 0, True, d)
    end_phase(nc, s)
    inverse_phase(nc, s, "_0", K, U, ysp, n, images, None, stats)
    end_phase(nc, s)
    norm_phase(nc, s, "_0", K, n, stats, scale_bias)
    end_phase(nc, s)
    with nc.Fori(1, layers) as layer:
        forward_phase(nc, s, "", K, lambda i: U[i], n, lambda i: xsp[i], scale_bias, weight_loader(s, K, fw1, fw2, layer))
        end_phase(nc, s)
        mix_phase(nc, s, "", K, B, xsp.rearrange("n p m -> (n p) m"), ysp, par, layer, False, d)
        end_phase(nc, s)
        inverse_phase(nc, s, "", K, U, ysp, n, None, scale_bias, stats)
        end_phase(nc, s)
        norm_phase(nc, s, "", K, n, stats, scale_bias)
        end_phase(nc, s)
    project_phase(nc, s, K, U, n, h_img, scale_bias, d["q_w"], d["q_b"])
    end_phase(nc, s)


def token_constants(T, D):
    t = np.arange(T)
    gap = t[None, :] - 1 - t[:, None]
    decay = np.where(gap >= 0, np.float64(DECAY) ** np.maximum(gap, 0), 0.0)
    return {"decay": decay.astype(np.float32)}


class Chain:

    def __init__(self, eng, sem, base=0):
        self.eng, self.sem, self.base, self.n = eng, sem, base, 0

    def then(self, ins):
        self.n += 1
        ins.then_inc(self.sem, 1)
        self.eng.wait_ge(self.sem, self.base + self.n)


def norm_statistics(nc, chain, st, w):
    ve = nc.vector
    me, se, mo, so = (st[:, :, j] for j in (1, 2, 4, 5))
    chain.then(ve.tensor_tensor(w[:, 0], me, mo, ALU.add))
    chain.then(ve.tensor_tensor(w[:, 1], me, mo, ALU.subtract))
    chain.then(ve.tensor_tensor(w[:, 2], se, so, ALU.add))
    chain.then(ve.tensor_scalar(w[:, 0], w[:, 0], 0.5, None, ALU.mult))
    chain.then(ve.scalar_tensor_tensor(out=w[:, 1], in0=w[:, 1], scalar=0.25, in1=w[:, 1], op0=ALU.mult, op1=ALU.mult))
    chain.then(ve.tensor_scalar(w[:, 2], w[:, 2], 1.0 / S, EPS, ALU.mult, ALU.add))
    chain.then(ve.tensor_tensor(w[:, 3], w[:, 1], w[:, 2], ALU.add))


def spread_over(ap, D):
    return ap.rearrange("p (n o) -> p n o", o=1).broadcast_to([ap.shape[0], ap.shape[1], D])


def token_norm_phase(nc, sems, W, h_img, txt, d, le_dram):
    s = sems
    h = W["e"]
    T, B, D = h.shape
    with ExitStack() as ctx:
        le = ctx.enter_context(nc.sbuf_tensor("t_le", [T, B, D], F32))
        st = ctx.enter_context(nc.sbuf_tensor("t_st", [T, B, 6], F32))
        w = ctx.enter_context(nc.sbuf_tensor("t_w", [T, 6, B], F32))
        raw = ctx.enter_context(nc.sbuf_tensor("t_raw", [P, 2, 2, D], F32))
        rawe = ctx.enter_context(nc.sbuf_tensor("t_rawe", [D, 2, P], F32))
        ps = ctx.enter_context(nc.psum_tensor("t_ps", [P, 6, P], F32))
        block = ctx.enter_context(nc.Block())

        @block.sync
        def _(eng):
            eng.dma_start(h[0:S], h_img.rearrange("n g (t d) -> t (n g) d", d=D)).then_inc(s.in_a, 16)
            eng.dma_start(h[S:T], txt.rearrange("b t d -> t b d")).then_inc(s.in_a, 16)
            for j, name in enumerate(("Dx", "Dy")):
                eng.dma_start(raw[:, j], d[name].rearrange("(q p) d -> p q d", p=P)).then_inc(s.w_in, 16)
            eng.dma_start(rawe[:, :, :], d["E"].rearrange("d (q n) -> d q n", q=2)).then_inc(s.w_in, 16)
            eng.dma_start(W["decay"][:, :], d["decay"]).then_inc(s.const_in, 16)
            eng.wait_ge(s.const_in, 16)
            eng.wait_ge(s.aggr, 3)
            eng.dma_start(le_dram, le[:, :, :]).then_inc(s.y_out0, 16)
            eng.wait_ge(s.y_out0, 16)

        @block.tensor
        def _(pe):
            pe.wait_ge(s.w_in, 48)
            for j in range(2):
                for q in range(2):
                    nc.tensor.transpose(ps[0:D, 2 * j + q, :], raw[:, j, q, :], W["eye"][:, :])
            for q in range(2):
                ins = nc.tensor.transpose(ps[:, 4 + q, 0:D], rawe[:, q, :], W["eye"][0:D, 0:D])
            ins.then_inc(s.pe_step, 1)

        @block.scalar
        def _(act):
            act.wait_ge(s.aggr, 1)
            nc.scalar.activation(w[:, 4], w[:, 3], ACT.Sqrt).then_inc(s.act_step, 1)
            act.wait_ge(s.aggr, 2)
            nc.scalar.activation(w[:, 5], w[:, 2], ACT.Sqrt).then_inc(s.act_step, 1)

        @block.vector
        def _(dve):
            ve = nc.vector
            c = Chain(dve, s.step)
            c.then(ve.memset(W["ones"][:, :], 1.0))
            dve.wait_ge(s.pe_step, 1)
            for j, t in enumerate(("DxT", "DyT")):
                c.then(ve.tensor_copy(W[t][:, :], ps[0:D, 2 * j:2 * j + 2, :].rearrange("p q n -> p (q n)")))
            c.then(ve.tensor_copy(W["ET"][:, :, :], ps[:, 4:6, 0:D]))
            dve.wait_ge(s.in_a, 32)
            with dve.Fori(0, B // 8) as m:
                for b in range(8):
                    ve.bn_stats(st[:, bass.ds(8 * m + b, 1), :].rearrange("p o s -> p (o s)"),
                                h[:, bass.ds(8 * m + b, 1), :].rearrange("p o d -> p (o d)")).then_inc(s.st_done, 1)
            dve.wait_ge(s.st_done, B)
            norm_statistics(nc, c, st, w)
            dve.sem_inc(s.aggr, 1)
            dve.wait_ge(s.act_step, 1)
            c.then(ve.reciprocal(w[:, 1], w[:, 4]))
            c.then(ve.tensor_tensor(h[:, :, :], h[:, :, :], spread_over(w[:, 0], D), ALU.subtract))
            c.then(ve.tensor_tensor(h[:, :, :], h[:, :, :], spread_over(w[:, 1], D), ALU.mult))
            c.then(ve.tensor_scalar(w[:, 3], w[:, 3], EPS, None, ALU.subtract))
            c.then(ve.tensor_tensor(w[:, 2], w[:, 1], w[:, 1], ALU.mult))
            c.then(ve.tensor_tensor(w[:, 2], w[:, 2], w[:, 3], ALU.mult))
            c.then(ve.tensor_scalar(w[:, 2], w[:, 2], EPS, None, ALU.add))
            dve.sem_inc(s.aggr, 1)
            dve.wait_ge(s.act_step, 2)
            c.then(ve.reciprocal(w[:, 3], w[:, 5]))
            c.then(ve.tensor_tensor(le[:, :, :], h[:, :, :], spread_over(w[:, 3], D), ALU.mult))
            dve.sem_inc(s.aggr, 1)


def update_phase(nc, sems, W, usum):
    s = sems
    T, B, D = W["e"].shape
    n, CT = B // 4, 4 * T
    with ExitStack() as ctx:
        et = ctx.enter_context(nc.sbuf_tensor("up_et", [D, 2, CT], F32))
        eb = ctx.enter_context(nc.sbuf_tensor("up_eb", [T, 2, 4, D], F32))
        row = ctx.enter_context(nc.sbuf_tensor("up_row", [1, B * T], F32))
        pt = [ctx.enter_context(nc.psum_tensor(f"up_t{b}", [D, CH], F32)) for b in range(2)]
        pu = [ctx.enter_context(nc.psum_tensor(f"up_u{b}", [P, CH], F32)) for b in range(4)]
        pr = [ctx.enter_context(nc.psum_tensor(f"up_r{b}", [1, CH], F32)) for b in range(2)]
        block = ctx.enter_context(nc.Block())

        @block.tensor
        def _(pe):
            def sums(i, par):
                pe.wait_ge(s.u_in0, 2 * i + 2)
                at_least(pe, s.sp_ready, i - 1)
                for q in range(2):
                    ins = nc.tensor.matmul(pr[par][0:1, 0:CT], W["ones"][:, 0:1], W["x"][:, q, bass.ds(CT * i, CT)],
                                           start=(q == 0), stop=(q == 1))
                ins.then_inc(s.fx_done, 1)

            def body(i, par, r, last):
                pe.wait_ge(s.a_ready, i + 1)
                at_least(pe, s.vt_ready, i - 1)
                pe.nop(nofuse=True)
                for b in range(4):
                    ins = nc.tensor.transpose(pt[par][:, T * b:T * b + T], eb[:, par, b, :], W["eye"][0:T, 0:T])
                ins.then_inc(s.tr_done, 1)
                if not (isinstance(i, int) and i == 0):
                    sums(i - 1, 1 - par)
                pe.wait_ge(s.vt_ready, i + 1)
                at_least(pe, s.u_in0, 2 * (i - 1))
                for q in range(2):
                    ins = nc.tensor.matmul(pu[2 * par + q][:, 0:CT], W["DxT"][:, P * q:P * q + P], et[:, par, :],
                                           start=True, stop=True)
                ins.then_inc(s.fy_done, 1)
                if last:
                    sums(i, par)

            walk(pe, n, body)

        @block.gpsimd
        def _(pool):
            def body(i, par, r, last):
                at_least(pool, s.tr_done, i - 1)
                nc.gpsimd.tensor_copy(eb[:, par, :, :], W["e"][:, bass.ds(4 * i, 4), :]).then_inc(s.a_ready, 1)

            walk(pool, n, body)

        @block.scalar
        def _(act):
            def body(i, par, r, last):
                act.wait_ge(s.fy_done, i + 1)
                for q in range(2):
                    nc.scalar.activation(W["x"][:, q, bass.ds(CT * i, CT)], pu[2 * par + q][:, 0:CT], ACT.Relu)\
                        .then_inc(s.u_in0, 1)

            walk(act, n, body)

        @block.vector
        def _(dve):
            def sums_out(i, par):
                dve.wait_ge(s.fx_done, i + 1)
                nc.vector.tensor_copy(row[0:1, bass.ds(CT * i, CT)], pr[par][0:1, 0:CT]).then_inc(s.sp_ready, 1)

            def body(i, par, r, last):
                dve.wait_ge(s.tr_done, i + 1)
                at_least(dve, s.fy_done, i - 1)
                nc.vector.tensor_copy(et[:, par, :], pt[par][:, 0:CT]).then_inc(s.vt_ready, 1)
                if not (isinstance(i, int) and i == 0):
                    sums_out(i - 1, 1 - par)
                if last:
                    sums_out(i, par)

            walk(dve, n, body)

        @block.sync
        def _(eng):
            eng.wait_ge(s.sp_ready, n)
            eng.dma_start(usum.rearrange("(o b) t -> o (b t)", o=1), row[:, :]).then_inc(s.y_out0, 16)
            eng.wait_ge(s.y_out0, 16)


def decay_phase(nc, sems, usum, coef):
    s = sems
    B, T = usum.shape
    with ExitStack() as ctx:
        us = ctx.enter_context(nc.sbuf_tensor("d_us", [B, T], F32))
        sg = ctx.enter_context(nc.sbuf_tensor("d_sg", [B, T], F32))
        sm = ctx.enter_context(nc.sbuf_tensor("d_sm", [B, T], F32))
        cf = ctx.enter_context(nc.sbuf_tensor("d_cf", [B, 2, T], F32))
        block = ctx.enter_context(nc.Block())

        @block.sync
        def _(eng):
            eng.dma_start(us[:, :], usum).then_inc(s.in_a, 16)
            eng.wait_ge(s.aggr, 1)
            eng.dma_start(coef.rearrange("q b t -> b q t"), cf[:, :, :]).then_inc(s.y_out0, 16)
            eng.wait_ge(s.y_out0, 16)

        @block.vector
        def _(dve):
            ve = nc.vector
            c = Chain(dve, s.step)
            dve.wait_ge(s.in_a, 16)
            c.then(ve.tensor_tensor_scan(sg[:, :], us[:, :], us[:, :], 0.0, ALU.max, ALU.max))
            c.then(ve.tensor_scalar(sg[:, :], sg[:, :], 0.0, None, ALU.is_gt))
            c.then(ve.tensor_copy(sm[:, 0:1], us[:, 0:1]))
            for sweep in range(5):
                c.then(ve.scalar_tensor_tensor(out=sm[:, 1:T], in0=sg[:, 0:T - 1], scalar=DECAY, in1=us[:, 1:T],
                                               op0=ALU.mult, op1=ALU.add))
                c.then(ve.tensor_scalar(sg[:, :], sm[:, :], 1e12, 1.0, ALU.mult, ALU.min))
            c.then(ve.scalar_tensor_tensor(out=sm[:, 1:T], in0=sg[:, 0:T - 1], scalar=DECAY, in1=us[:, 1:T],
                                           op0=ALU.mult, op1=ALU.add))
            c.then(ve.tensor_scalar(sm[:, :], sm[:, :], 1e-12, None, ALU.max))
            c.then(ve.reciprocal(cf[:, 0, :], sm[:, :]))
            c.then(ve.tensor_scalar(cf[:, 1, :], cf[:, 0, :], DECAY, None, ALU.mult))
            c.then(ve.memset(cf[:, 1, 0:1], 0.0))
            dve.sem_inc(s.aggr, 1)


def attention_phase(nc, sems, W, h_img, txt, coef, le_dram, e2t_dram):
    s = sems
    T, B, D = W["e"].shape
    NB = 8
    n, HT, CT = B // NB, 4 * T, NB * T
    with ExitStack() as ctx:
        def sb(name, shape):
            return ctx.enter_context(nc.sbuf_tensor("at_" + name, shape, F32))

        cf = sb("cf", [P, 2, 2, CT])
        x = sb("x", [P, 2, 2, CT])
        hb = sb("h", [T, 2, NB, D])
        sc = sb("sc", [T, CT])
        la = sb("la", [T, NB, D])
        lat = sb("lat", [D, CT])
        y = sb("y", [P, 2, CT])
        e2 = sb("e2", [T, NB, D])
        e2t = sb("e2t", [D, 2, CT])
        le = sb("le", [T, 2, NB, D])
        st = sb("st", [T, NB, 6])
        w = sb("w", [T, 6, NB])
        ps_s = [ctx.enter_context(nc.psum_tensor(f"at_ps{b}", [T, CH], F32)) for b in range(2)]
        ps_a = ctx.enter_context(nc.psum_tensor("at_pa", [T, CH], F32))
        ps_t = [ctx.enter_context(nc.psum_tensor(f"at_pt{b}", [D, CH], F32)) for b in range(2)]
        ps_y = [ctx.enter_context(nc.psum_tensor(f"at_py{b}", [P, CH], F32)) for b in range(2)]
        ps_v = ctx.enter_context(nc.psum_tensor("at_pv", [T, CH], F32))
        cf_in, h_in, le_in, e_out = [s.u_in0, s.u_in1], [s.y_in0, s.y_in1], [s.sp_out0, s.sp_out1], [s.u_out0, s.u_out1]
        block = ctx.enter_context(nc.Block())

        @block.sync
        def _(eng):
            def store(i, par):
                eng.wait_ge(s.t_ready, 2 * i + 2)
                eng.dma_start(e2t_dram[:, bass.ds(CT * i, CT)], e2t[:, par, :]).then_inc(e_out[par], 16)

            def body(i, par, r, last):
                at_least(eng, s.bn_done, 2 * (i - 1))
                for q in range(2):
                    eng.dma_start(cf[:, par, q, :], coef[q].rearrange("(n o b) t -> n o (b t)", o=1, b=NB)[i]
                                  .broadcast_to([P, CT])).then_inc(cf_in[par], 16)
                at_least(eng, s.fx_done, i - 1)
                eng.dma_start(le[:, par], le_dram[:, bass.ds(NB * i, NB), :]).then_inc(le_in[par], 16)
                at_least(eng, s.uo_ready, i - 1)
                hv = h_img.rearrange("(n a) g (t d) -> n t (a g) d", a=NB // G, d=D)
                eng.dma_start(hb[0:S, par], hv[i]).then_inc(h_in[par], 16)
                eng.dma_start(hb[S:T, par], txt.rearrange("(n b) t d -> n t b d", b=NB)[i]).then_inc(h_in[par], 16)
                if not (isinstance(i, int) and i < 2):
                    store(i - 2, par)

            walk(eng, n, body)
            store(n - 2, 0)
            store(n - 1, 1)
            eng.wait_ge(s.u_out0, 8 * n)
            eng.wait_ge(s.u_out1, 8 * n)

        @block.gpsimd
        def _(pool):
            def body(i, par, r, last):
                pool.wait_ge(cf_in[par], 32 * r + 32)
                for q in range(2):
                    xq = W["x"][:, q, bass.ds(CT * i, CT)]
                    nc.gpsimd.tensor_tensor(xq, xq, cf[:, par, 0, :], ALU.mult).then_inc(s.a_ready, 1)

            walk(pool, n, body)

        @block.scalar
        def _(act):
            def body(i, par, r, last):
                act.wait_ge(s.aggr, 3 * i + 1)
                nc.scalar.activation(w[:, 4], w[:, 3], ACT.Sqrt).then_inc(s.act_step, 1)
                for q in range(2):
                    act.wait_ge(s.t2_done, 2 * i + q + 1)
                    nc.scalar.copy(lat[:, HT * q:HT * q + HT], ps_t[q][:, 0:HT]).then_inc(s.a2_ready, 1)
                for k in range(2):
                    act.wait_ge(s.aggr, 3 * i + 2 + k)
                    nc.scalar.activation(w[:, 4], w[:, 3], ACT.Sqrt).then_inc(s.act_step, 1)
                if not (isinstance(i, int) and i < 2):
                    act.wait_ge(e_out[par], 16 * r)
                for q in range(2):
                    act.wait_ge(s.tt_done, 2 * i + q + 1)
                    nc.scalar.copy(e2t[:, par, HT * q:HT * q + HT], ps_t[q][:, 0:HT]).then_inc(s.t_ready, 1)
                act.wait_ge(s.um_done, i + 1)
                nc.scalar.copy(W["gate"][:, bass.ds(NB * i, NB), :],
                               ps_a[:, 0:8 * NB].rearrange("p (b e) -> p b e", b=NB)).then_inc(s.sp_ready, 1)

            walk(act, n, body)

        CHAIN = 2 + 10 + 4 + 10 + 1 + 10 + 1

        @block.vector
        def _(dve):
            ve = nc.vector

            def norm(c, src, out, i, k):
                for b in range(NB):
                    ve.bn_stats(st[:, b, :], src[:, b, :]).then_inc(s.st_done, 1)
                dve.wait_ge(s.st_done, NB * (3 * i + k + 1))
                norm_statistics(nc, c, st, w)
                dve.sem_inc(s.aggr, 1)
                dve.wait_ge(s.act_step, 3 * i + k + 1)
                c.then(ve.reciprocal(w[:, 5], w[:, 4]))
                c.then(ve.tensor_tensor(out[:, :, :], src, spread_over(w[:, 0], D), ALU.subtract))
                c.then(ve.tensor_tensor(out[:, :, :], out[:, :, :], spread_over(w[:, 5], D), ALU.mult))

            def body(i, par, r, last):
                c = Chain(dve, s.step, CHAIN * i)
                for q in range(2):
                    dve.wait_ge(s.a_ready, 2 * i + q + 1)
                    at_least(dve, s.ix_done, i - 1)
                    ve.tensor_tensor_scan(x[:, par, q, :], cf[:, par, 1, :], W["x"][:, q, bass.ds(CT * i, CT)], 0.0,
                                          ALU.mult, ALU.add).then_inc(s.bn_done, 1)
                decay = W["decay"][:, :].rearrange("s (o t) -> s o t", o=1).broadcast_to([T, 4, T])
                for q in range(2):
                    dve.wait_ge(s.fy_done, 2 * i + q + 1)
                    c.then(ve.tensor_tensor(sc[:, HT * q:HT * q + HT].rearrange("s (b t) -> s b t", b=4),
                                            ps_s[q][:, 0:HT].rearrange("s (b t) -> s b t", b=4), decay, ALU.mult))
                dve.wait_ge(s.fx_done, i + 1)
                norm(c, ps_a[:, :].rearrange("t (b d) -> t b d", b=NB), la, i, 0)
                dve.sem_inc(s.pw_ready, 1)
                for q in range(2):
                    for hh in range(2):
                        dve.wait_ge(s.mix_done, 4 * i + 2 * q + hh + 1)
                        c.then(ve.scalar_tensor_tensor(out=y[:, q, HT * hh:HT * hh + HT], in0=ps_y[hh][:, 0:HT], scalar=0.0,
                                                       in1=x[:, par, q, HT * hh:HT * hh + HT], op0=ALU.max, op1=ALU.mult))
                        dve.sem_inc(s.mix_low, 1)
                dve.wait_ge(s.ix_done, i + 1)
                norm(c, ps_v[:, :].rearrange("t (b d) -> t b d", b=NB), e2, i, 1)
                dve.wait_ge(h_in[par], 32 * r + 32)
                c.then(ve.tensor_tensor(hb[:, par], hb[:, par], e2[:, :, :], ALU.add))
                norm(c, hb[:, par], e2, i, 2)
                c.then(ve.tensor_copy(W["h2"][:, bass.ds(NB * i, NB), :], hb[:, par]))
                dve.sem_inc(s.uo_ready, 1)
                assert c.n == CHAIN

            walk(dve, n, body)

        @block.tensor
        def _(pe):
            def body(i, par, r, last):
                pe.wait_ge(s.bn_done, 2 * i + 2)
                for q in range(2):
                    for b in range(4):
                        t = HT * q + T * b
                        for half in range(2):
                            xb = x[:, par, half, t:t + T]
                            ins = nc.tensor.matmul(ps_s[q][:, T * b:T * b + T], xb, xb, start=(half == 0), stop=(half == 1))
                    ins.then_inc(s.fy_done, 1)
                pe.wait_ge(s.step, CHAIN * i + 2)
                pe.wait_ge(le_in[par], 16 * r + 16)
                at_least(pe, s.sp_ready, i)
                for b in range(NB):
                    ins = nc.tensor.matmul(ps_a[:, D * b:D * b + D], sc[:, T * b:T * b + T],
                                           le[:, par, b, :], start=True, stop=True)
                ins.then_inc(s.fx_done, 1)
                pe.wait_ge(s.pw_ready, i + 1)
                pe.nop(nofuse=True)
                for q in range(2):
                    for b in range(4):
                        ins = nc.tensor.transpose(ps_t[q][:, T * b:T * b + T], la[:, 4 * q + b, :], W["eye"][0:T, 0:T])
                    ins.then_inc(s.t2_done, 1)
                for q in range(2):
                    for hh in range(2):
                        if q == 0:
                            pe.wait_ge(s.a2_ready, 2 * i + hh + 1)
                            at_least(pe, s.mix_low, 4 * i + hh - 1)
                        else:
                            pe.wait_ge(s.mix_low, 4 * i + hh + 1)
                        nc.tensor.matmul(ps_y[hh][:, 0:HT], W["DyT"][:, P * q:P * q + P], lat[:, HT * hh:HT * hh + HT],
                                         start=True, stop=True).then_inc(s.mix_done, 1)
                pe.wait_ge(s.mix_low, 4 * i + 4)
                for b in range(NB):
                    for q in range(2):
                        ins = nc.tensor.matmul(ps_v[:, D * b:D * b + D], y[:, q, T * b:T * b + T], W["ET"][:, q, :],
                                               start=(q == 0), stop=(q == 1))
                ins.then_inc(s.ix_done, 1)
                pe.wait_ge(s.uo_ready, i + 1)
                pe.nop(nofuse=True)
                for q in range(2):
                    for b in range(4):
                        ins = nc.tensor.transpose(ps_t[q][:, T * b:T * b + T], e2[:, 4 * q + b, :], W["eye"][0:T, 0:T])
                    ins.then_inc(s.tt_done, 1)
                pe.wait_ge(s.t_ready, 2 * i + 2)
                for b in range(NB):
                    ins = nc.tensor.matmul(ps_a[:, 8 * b:8 * b + 8], e2t[:, par, T * b:T * b + T], W["Wr"][:, :],
                                           start=True, stop=True)
                ins.then_inc(s.um_done, 1)

            walk(pe, n, body)


def gate_phase(nc, sems, W, d):
    s = sems
    T, B, D = W["e"].shape
    E = 8
    with ExitStack() as ctx:
        def sb(name, shape):
            return ctx.enter_context(nc.sbuf_tensor("g_" + name, shape, F32))

        p, q, first, tmp = (sb(x, [T, B, E]) for x in ("p", "q", "first", "tmp"))
        m = sb("m", [T, 4, B])
        b2 = sb("b2", [P, 16, D])
        b2s = sb("b2s", [T, D])
        mt = sb("mt", [P, 2, T])
        rank = sb("rank", [T, E])
        pt = [ctx.enter_context(nc.psum_tensor(f"g_pt{b}", [P, CH], F32)) for b in range(2)]
        pb = [ctx.enter_context(nc.psum_tensor(f"g_pb{b}", [T, CH], F32)) for b in range(4)]
        gate = W["gate"]
        block = ctx.enter_context(nc.Block())

        def per_token(j):
            return m[:, j, :].rearrange("p (n o) -> p n o", o=1).broadcast_to([T, B, E])

        @block.sync
        def _(eng):
            eng.dma_start(b2s[:, :], d["b2s"].rearrange("(o d) -> o d", o=1).broadcast_to([T, D])).then_inc(s.in_a, 16)
            eng.wait_ge(s.w_fix, 1)
            for b in range(16):
                eng.dma_start(b2[E * b:E * b + E, b, :], d["b2p"]).then_inc(s.w_in, 16)

        @block.gpsimd
        def _(pool):
            nc.gpsimd.memset(b2[:, :, :], 0.0).then_inc(s.w_fix, 1)

        @block.scalar
        def _(act):
            act.wait_ge(s.aggr, 1)
            nc.scalar.activation(p[:, :, :], q[:, :, :], ACT.Exp).then_inc(s.act_step, 1)

        @block.tensor
        def _(pe):
            pe.wait_ge(s.w_in, 256)
            pe.wait_ge(s.aggr, 2)
            for t in range(B // 16):
                at_least(pe, s.vt_ready, t - 1)
                nc.tensor.transpose(pt[t % 2][:, 0:T], gate[:, 16 * t:16 * t + 16, :].rearrange("p b e -> p (b e)"),
                                    W["eye"][0:T, 0:T]).then_inc(s.tr_done, 1)
                pe.wait_ge(s.vt_ready, t + 1)
                at_least(pe, s.st_done, 2 * t - 2)
                for hh in range(2):
                    ins = nc.tensor.matmul(pb[2 * (t % 2) + hh][:, :], mt[:, t % 2, :],
                                           b2[:, 8 * hh:8 * hh + 8, :].rearrange("p b d -> p (b d)"), start=True, stop=True)
                ins.then_inc(s.fx_done, 1)

        @block.vector
        def _(dve):
            ve = nc.vector
            c = Chain(dve, s.step)
            for e in range(E):
                c.then(ve.memset(rank[:, e:e + 1], float(E - e)))
            ranks = rank[:, :].rearrange("p (o e) -> p o e", o=1).broadcast_to([T, B, E])
            c.then(ve.tensor_reduce(m[:, 0, :], gate[:, :, :], AX.X, ALU.max))
            c.then(ve.tensor_tensor(q[:, :, :], gate[:, :, :], per_token(0), ALU.subtract))
            dve.sem_inc(s.aggr, 1)
            dve.wait_ge(s.act_step, 1)
            c.then(ve.tensor_reduce(m[:, 0, :], p[:, :, :], AX.X, ALU.add))
            c.then(ve.reciprocal(m[:, 1, :], m[:, 0, :]))
            c.then(ve.tensor_tensor(p[:, :, :], p[:, :, :], per_token(1), ALU.mult))
            for k in range(2):
                c.then(ve.tensor_reduce(m[:, 2 + k, :], p[:, :, :], AX.X, ALU.max))
                c.then(ve.tensor_tensor(q[:, :, :], p[:, :, :], per_token(2 + k), ALU.is_equal))
                c.then(ve.tensor_tensor(q[:, :, :], q[:, :, :], ranks, ALU.mult))
                c.then(ve.tensor_reduce(m[:, 0, :], q[:, :, :], AX.X, ALU.max))
                c.then(ve.tensor_tensor(q[:, :, :], ranks, per_token(0), ALU.is_equal))
                c.then(ve.tensor_tensor(tmp[:, :, :], q[:, :, :], per_token(2 + k), ALU.mult))
                if k == 0:
                    c.then(ve.tensor_copy(first[:, :, :], tmp[:, :, :]))
                    c.then(ve.scalar_tensor_tensor(out=p[:, :, :], in0=q[:, :, :], scalar=-2.0, in1=p[:, :, :],
                                                   op0=ALU.mult, op1=ALU.add))
            c.then(ve.tensor_tensor(tmp[:, :, :], tmp[:, :, :], first[:, :, :], ALU.add))
            c.then(ve.tensor_tensor(m[:, 0, :], m[:, 2, :], m[:, 3, :], ALU.add))
            c.then(ve.reciprocal(m[:, 1, :], m[:, 0, :]))
            c.then(ve.tensor_tensor(gate[:, :, :], tmp[:, :, :], per_token(1), ALU.mult))
            dve.sem_inc(s.aggr, 1)
            dve.wait_ge(s.in_a, 16)
            h2 = W["h2"]
            c.then(ve.tensor_tensor(h2[:, :, :], h2[:, :, :],
                                    b2s[:, :].rearrange("p (o d) -> p o d", o=1).broadcast_to([T, B, D]), ALU.add))
            for t in range(B // 16):
                dve.wait_ge(s.tr_done, t + 1)
                at_least(dve, s.fx_done, t - 1)
                ve.tensor_copy(mt[:, t % 2, :], pt[t % 2][:, 0:T]).then_inc(s.vt_ready, 1)
                dve.wait_ge(s.fx_done, t + 1)
                for hh in range(2):
                    rows = h2[:, 16 * t + 8 * hh:16 * t + 8 * hh + 8, :]
                    ve.tensor_tensor(rows, rows, pb[2 * (t % 2) + hh][:, :].rearrange("p (b d) -> p b d", b=8), ALU.add)\
                        .then_inc(s.st_done, 1)


def expert_phase(nc, sems, W, d, out, e2t_dram):
    s = sems
    T, B, D = W["e"].shape
    E, NB = 8, 4
    n, CT = B // NB, NB * T
    TILES = 2 * (E + 1)
    with ExitStack() as ctx:
        def sb(name, shape):
            return ctx.enter_context(nc.sbuf_tensor("x_" + name, shape, F32))

        w1 = sb("w1", [D, E + 1, 2 * P])
        w2 = sb("w2", [P, E + 1, 2, D])
        b1 = sb("b1", [P, E + 1, 2])
        et = sb("et", [D, 2, CT])
        ht = sb("ht", [P, 4, CT])
        prod = sb("prod", [T, 2, E, D])
        part = sb("part", [T, NB, D])
        res = sb("res", [T, 2, NB, D])
        ps_h = [ctx.enter_context(nc.psum_tensor(f"x_ph{b}", [P, CH], F32)) for b in range(3)]
        ps_e = [ctx.enter_context(nc.psum_tensor(f"x_pe{b}", [T, CH], F32)) for b in range(4)]
        ps_s = ctx.enter_context(nc.psum_tensor("x_ps", [T, CH], F32))
        o_out, e_in = [s.u_out0, s.u_out1], [s.u_in0, s.u_in1]
        block = ctx.enter_context(nc.Block())

        @block.sync
        def _(eng):
            eng.dma_start(w1[:, 0, :], d["W1s"]).then_inc(s.w_in, 16)
            eng.dma_start(w1[:, 1:, :], d["W1p"].rearrange("e d f -> d e f")).then_inc(s.w_in, 16)
            eng.dma_start(w2[:, 0], d["W2s"].rearrange("(t p) d -> p t d", p=P)).then_inc(s.w_in, 16)
            for e in range(E):
                eng.dma_start(w2[:, 1 + e], d["W2p"][e].rearrange("(t p) d -> p t d", p=P)).then_inc(s.w_in, 16)
            with nc.allow_non_contiguous_dma("biases to partitions"):
                eng.dma_start(b1[:, 0, :], d["b1s"].rearrange("(t p) -> p t", p=P)).then_inc(s.w_in, 16)
                eng.dma_start(b1[:, 1:, :].rearrange("p e t -> p (e t)"),
                              d["b1p"].rearrange("e (t p) -> p (e t)", p=P)).then_inc(s.w_in, 16)
            ov = out.rearrange("(n b) t d -> n t b d", b=NB)

            def store(i, par):
                eng.wait_ge(s.uo_ready, i + 1)
                eng.dma_start(ov[i], res[:, par]).then_inc(o_out[par], 16)

            def body(i, par, r, last):
                at_least(eng, s.fy_done, TILES * (i - 1))
                eng.dma_start(et[:, par, :], e2t_dram[:, bass.ds(CT * i, CT)]).then_inc(e_in[par], 16)
                if not (isinstance(i, int) and i < 2):
                    store(i - 2, par)

            walk(eng, n, body)
            store(n - 2, 0)
            store(n - 1, 1)
            eng.wait_ge(s.u_out0, 8 * n)
            eng.wait_ge(s.u_out1, 8 * n)

        @block.scalar
        def _(act):
            act.wait_ge(s.w_in, 16 * 13)

            def body(i, par, r, last):
                for j in range(TILES):
                    t = TILES * i + j
                    act.wait_ge(s.fy_done, t + 1)
                    if not (isinstance(i, int) and i == 0 and j < 4):
                        act.wait_ge(s.fx_done, t - 3)
                    nc.scalar.activation(ht[:, (TILES * par + j) % 4, :], ps_h[j % 3][:, 0:CT], ACT.Gelu,
                                         bias=b1[:, j // 2, j % 2:j % 2 + 1]).then_inc(s.a_ready, 1)

            walk(act, n, body)

        @block.vector
        def _(dve):
            ve = nc.vector

            def body(i, par, r, last):
                if not (isinstance(i, int) and i < 2):
                    dve.wait_ge(o_out[par], 16 * r)
                dve.wait_ge(s.fx_done, TILES * i + 2)
                ve.tensor_tensor(res[:, par], W["h2"][:, bass.ds(NB * i, NB), :],
                                 ps_s[:, 0:NB * D].rearrange("p (b d) -> p b d", b=NB), ALU.add).then_inc(s.s_ready, 1)
                dve.wait_ge(s.fx_done, TILES * i + TILES)
                for b in range(NB):
                    at_least(dve, s.st_done, NB * i + b - 1)
                    g = W["gate"][:, bass.ds(NB * i + b, 1), :].rearrange("p o e -> p (o e)")
                    ve.tensor_tensor(prod[:, b % 2], ps_e[b][:, :].rearrange("p (e d) -> p e d", e=E),
                                     spread_over(g, D), ALU.mult).then_inc(s.t_ready, 1)
                    dve.wait_ge(s.t_ready, NB * i + b + 1)
                    ve.tensor_reduce(part[:, b, :], prod[:, b % 2].rearrange("p e d -> p d e"), AX.X, ALU.add)\
                        .then_inc(s.st_done, 1)
                dve.wait_ge(s.st_done, NB * i + NB)
                dve.wait_ge(s.s_ready, i + 1)
                ve.tensor_tensor(res[:, par], res[:, par], part[:, :, :], ALU.add).then_inc(s.uo_ready, 1)
                dve.wait_ge(s.uo_ready, i + 1)

            walk(dve, n, body)

        @block.tensor
        def _(pe):
            pe.wait_ge(s.w_in, 16 * 13)

            def hidden(i, par, r, j):
                t = TILES * i + j
                if j == 0:
                    pe.wait_ge(e_in[par], 16 * r + 16)
                if not (isinstance(i, int) and i == 0 and j < 3):
                    pe.wait_ge(s.a_ready, t - 2)
                nc.tensor.matmul(ps_h[j % 3][:, 0:CT], w1[:, j // 2, P * (j % 2):P * (j % 2) + P],
                                 et[:, par, :], start=True, stop=True).then_inc(s.fy_done, 1)

            def outputs(i, par, j):
                pe.wait_ge(s.a_ready, TILES * i + j + 1)
                e, half = j // 2, j % 2
                if j == 0:
                    at_least(pe, s.s_ready, i)
                for b in range(NB):
                    if j == 2:
                        at_least(pe, s.t_ready, NB * (i - 1) + b + 1)
                    if e == 0:
                        o, start = ps_s[:, D * b:D * b + D], half == 0 and b == 0
                    else:
                        o, start = ps_e[b][:, D * (e - 1):D * e], half == 0
                    ins = nc.tensor.matmul(o, ht[:, (TILES * par + j) % 4, T * b:T * b + T], w2[:, e, half, :],
                                           start=start, stop=(half == 1), skip_group_check=True)
                ins.then_inc(s.fx_done, 1)

            def body(i, par, r, last):
                for j in range(TILES):
                    hidden(i, par, r, j)
                    if j >= 1:
                        outputs(i, par, j - 1)
                outputs(i, par, TILES - 1)

            walk(pe, n, body)


def tokens(nc, ctx, sems, d, h_img, out):
    B, L, D = d["txt"].shape
    T = S + L

    def sb(name, shape, c=ctx):
        return c.enter_context(nc.sbuf_tensor("w_" + name, shape, F32))

    usum = nc.dram_tensor("update_sums", (B, T), F32).ap()
    coef = nc.dram_tensor("state_coefficients", (2, B, T), F32).ap()
    le_dram = nc.dram_tensor("normed_rows", (T, B, D), F32).ap()
    e2t_dram = nc.dram_tensor("expert_inputs", (D, B * T), F32).ap()
    W = {"gate": sb("gate", [T, B, 8]), "Wr": sb("Wr", [D, 8]), "eye": sb("eye", [P, P]), "h2": sb("h2", [T, B, D])}
    W["e"] = W["h2"]
    with nc.Block() as block:
        @block.sync
        def _(eng):
            eng.dma_start(W["Wr"][:, :], d["Wr"]).then_inc(sems.const_in, 16)
            eng.dma_start(W["eye"][:, :], d["eye"]).then_inc(sems.const_in, 16)
            eng.wait_ge(sems.const_in, 32)
    end_phase(nc, sems)
    with ExitStack() as c:
        for name, shape in (("DxT", [D, 2 * P]), ("DyT", [D, 2 * P]), ("ET", [P, 2, D]), ("decay", [T, T]), ("ones", [P, 1])):
            W[name] = sb(name, shape, c)
        token_norm_phase(nc, sems, W, h_img, d["txt"], d, le_dram)
        end_phase(nc, sems)
        W["x"] = sb("x", [P, 2, B * T], c)
        update_phase(nc, sems, W, usum)
        end_phase(nc, sems)
        decay_phase(nc, sems, usum, coef)
        end_phase(nc, sems)
        attention_phase(nc, sems, W, h_img, d["txt"], coef, le_dram, e2t_dram)
        end_phase(nc, sems)
    gate_phase(nc, sems, W, d)
    end_phase(nc, sems)
    expert_phase(nc, sems, W, d, out, e2t_dram)
    end_phase(nc, sems)

def program(nc, d, out):
    B = d["x"].shape[0]
    h_img = nc.dram_tensor("image_rows", (B // G, G, PX), F32).ap()
    with ExitStack() as ctx:
        sems = Semaphores(ctx, nc)
        with ExitStack() as c:
            operator(nc, c, sems, d, h_img)
        tokens(nc, ctx, sems, d, h_img, out)


INPUTS = ("x", "txt", "L0_tok_p_w", "L0_tok_p_b", "L0_tok_fw1", "L0_tok_fw2", "L0_tok_w_w", "L0_tok_w_b", "L0_tok_bn_g",
          "L0_tok_bn_b", "L0_tok_q_w", "L0_tok_q_b", "L0_attn_E", "L0_attn_Dx", "L0_attn_Dy", "L0_ffn_Wr", "L0_ffn_W1s",
          "L0_ffn_b1s", "L0_ffn_W2s", "L0_ffn_b2s", "L0_ffn_W1p", "L0_ffn_b1p", "L0_ffn_W2p", "L0_ffn_b2p")


def kernel(**inputs):
    from concourse import bacc
    from concourse.bass_utils import run_bass_kernel_spmd

    nc = bacc.Bacc("TRN2", target_bir_lowering=False, num_devices=1)
    arrays, d = {}, {}
    named = [(n, n.split("_", 2)[2] if n.startswith("L0_") else n, inputs[n]) for n in INPUTS]
    B, L, D = inputs["txt"].shape
    consts = {**shape_constants(), **token_constants(S + L, D)}
    named += [("const_" + n, n, a) for n, a in consts.items()]
    for full, short, a in named:
        a = np.ascontiguousarray(a)
        arrays[f"in_{full}_dram"] = a
        d[short] = nc.dram_tensor(f"in_{full}_dram", a.shape, mybir.dt.from_np(a.dtype), kind="ExternalInput").ap()
    out = nc.dram_tensor("out_0_dram", (B, S + L, D), F32, kind="ExternalOutput").ap()
    program(nc, d, out)
    r = run_bass_kernel_spmd(nc, [arrays], core_ids=[0])
    return r.results[0]["out_0_dram"]
```

```python
from contextlib import ExitStack

import numpy as np

import concourse.bass as bass
from concourse import mybir

F32 = mybir.dt.float32
BF16 = mybir.dt.bfloat16
ALU = mybir.AluOpType
ACT = mybir.ActivationFunctionType
AX = mybir.AxisListType

P = 128
S = 64
C = 32
G = P // C
PX = S * S
M1 = M2 = 12
KX = 2 * M1
MODES = M1 * M2
SPEC = KX * M2
ROW = M2 * C
CH = 512
NCH = PX // CH
EPS = 1e-5
DECAY = 0.97


def shape_constants():
    f = np.float64
    ang = 2 * np.pi / S
    y = np.arange(S, dtype=f)
    ky = np.arange(M2, dtype=f)
    kx = np.concatenate([np.arange(M1), np.arange(S - M1, S)]).astype(f)
    eye4 = np.eye(4)
    row = np.zeros((S, 32))
    row[:, 0:2 * M2:2] = np.cos(ang * np.outer(y, ky))
    row[:, 1:2 * M2:2] = -np.sin(ang * np.outer(y, ky))
    dfty = np.stack([np.kron(eye4, row[32 * t:32 * t + 32]) for t in range(2)], 1)
    wt = np.where(ky == 0, 1.0, 2.0)[:, None] / S
    inv = np.zeros((32, S))
    inv[0:2 * M2:2] = wt * np.cos(ang * np.outer(ky, y))
    inv[3:2 * M2:2] = (-wt * np.sin(ang * np.outer(ky, y)))[1:]
    idfty = np.kron(eye4, inv)
    r, a_, b_ = (t.reshape(-1) for t in np.meshgrid(range(4), range(4), range(4), indexing="ij"))
    x = 16 * r + 4 * a_ + b_
    c, sn = np.cos(ang * np.outer(x, kx)), np.sin(ang * np.outer(x, kx))
    dftx = np.zeros((P, 2, 2, 2, 32))
    idftx = np.zeros((2, 2, 32, 2, P))
    for h in range(2):
        p = 32 * a_ + 16 * h + 4 * r + b_
        dftx[p, 0, 0, h, :KX], dftx[p, 1, 0, h, :KX] = c, sn
        dftx[p, 0, 1, h, :KX], dftx[p, 1, 1, h, :KX] = -sn, c
        p = 32 * b_ + 16 * h + 4 * a_ + r
        for k in range(KX):
            idftx[0, h, k, 0, p], idftx[1, h, k, 0, p] = c[:, k] / S, -sn[:, k] / S
            idftx[0, h, k, 1, p], idftx[1, h, k, 1, p] = sn[:, k] / S, c[:, k] / S
    lin = np.linspace(0.0, 1.0, S, dtype=np.float32)
    planes = np.stack([np.broadcast_to(lin[:, None], (S, S)), np.broadcast_to(lin[None], (S, S)), np.ones((S, S))])
    px = planes.reshape(3, 4, 4, 4, S).transpose(0, 2, 1, 3, 4)
    px = np.broadcast_to(px[:, :, None], (3, 4, G, 4, 4, S)).reshape(12, PX)
    ft = np.fft.fft2(planes.astype(f))[:, kx.astype(int)][..., :M2]
    ft = np.stack([ft.real, ft.imag], 0)
    out = {
        "dfty": dfty, "dftx": dftx.reshape(P, 2, P), "idftx": idftx.reshape(P, 2, P), "idfty": idfty,
        "eye": np.eye(P), "groupmean": np.tile(np.eye(C), (4, 4)) / 4, "grid_px": px, "grid_ft": ft.reshape(2, 3, 2 * MODES),
    }
    return {k: np.ascontiguousarray(v, dtype=np.float32) for k, v in out.items()}


def at_least(eng, sem, value):
    if isinstance(value, int) and value <= 0:
        return
    eng.wait_ge(sem, value)


def walk(eng, n, body):
    if n == 1:
        body(0, 0, 0, True)
        return
    body(0, 0, 0, False)
    body(1, 1, 0, n == 2)
    if n > 4:
        with eng.Fori(1, n // 2 - 1) as m:
            body(2 * m, 0, m, False)
            body(2 * m + 1, 1, m, False)
    if n > 2:
        body(n - 2, 0, n // 2 - 1, False)
        body(n - 1, 1, n // 2 - 1, True)


class Semaphores:

    def __init__(self, ctx, nc):
        def sem(name):
            return ctx.enter_context(nc.semaphore(name))

        self.in_a = sem("in_a")
        self.in_b = sem("in_b")
        self.par_in = sem("par_in")
        self.const_in = sem("const_in")
        self.u_in0 = sem("u_in0")
        self.u_in1 = sem("u_in1")
        self.y_in0 = sem("y_in0")
        self.y_in1 = sem("y_in1")
        self.bn_done = sem("bn_done")
        self.tr_done = sem("tr_done")
        self.vt_ready = sem("vt_ready")
        self.fy_done = sem("fy_done")
        self.a_ready = sem("a_ready")
        self.t2_done = sem("t2_done")
        self.a2_ready = sem("a2_ready")
        self.fx_done = sem("fx_done")
        self.sp_ready = sem("sp_ready")
        self.sp_out0 = sem("sp_out0")
        self.sp_out1 = sem("sp_out1")
        self.w_in = sem("w_in")
        self.w_tmp = sem("w_tmp")
        self.w_fix = sem("w_fix")
        self.mix_done = sem("mix_done")
        self.mix_low = sem("mix_low")
        self.mix_high = sem("mix_high")
        self.y_out0 = sem("y_out0")
        self.y_out1 = sem("y_out1")
        self.ix_done = sem("ix_done")
        self.s_ready = sem("s_ready")
        self.tt_done = sem("tt_done")
        self.t_ready = sem("t_ready")
        self.um_done = sem("um_done")
        self.uo_ready = sem("uo_ready")
        self.st_done = sem("st_done")
        self.u_out0 = sem("u_out0")
        self.u_out1 = sem("u_out1")
        self.step = sem("step")
        self.aggr = sem("aggr")
        self.pe_step = sem("pe_step")
        self.act_step = sem("act_step")
        self.hq_done = sem("hq_done")
        self.hq_ready = sem("hq_ready")
        self.hq_out0 = sem("hq_out0")
        self.hq_out1 = sem("hq_out1")
        self.pw_done = sem("pw_done")
        self.pw_ready = sem("pw_ready")
        self.range = range(self.in_a.num, self.pw_ready.num + 1)


def end_phase(nc, sems):
    nc.gpsimd.sem_clear(sems.range)
    nc.all_engine_barrier()


def forward_phase(nc, sems, tag, K, load, n, spectrum, scale_bias, load_weights):
    s = sems
    with ExitStack() as ctx:
        u = ctx.enter_context(nc.sbuf_tensor(f"f_u{tag}", [P, 2, PX], F32))
        vt = ctx.enter_context(nc.sbuf_tensor(f"f_vt{tag}", [P, 2, 1024], F32))
        at = ctx.enter_context(nc.sbuf_tensor(f"f_at{tag}", [P, 2, 2, C, 32], F32))
        sp = ctx.enter_context(nc.sbuf_tensor(f"f_sp{tag}", [P, 2, 2, 32, M2], F32))
        pf = ctx.enter_context(nc.psum_tensor(f"f_pf{tag}", [P, 2, 2, CH], F32))
        px = ctx.enter_context(nc.psum_tensor(f"f_px{tag}", [P, 2, CH], F32))
        u_in, sp_out = [s.u_in0, s.u_in1], [s.sp_out0, s.sp_out1]
        block = ctx.enter_context(nc.Block())

        @block.sync
        def _(eng):
            def store(i, par):
                eng.wait_ge(s.sp_ready, 2 * i + 2)
                eng.dma_start(spectrum(i).rearrange("q p m -> p q m"),
                              sp[:, par].rearrange("p q x k -> p q (x k)")[:, :, 0:SPEC]).then_inc(sp_out[par], 16)

            def body(i, par, r, last):
                at_least(eng, s.vt_ready, 4 * (i - 1))
                load(eng, u[:, par], i, u_in[par])
                if isinstance(i, int) and i == min(n - 1, 1):
                    load_weights(eng)
                if not (isinstance(i, int) and i < 2):
                    store(i - 2, par)

            walk(eng, n, body)
            for i in range(max(n - 2, 0), n):
                store(i, i % 2)
            eng.wait_ge(s.sp_out0, 16 * ((n + 1) // 2))
            if n > 1:
                eng.wait_ge(s.sp_out1, 16 * (n // 2))

        @block.gpsimd
        def _(pool):
            turn_weights(pool, s.w_in, s.w_fix, K, 0)
            if n > 1:
                turn_weights(pool, s.w_in, s.w_fix, K, 1, 3 * PIECES)

        @block.scalar
        def _(act):
            def body(i, par, r, last):
                act.wait_ge(u_in[par], 16 * load.count * (r + 1))
                for k in range(4):
                    t = u[:, par, 1024 * k:1024 * k + 1024]
                    nc.scalar.activation(t, t, ACT.Relu, bias=scale_bias[1], scale=scale_bias[0]).then_inc(s.bn_done, 1)

            if scale_bias is not None:
                walk(act, n, body)

        @block.vector
        def _(dve):
            ve = nc.vector

            def pixels_turn(i, par, g):
                if scale_bias is not None:
                    dve.wait_ge(s.bn_done, 4 * i + g + 1)
                elif g == 0:
                    dve.wait_ge(u_in[par], 16 * load.count)
                at_least(dve, s.fy_done, 4 * i + g - 1)
                ve.transpose(vt[:, g % 2, :], u[:, par, 1024 * g:1024 * g + 1024]).then_inc(s.vt_ready, 1)

            def rows_turn(i, par, q):
                dve.wait_ge(s.fy_done, 4 * i + 2 * q + 2)
                at_least(dve, s.fx_done, 2 * (i - 1))
                ve.transpose(at[:, par, q], pf[:, q].rearrange("p h (x c) -> p c h x", c=C)).then_inc(s.a2_ready, 1)

            def modes_turn(i, par, q, r):
                dve.wait_ge(s.fx_done, 2 * i + q + 1)
                if q == 0 and not (isinstance(i, int) and i < 2):
                    dve.wait_ge(sp_out[par], 16 * r)
                ve.transpose(sp[:, par, q].rearrange("p x k -> p k x"),
                             px[:, q, 0:ROW].rearrange("p (k c) -> p k c", c=C)).then_inc(s.sp_ready, 1)

            def body(i, par, r, last):
                later = not (isinstance(i, int) and i == 0)
                pixels_turn(i, par, 0)
                if later:
                    rows_turn(i - 1, 1 - par, 1)
                pixels_turn(i, par, 1)
                if later:
                    modes_turn(i - 1, 1 - par, 1, 0)
                pixels_turn(i, par, 2)
                rows_turn(i, par, 0)
                pixels_turn(i, par, 3)
                modes_turn(i, par, 0, r)
                if last:
                    rows_turn(i, par, 1)
                    modes_turn(i, par, 1, r)

            walk(dve, n, body)
            if n == 1:
                turn_weights(dve, s.w_in, s.w_tmp, K, 1)

        @block.tensor
        def _(pe):
            def transform_y(i, g):
                pe.wait_ge(s.vt_ready, 4 * i + g + 1)
                if g % 2 == 0:
                    at_least(pe, s.a2_ready, 2 * (i - 1) + g // 2 + 1)
                rhs = vt[:, g % 2, :].rearrange("p (x t c) -> p t x c", t=2, c=C)
                for t in range(2):
                    ins = nc.tensor.matmul(pf[:, g // 2, g % 2, :], K["dfty"][:, t, :], rhs[:, t],
                                           start=(t == 0), stop=(t == 1))
                ins.then_inc(s.fy_done, 1)

            def transform_x(i, par, q):
                pe.wait_ge(s.a2_ready, 2 * i + q + 1)
                at_least(pe, s.sp_ready, 2 * (i - 1) + q + 1)
                rhs = at[:, par, q].rearrange("p c (k r) -> p r k c", r=2)
                for t in range(2):
                    ins = nc.tensor.matmul(px[:, q, 0:ROW], K["dftx"][:, t, :], rhs[:, t, 0:M2],
                                           start=(t == 0), stop=(t == 1))
                ins.then_inc(s.fx_done, 1)

            def body(i, par, r, last):
                transform_y(i, 0)
                if not (isinstance(i, int) and i == 0):
                    transform_x(i - 1, 1 - par, 1)
                transform_y(i, 1)
                transform_y(i, 2)
                transform_x(i, par, 0)
                transform_y(i, 3)
                if last:
                    transform_x(i, par, 1)

            walk(pe, n, body)


PIECES = 4


def turn_weights(eng, w_in, done, K, h, base=0):
    w, tmp = K["mixw"], K["mixtmp"]
    eng.wait_ge(w_in, 128)
    rows = slice(2 * h * C + C, 2 * h * C + 2 * C)
    size = 2 * C * MODES // PIECES
    flat = w[rows].rearrange("p k m r -> p (k m) r")
    for t in range(PIECES):
        re, im = (flat[:, size * t:size * t + size, j] for j in range(2))
        at_least(eng, done, base + 3 * t)
        eng.tensor_copy(tmp[rows, :], re).then_inc(done, 1)
        eng.wait_ge(done, base + 3 * t + 1)
        eng.tensor_scalar(re, im, -1.0, None, ALU.mult).then_inc(done, 1)
        eng.wait_ge(done, base + 3 * t + 2)
        eng.tensor_copy(im, tmp[rows, :]).then_inc(done, 1)
    eng.wait_ge(done, base + 3 * PIECES)


def weight_loader(s, K, fw1, fw2, layer):
    def load(eng):
        for k, fw in enumerate((fw1, fw2)):
            src = fw[layer].rearrange("i o x y r -> i (o x y) r")
            for block in range(4):
                eng.dma_start(K["mixw"][C * block:C * block + C, k], src).then_inc(s.w_in, 16)
    return load


def mix_phase(nc, sems, tag, K, B, xsp, ysp, par, layer, first, consts):
    s = sems
    HB = B // 2
    with ExitStack() as ctx:
        xm = ctx.enter_context(nc.sbuf_tensor(f"m_x{tag}", [P, 2, HB, MODES], F32))
        ys = ctx.enter_context(nc.sbuf_tensor(f"m_y{tag}", [P, 2, 2, ROW], F32))
        bank = [ctx.enter_context(nc.psum_tensor(f"m_p{tag}{b}", [P, CH], F32)) for b in range(4)]
        pp = [ctx.enter_context(nc.psum_tensor(f"m_pp{tag}{b}", [P, CH], F32)) for b in range(2)]
        wv = K["mixw"][:, :, :, :].rearrange("p k (o x y) r -> p k o x y r", o=C, x=M1)
        wflat = K["mixw"][:, :, :, :].rearrange("p k m r -> p (k m r)")
        folds = 4 * C * MODES // CH
        x_in, y_out = [s.in_a, s.in_b], [s.y_out0, s.y_out1]
        block = ctx.enter_context(nc.Block())

        @block.sync
        def _(eng):
            for k in range(2):
                cut = slice(MODES * k, MODES * k + MODES)
                for h in range(2):
                    for ri in range(2):
                        if first:
                            a = 64 * h + 4 * ri
                            eng.dma_start(xm[a:a + 1, k].rearrange("o (n q) m -> o n q m", q=2),
                                          xsp.rearrange("q (r h o n) m -> r h o n q m", r=2, h=2, o=1)[ri, h][:, :, :, cut])\
                                .then_inc(x_in[k], 16)
                            eng.dma_start(xm[a + 1:a + 4, k], consts["grid_ft"][ri][:, cut].rearrange("j (o m) -> j o m", o=1)
                                          .broadcast_to([3, HB, MODES])).then_inc(x_in[k], 16)
                        else:
                            a = 64 * h + 32 * ri
                            eng.dma_start(xm[a:a + C, k], xsp.rearrange("b (r h c) m -> r h c b m", r=2, h=2)[ri, h][:, :, cut])\
                                .then_inc(x_in[k], 16)
            for q in range(KX):
                eng.wait_ge(s.mix_low, q + 1)
                eng.wait_ge(s.mix_high, q + 1)
                for h in range(2):
                    eng.dma_start(ysp.rearrange("b (r h x) m -> h x b r m", r=2, h=2)[h, q],
                                  ys[64 * h:64 * h + HB, q % 2]).then_inc(y_out[q % 2], 16)
            eng.wait_ge(s.y_out0, 16 * KX)
            eng.wait_ge(s.y_out1, 16 * KX)

        @block.scalar
        def _(act):
            for g in range(4):
                rows = slice(C * g, C * g + C)
                act.dma_start(K["wbd"][rows, rows], par["w_w"][layer]).then_inc(s.par_in, 16)
                for name in ("w_b", "bn_g", "bn_b"):
                    act.dma_start(K[name][rows, :], par[name][layer].rearrange("(c o) -> c o", o=1)).then_inc(s.par_in, 16)
            for q in range(KX):
                act.wait_ge(s.mix_done, 2 * q + 2)
                if q >= 2:
                    act.wait_ge(y_out[q % 2], 32 * (q // 2))
                out = ys[:, q % 2].rearrange("b r (k c) -> b r k c", c=C)[:, :, 6:12, :]
                nc.scalar.copy(out, bank[(2 * q + 1) % 4][:, 0:ROW]).then_inc(s.mix_high, 1)
            act.wait_ge(s.par_in, 16 * 16)

        @block.vector
        def _(dve):
            if first:
                for n in range(folds):
                    dve.wait_ge(s.pw_done, n + 1)
                    nc.vector.tensor_copy(wflat[:, CH * n:CH * n + CH], pp[n % 2][:, :]).then_inc(s.pw_ready, 1)
                dve.wait_ge(s.pw_done, folds + 1)
                nc.vector.tensor_copy(K["pwbd"][:, :], pp[1][0:16, 0:P]).then_inc(s.pw_ready, 1)
            for q in range(KX):
                dve.wait_ge(s.mix_done, 2 * q + 1)
                if q >= 2:
                    dve.wait_ge(y_out[q % 2], 32 * (q // 2))
                out = ys[:, q % 2].rearrange("b r (k c) -> b r k c", c=C)[:, :, 0:6, :]
                nc.vector.tensor_copy(out, bank[2 * q % 4][:, 0:ROW]).then_inc(s.mix_low, 1)

        @block.tensor
        def _(pe):
            if first:
                for n in range(folds):
                    at_least(pe, s.pw_ready, n - 1)
                    nc.tensor.matmul(pp[n % 2][:, :], K["lift_mix"][:, :], wflat[:, CH * n:CH * n + CH],
                                     start=True, stop=True).then_inc(s.pw_done, 1)
                pe.wait_ge(s.par_in, 16 * 16)
                pe.wait_ge(s.pw_ready, folds)
                nc.tensor.matmul(pp[1][0:16, 0:P], K["lift_px"][:, :], K["wbd"][:, :],
                                 start=True, stop=True).then_inc(s.pw_done, 1)
            depth = 8 if first else 2 * C
            for q in range(KX):
                k, x = q // M1, q % M1
                if x == 0:
                    pe.wait_ge(x_in[k], 128 if first else 64)
                for half in range(2):
                    n = 2 * q + half
                    at_least(pe, s.mix_high if half else s.mix_low, q - 1)
                    for t in range(6):
                        y = 6 * half + t
                        for h in range(2):
                            rows = slice(64 * h, 64 * h + depth)
                            out = bank[n % 4][64 * h:64 * h + HB, 0:ROW].rearrange("b (r k c) -> b k c r", r=2, k=6)[:, t]
                            ins = nc.tensor.matmul(out, xm[rows, k, :, M2 * x + y], wv[rows, k, :, x, y, :],
                                                   start=True, stop=True)
                    ins.then_inc(s.mix_done, 1)


def inverse_phase(nc, sems, tag, K, U, ysp, n, images, scale_bias, stats):
    s = sems
    first = images is not None
    with ExitStack() as ctx:
        v = ctx.enter_context(nc.sbuf_tensor(f"i_v{tag}", [16 if first else P, 2, PX], F32))
        ysb = ctx.enter_context(nc.sbuf_tensor(f"i_y{tag}", [P, 2, 2, ROW], F32))
        st = ctx.enter_context(nc.sbuf_tensor(f"i_t{tag}", [P, 2, 2, C, 32], F32))
        uo = ctx.enter_context(nc.sbuf_tensor(f"i_u{tag}", [P, 2, PX], F32))
        ps_x = ctx.enter_context(nc.psum_tensor(f"i_px{tag}", [P, 2, CH], F32))
        ps_u = [ctx.enter_context(nc.psum_tensor(f"i_pu{tag}{b}", [P, CH], F32)) for b in range(4)]
        u_in, y_in, u_out = [s.u_in0, s.u_in1], [s.y_in0, s.y_in1], [s.u_out0, s.u_out1]
        loads = 4 if first else 1
        block = ctx.enter_context(nc.Block())

        @block.sync
        def _(eng):
            if first:
                for par in range(2):
                    eng.dma_start(v[4:16, par], K["grid_px"]).then_inc(s.const_in, 16)

            def store(i, par):
                eng.wait_ge(s.uo_ready, NCH * i + NCH)
                eng.dma_start(U[i], uo[:, par]).then_inc(u_out[par], 16)

            def body(i, par, r, last):
                at_least(eng, s.ix_done, 4 * (i - 1))
                eng.dma_start(ysb[:, par], ysp[bass.ds(2 * i, 2)].rearrange("q p m -> p q m")).then_inc(y_in[par], 16)
                at_least(eng, s.um_done, NCH * (i - 1))
                if first:
                    img = images.rearrange("(n g) (r a b) y -> n a g r (b y)", g=G, r=4, a=4)[i]
                    for a in range(4):
                        eng.dma_start(v[a:a + 1, par].rearrange("o (g r m) -> o g r m", g=G, r=4), img[a:a + 1])\
                            .then_inc(u_in[par], 16)
                else:
                    eng.dma_start(v[:, par], U[i]).then_inc(u_in[par], 16)
                if not (isinstance(i, int) and i < 2):
                    store(i - 2, par)

            walk(eng, n, body)
            store(n - 2, 0)
            store(n - 1, 1)
            eng.wait_ge(s.u_out0, 8 * n)
            eng.wait_ge(s.u_out1, 8 * n)

        @block.scalar
        def _(act):
            def norm(i, par, r):
                act.wait_ge(u_in[par], 16 * r + 16)
                for k in range(4):
                    px = v[:, par, 1024 * k:1024 * k + 1024]
                    nc.scalar.activation(px, px, ACT.Relu, bias=scale_bias[1], scale=scale_bias[0])\
                        .then_inc(s.bn_done, 1)

            def body(i, par, r, last):
                if not first and isinstance(i, int) and i == 0:
                    norm(0, 0, 0)
                for k in range(NCH):
                    c = NCH * i + k
                    act.wait_ge(s.um_done, c + 1)
                    if k == 0 and not (isinstance(i, int) and i < 2):
                        act.wait_ge(u_out[par], 16 * r)
                        act.wait_ge(s.st_done, NCH * (i - 1))
                    nc.scalar.activation(uo[:, par, CH * k:CH * k + CH], ps_u[k % 4][:, :], ACT.Identity,
                                         bias=K["w_b"][:, 0:1]).then_inc(s.uo_ready, 1)
                    if k == 3 and not first and not last:
                        norm(i + 1, 1 - par, r if par == 0 else r + 1)

            walk(act, n, body)

        def turned(dve, i, par, j):
            dve.wait_ge(s.ix_done, 4 * i + j + 1)
            at_least(dve, s.um_done, NCH * (i - 1))
            nc.vector.transpose(st[:, par, j // 2, 16 * (j % 2):16 * (j % 2) + 16, :],
                                ps_x[:, j % 2, :].rearrange("p (c k) -> p c k", k=32)).then_inc(s.t_ready, 1)

        @block.vector
        def _(dve):
            for b in range(2):
                nc.vector.memset(ps_x[:, b, :], 0.0).then_inc(s.s_ready, 1)
            for j in range(4):
                turned(dve, 0, 0, j)

            def body(i, par, r, last):
                for k in range(NCH):
                    c = NCH * i + k
                    dve.wait_ge(s.uo_ready, c + 1)
                    nc.vector.bn_stats(stats[:, bass.ds(6 * c, 6)], uo[:, par, CH * k:CH * k + CH])\
                        .then_inc(s.st_done, 1)
                    if not last and k % 2 == 1:
                        turned(dve, i + 1, 1 - par, k // 2)

            walk(dve, n, body)

        @block.tensor
        def _(pe):
            def inverse_x(i, par, r, j):
                if j == 0:
                    pe.wait_ge(y_in[par], 16 * r + 16)
                at_least(pe, s.t_ready, 4 * i + j - 1)
                rhs = ysb[:, par, j // 2, :].rearrange("p (k c) -> p c k", c=C)[:, 16 * (j % 2):16 * (j % 2) + 16, :]
                out = ps_x[:, j % 2, :].rearrange("p (c k r) -> p r c k", k=16, r=2)
                for t in range(2):
                    ins = nc.tensor.matmul(out[:, t, :, 0:M2], K["idftx"][:, t, :], rhs, start=True, stop=True,
                                           skip_group_check=True)
                ins.then_inc(s.ix_done, 1)

            def pixels(i, par, r, k):
                c = NCH * i + k
                if first:
                    if k == 0:
                        pe.wait_ge(s.const_in, 32)
                        pe.wait_ge(u_in[par], 16 * loads * (r + 1))
                else:
                    pe.wait_ge(s.bn_done, 4 * i + k // 2 + 1)
                pe.wait_ge(s.t_ready, 4 * i + 2 * (k // 4) + 2)
                at_least(pe, s.uo_ready, c - 3)
                weights = K["pwbd"] if first else K["wbd"]
                bank = ps_u[k % 4]
                nc.tensor.matmul(bank[:, :], weights[:, :], v[:, par, CH * k:CH * k + CH], start=True, stop=False,
                                 skip_group_check=True)
                g = k // 2
                for e in range(2):
                    for a in range(4):
                        rr = 2 * (k % 2) + e
                        ins = nc.tensor.matmul(bank[32 * a:32 * a + 32, 256 * e:256 * e + 256],
                                               st[:, par, g // 2, :, 16 * (g % 2) + 4 * a + rr], K["idfty"][:, :],
                                               start=False, stop=True, skip_group_check=True)
                ins.then_inc(s.um_done, 1)

            pe.wait_ge(s.s_ready, 2)
            for j in range(4):
                inverse_x(0, 0, 0, j)

            def body(i, par, r, last):
                for k in range(NCH):
                    pixels(i, par, r, k)
                    if not last and k % 2 == 0:
                        inverse_x(i + 1, 1 - par, r if par == 0 else r + 1, k // 2)

            walk(pe, n, body)


def norm_phase(nc, sems, tag, K, n, stats, scale_bias):
    s = sems
    scale, bias = scale_bias
    with ExitStack() as ctx:
        mv = ctx.enter_context(nc.sbuf_tensor(f"n_mv{tag}", [P, 2], F32))
        avg = ctx.enter_context(nc.sbuf_tensor(f"n_avg{tag}", [P, 2], F32))
        dm = ctx.enter_context(nc.sbuf_tensor(f"n_dm{tag}", [P, 2], F32))
        sd = ctx.enter_context(nc.sbuf_tensor(f"n_sd{tag}", [P, 4], F32))
        ps = ctx.enter_context(nc.psum_tensor(f"n_ps{tag}", [P, CH], F32))
        block = ctx.enter_context(nc.Block())

        @block.vector
        def _(dve):
            count = 0

            def then(ins):
                nonlocal count
                count += 1
                ins.then_inc(s.step, 1)
                dve.wait_ge(s.step, count)

            then(nc.vector.bn_aggr(mv[:, :], stats[:, 0:6 * NCH * n]))
            dve.sem_inc(s.aggr, 1)
            dve.wait_ge(s.pe_step, 1)
            then(nc.vector.tensor_copy(avg[:, :], ps[:, 0:2]))
            then(nc.vector.tensor_tensor(dm[:, 0:1], mv[:, 0:1], avg[:, 0:1], ALU.subtract))
            then(nc.vector.tensor_tensor(dm[:, 1:2], dm[:, 0:1], dm[:, 0:1], ALU.mult))
            dve.sem_inc(s.aggr, 1)
            dve.wait_ge(s.pe_step, 2)
            then(nc.vector.tensor_tensor(sd[:, 0:1], avg[:, 1:2], ps[:, 2:3], ALU.add))
            then(nc.vector.tensor_scalar(sd[:, 1:2], sd[:, 0:1], EPS, None, ALU.add))
            dve.sem_inc(s.aggr, 1)
            dve.wait_ge(s.act_step, 1)
            then(nc.vector.reciprocal(sd[:, 3:4], sd[:, 2:3]))
            then(nc.vector.tensor_tensor(scale, sd[:, 3:4], K["bn_g"][:, 0:1], ALU.mult))
            then(nc.vector.tensor_tensor(sd[:, 0:1], avg[:, 0:1], scale, ALU.mult))
            then(nc.vector.tensor_tensor(bias, K["bn_b"][:, 0:1], sd[:, 0:1], ALU.subtract))

        @block.scalar
        def _(act):
            act.wait_ge(s.aggr, 3)
            nc.scalar.activation(sd[:, 2:3], sd[:, 1:2], ACT.Sqrt).then_inc(s.act_step, 1)

        @block.tensor
        def _(pe):
            pe.wait_ge(s.aggr, 1)
            nc.tensor.matmul(ps[:, 0:2], K["groupmean"][:, :], mv[:, :], start=True, stop=True).then_inc(s.pe_step, 1)
            pe.wait_ge(s.aggr, 2)
            nc.tensor.matmul(ps[:, 2:3], K["groupmean"][:, :], dm[:, 1:2], start=True, stop=True).then_inc(s.pe_step, 1)


def project_phase(nc, sems, K, U, n, h_img, scale_bias, q_w, q_b):
    s = sems
    scale, bias = scale_bias
    with ExitStack() as ctx:
        u = ctx.enter_context(nc.sbuf_tensor("proj_u", [P, 2, PX], F32))
        hb = ctx.enter_context(nc.sbuf_tensor("proj_h", [P, 2, 2, CH], F32))
        qbd = ctx.enter_context(nc.sbuf_tensor("proj_w", [P, P], F32))
        qc = ctx.enter_context(nc.sbuf_tensor("proj_c", [P, 4], F32))
        qbias = ctx.enter_context(nc.sbuf_tensor("proj_b", [P, 1], F32))
        ones = ctx.enter_context(nc.sbuf_tensor("proj_1", [P, P], F32))
        bank = [ctx.enter_context(nc.psum_tensor(f"proj_p{b}", [P, CH], F32)) for b in range(4)]
        pc = ctx.enter_context(nc.psum_tensor("proj_pc", [P, CH], F32))
        u_in, out = [s.u_in0, s.u_in1], [s.hq_out0, s.hq_out1]
        block = ctx.enter_context(nc.Block())

        @block.sync
        def _(eng):
            for g in range(G):
                eng.dma_start(qc[C * g:C * g + C, 0:1], q_w).then_inc(s.const_in, 16)
            eng.dma_start(qc[:, 1:2], q_b.rearrange("(a o) -> a o", o=1).broadcast_to([P, 1])).then_inc(s.const_in, 16)

            def store(i, par):
                eng.wait_ge(s.hq_ready, 2 * i + 2)
                for j in range(4):
                    for kk in range(2):
                        eng.dma_start(h_img[i, 2 * kk + j // 2].rearrange("(t r a m) -> t a r m", t=2, r=2, a=4)[j % 2],
                                      hb[32 * j:32 * j + 4, par, kk].rearrange("p (r m) -> p r m", r=2))\
                            .then_inc(out[par], 16)

            def body(i, par, r, last):
                at_least(eng, s.hq_done, 2 * (i - 1))
                eng.dma_start(u[:, par], U[i]).then_inc(u_in[par], 16)
                if not (isinstance(i, int) and i < 2):
                    store(i - 2, par)

            walk(eng, n, body)
            store(n - 2, 0)
            store(n - 1, 1)
            eng.wait_ge(s.hq_out0, 64 * n)
            eng.wait_ge(s.hq_out1, 64 * n)

        @block.vector
        def _(dve):
            nc.vector.memset(qbd[:, :], 0.0).then_inc(s.step, 1)
            nc.vector.memset(ones[:, :], 1.0 / G).then_inc(s.step, 1)
            for b in range(4):
                nc.vector.memset(bank[b][:, :], 0.0).then_inc(s.step, 1)
            dve.wait_ge(s.const_in, 16 * (G + 1))
            dve.wait_ge(s.step, 6)
            for g in range(G):
                rows = slice(C * g, C * g + C)
                nc.vector.tensor_tensor(qbd[rows, g:g + 1], qc[rows, 0:1], scale[rows, :], ALU.mult).then_inc(s.step, 1)
            nc.vector.tensor_tensor(qc[:, 2:3], qc[:, 0:1], bias, ALU.mult).then_inc(s.step, 1)
            dve.wait_ge(s.pe_step, 1)
            nc.vector.tensor_tensor(qbias[:, :], pc[:, 0:1], qc[:, 1:2], ALU.add).then_inc(s.step, 1)

        @block.scalar
        def _(act):
            act.wait_ge(s.step, 12)

            def body(i, par, r, last):
                for kk in range(2):
                    act.wait_ge(s.hq_done, 2 * i + kk + 1)
                    if kk == 0 and not (isinstance(i, int) and i < 2):
                        act.wait_ge(out[par], 128 * r)
                    nc.scalar.activation(hb[:, par, kk, :], bank[2 * par + kk][:, :], ACT.Identity,
                                         bias=qbias[:, 0:1]).then_inc(s.hq_ready, 1)

            walk(act, n, body)

        @block.tensor
        def _(pe):
            pe.wait_ge(s.step, 11)
            nc.tensor.matmul(pc[:, 0:1], ones[:, :], qc[:, 2:3], start=True, stop=True).then_inc(s.pe_step, 1)

            def body(i, par, r, last):
                pe.wait_ge(u_in[par], 16 * r + 16)
                for kk in range(2):
                    at_least(pe, s.hq_ready, 2 * i + kk - 3)
                    for j in range(4):
                        k = 4 * kk + j
                        ins = nc.tensor.matmul(bank[2 * par + kk][32 * j:32 * j + G, :], qbd[:, 0:G],
                                               u[:, par, CH * k:CH * k + CH], start=True, stop=True)
                    ins.then_inc(s.hq_done, 1)

            walk(pe, n, body)


def operator(nc, ctx, sems, d, h_img):
    B = d["x"].shape[0]
    n = B // G
    layers = d["w_w"].shape[0]

    def sb(name, shape):
        return ctx.enter_context(nc.sbuf_tensor("k_" + name, shape, F32))

    K = {
        "mixw": sb("mixw", [P, 2, C * MODES, 2]), "mixtmp": sb("mixtmp", [P, 2 * C * MODES // PIECES]),
        "wbd": sb("wbd", [P, P]), "pwbd": sb("pwbd", [16, P]), "lift_mix": sb("lift_mix", [P, P]),
        "lift_px": sb("lift_px", [P, 4 * G]), "w_b": sb("w_b", [P, 1]), "bn_g": sb("bn_g", [P, 1]), "bn_b": sb("bn_b", [P, 1]),
    }
    for name in ("dfty", "dftx", "idftx", "idfty", "eye", "groupmean"):
        K[name] = sb(name, list(d[name].shape))
    K["grid_px"] = d["grid_px"]
    stats = sb("stats", [P, 6 * NCH * n])
    sb_t = sb("scale_bias", [P, 2])
    scale_bias = (sb_t[:, 0:1], sb_t[:, 1:2])
    U = nc.dram_tensor("u_scratch", (n, P, PX), F32).ap()
    xsp = nc.dram_tensor("x_spectrum", (2 * n, P, SPEC), F32).ap()
    isp = nc.dram_tensor("image_spectrum", (2, P, SPEC), F32).ap()
    ysp = nc.dram_tensor("y_spectrum", (2 * n, P, ROW), F32).ap()
    par = {"w_w": d["w_w"], "w_b": d["w_b"], "bn_g": d["bn_g"], "bn_b": d["bn_b"]}
    images = d["x"].rearrange("b x y o -> b x (y o)")

    def load_images(eng, buf, i, sem):
        img = images.rearrange("(n g) (r a b) y -> a n g r (b y)", g=G, r=4, a=4)
        for a in range(4):
            eng.dma_start(buf[C * a:C * a + C].rearrange("p (g r m) -> p g r m", g=G, r=4), img[a]).then_inc(sem, 16)

    load_images.count = 4

    def load_group(eng, buf, i, sem):
        eng.dma_start(buf, U[i]).then_inc(sem, 16)

    load_group.count = 1
    s = sems

    with nc.sbuf_tensor("zero", [P, 8 * ROW], F32) as zero, nc.Block() as block:
        names = ("dfty", "dftx", "idftx", "idfty", "eye", "groupmean")

        @block.vector
        def _(dve):
            for t in ("wbd", "lift_mix", "lift_px"):
                nc.vector.memset(K[t][:, :], 0.0).then_inc(s.step, 1)
            nc.vector.memset(zero[:, :], 0.0).then_inc(s.step, 1)

        @block.sync
        def _(eng):
            for name in names:
                eng.dma_start(K[name][:], d[name]).then_inc(s.const_in, 16)
            eng.wait_ge(s.step, 4)
            zeros = zero[:, :].rearrange("p (x m) -> p x m", m=ROW)
            for t in range(4 * 2 * n // P):
                eng.dma_start(ysp.rearrange("b (r x) m -> (b r) x m", x=32)[P * t:P * t + P, KX:32], zeros).then_inc(s.in_a, 16)
            eng.wait_ge(s.in_a, 16 * (4 * 2 * n // P))
            with nc.allow_non_contiguous_dma("lifting weights, 128 words a piece"):
                for q in range(4):
                    rows, col = slice(C * q, C * q + C), 64 * (q // 2) + 4 * (q % 2)
                    eng.dma_start(K["lift_mix"][rows, col:col + 3], d["p_w"].rearrange("j c -> c j")).then_inc(s.const_in, 16)
                    eng.dma_start(K["lift_mix"][rows, col + 3:col + 4], d["p_b"].rearrange("(c o) -> c o", o=1)).then_inc(s.const_in, 16)
                    eng.dma_start(K["lift_px"][rows, q:3 * G:G], d["p_w"].rearrange("j c -> c j")).then_inc(s.const_in, 16)
                    eng.dma_start(K["lift_px"][rows, 3 * G + q:3 * G + q + 1], d["p_b"].rearrange("(c o) -> c o", o=1)).then_inc(s.const_in, 16)
            eng.wait_ge(s.const_in, 16 * (len(names) + 16))
    end_phase(nc, s)

    fw1, fw2 = d["fw1"], d["fw2"]
    forward_phase(nc, s, "_0", K, load_images, 1, lambda i: isp, None, weight_loader(s, K, fw1, fw2, 0))
    end_phase(nc, s)
    mix_phase(nc, s, "_0", K, B, isp, ysp, par, 0, True, d)
    end_phase(nc, s)
    inverse_phase(nc, s, "_0", K, U, ysp, n, images, None, stats)
    end_phase(nc, s)
    norm_phase(nc, s, "_0", K, n, stats, scale_bias)
    end_phase(nc, s)
    with nc.Fori(1, layers) as layer:
        forward_phase(nc, s, "", K, load_group, n, lambda i: xsp[bass.ds(2 * i, 2)], scale_bias, weight_loader(s, K, fw1, fw2, layer))
        end_phase(nc, s)
        mix_phase(nc, s, "", K, B, xsp, ysp, par, layer, False, d)
        end_phase(nc, s)
        inverse_phase(nc, s, "", K, U, ysp, n, None, scale_bias, stats)
        end_phase(nc, s)
        norm_phase(nc, s, "", K, n, stats, scale_bias)
        end_phase(nc, s)
    project_phase(nc, s, K, U, n, h_img, scale_bias, d["q_w"], d["q_b"])
    end_phase(nc, s)


def token_constants(T, D):
    t = np.arange(T)
    gap = t[None, :] - 1 - t[:, None]
    decay = np.where(gap >= 0, np.float64(DECAY) ** np.maximum(gap, 0), 0.0)
    return {"decay": decay.astype(np.float32)}


class Chain:

    def __init__(self, eng, sem, base=0):
        self.eng, self.sem, self.base, self.n = eng, sem, base, 0

    def then(self, ins):
        self.n += 1
        ins.then_inc(self.sem, 1)
        self.eng.wait_ge(self.sem, self.base + self.n)


def norm_statistics(nc, chain, st, w):
    ve = nc.vector
    me, se, mo, so = (st[:, :, j] for j in (1, 2, 4, 5))
    chain.then(ve.tensor_tensor(w[:, 0], me, mo, ALU.add))
    chain.then(ve.tensor_tensor(w[:, 1], me, mo, ALU.subtract))
    chain.then(ve.tensor_tensor(w[:, 2], se, so, ALU.add))
    chain.then(ve.tensor_scalar(w[:, 0], w[:, 0], 0.5, None, ALU.mult))
    chain.then(ve.scalar_tensor_tensor(out=w[:, 1], in0=w[:, 1], scalar=0.25, in1=w[:, 1], op0=ALU.mult, op1=ALU.mult))
    chain.then(ve.tensor_scalar(w[:, 2], w[:, 2], 1.0 / S, EPS, ALU.mult, ALU.add))
    chain.then(ve.tensor_tensor(w[:, 3], w[:, 1], w[:, 2], ALU.add))


def spread_over(ap, D):
    return ap.rearrange("p (n o) -> p n o", o=1).broadcast_to([ap.shape[0], ap.shape[1], D])


def token_norm_phase(nc, sems, W, h_img, txt, d, le_dram):
    s = sems
    h = W["e"]
    T, B, D = h.shape
    with ExitStack() as ctx:
        le = ctx.enter_context(nc.sbuf_tensor("t_le", [T, B, D], F32))
        st = ctx.enter_context(nc.sbuf_tensor("t_st", [T, B, 6], F32))
        w = ctx.enter_context(nc.sbuf_tensor("t_w", [T, 6, B], F32))
        raw = ctx.enter_context(nc.sbuf_tensor("t_raw", [P, 2, 2, D], F32))
        rawe = ctx.enter_context(nc.sbuf_tensor("t_rawe", [D, 2, P], F32))
        ps = ctx.enter_context(nc.psum_tensor("t_ps", [P, 6, P], F32))
        block = ctx.enter_context(nc.Block())

        @block.sync
        def _(eng):
            eng.dma_start(h[0:S], h_img.rearrange("n g (t d) -> t (n g) d", d=D)).then_inc(s.in_a, 16)
            eng.dma_start(h[S:T], txt.rearrange("b t d -> t b d")).then_inc(s.in_a, 16)
            for j, name in enumerate(("Dx", "Dy")):
                eng.dma_start(raw[:, j], d[name].rearrange("(q p) d -> p q d", p=P)).then_inc(s.w_in, 16)
            eng.dma_start(rawe[:, :, :], d["E"].rearrange("d (q n) -> d q n", q=2)).then_inc(s.w_in, 16)
            eng.dma_start(W["decay"][:, :], d["decay"]).then_inc(s.const_in, 16)
            eng.wait_ge(s.const_in, 16)
            eng.wait_ge(s.aggr, 3)
            eng.dma_start(le_dram, le[:, :, :]).then_inc(s.y_out0, 16)
            eng.wait_ge(s.y_out0, 16)

        @block.tensor
        def _(pe):
            pe.wait_ge(s.w_in, 48)
            for j in range(2):
                for q in range(2):
                    nc.tensor.transpose(ps[0:D, 2 * j + q, :], raw[:, j, q, :], W["eye"][:, :])
            for q in range(2):
                ins = nc.tensor.transpose(ps[:, 4 + q, 0:D], rawe[:, q, :], W["eye"][0:D, 0:D])
            ins.then_inc(s.pe_step, 1)

        @block.scalar
        def _(act):
            act.wait_ge(s.aggr, 1)
            nc.scalar.activation(w[:, 4], w[:, 3], ACT.Sqrt).then_inc(s.act_step, 1)
            act.wait_ge(s.aggr, 2)
            nc.scalar.activation(w[:, 5], w[:, 2], ACT.Sqrt).then_inc(s.act_step, 1)

        @block.vector
        def _(dve):
            ve = nc.vector
            c = Chain(dve, s.step)
            c.then(ve.memset(W["ones"][:, :], 1.0))
            dve.wait_ge(s.pe_step, 1)
            for j, t in enumerate(("DxT", "DyT")):
                c.then(ve.tensor_copy(W[t][:, :], ps[0:D, 2 * j:2 * j + 2, :].rearrange("p q n -> p (q n)")))
            c.then(ve.tensor_copy(W["ET"][:, :, :], ps[:, 4:6, 0:D]))
            dve.wait_ge(s.in_a, 32)
            with dve.Fori(0, B // 8) as m:
                for b in range(8):
                    ve.bn_stats(st[:, bass.ds(8 * m + b, 1), :].rearrange("p o s -> p (o s)"),
                                h[:, bass.ds(8 * m + b, 1), :].rearrange("p o d -> p (o d)")).then_inc(s.st_done, 1)
            dve.wait_ge(s.st_done, B)
            norm_statistics(nc, c, st, w)
            dve.sem_inc(s.aggr, 1)
            dve.wait_ge(s.act_step, 1)
            c.then(ve.reciprocal(w[:, 1], w[:, 4]))
            c.then(ve.tensor_tensor(h[:, :, :], h[:, :, :], spread_over(w[:, 0], D), ALU.subtract))
            c.then(ve.tensor_tensor(h[:, :, :], h[:, :, :], spread_over(w[:, 1], D), ALU.mult))
            c.then(ve.tensor_scalar(w[:, 3], w[:, 3], EPS, None, ALU.subtract))
            c.then(ve.tensor_tensor(w[:, 2], w[:, 1], w[:, 1], ALU.mult))
            c.then(ve.tensor_tensor(w[:, 2], w[:, 2], w[:, 3], ALU.mult))
            c.then(ve.tensor_scalar(w[:, 2], w[:, 2], EPS, None, ALU.add))
            dve.sem_inc(s.aggr, 1)
            dve.wait_ge(s.act_step, 2)
            c.then(ve.reciprocal(w[:, 3], w[:, 5]))
            c.then(ve.tensor_tensor(le[:, :, :], h[:, :, :], spread_over(w[:, 3], D), ALU.mult))
            dve.sem_inc(s.aggr, 1)


def update_phase(nc, sems, W, usum):
    s = sems
    T, B, D = W["e"].shape
    n, CT = B // 4, 4 * T
    with ExitStack() as ctx:
        et = ctx.enter_context(nc.sbuf_tensor("up_et", [D, 2, CT], F32))
        eb = ctx.enter_context(nc.sbuf_tensor("up_eb", [T, 2, 4, D], F32))
        row = ctx.enter_context(nc.sbuf_tensor("up_row", [1, B * T], F32))
        pt = [ctx.enter_context(nc.psum_tensor(f"up_t{b}", [D, CH], F32)) for b in range(2)]
        pu = [ctx.enter_context(nc.psum_tensor(f"up_u{b}", [P, CH], F32)) for b in range(4)]
        pr = [ctx.enter_context(nc.psum_tensor(f"up_r{b}", [1, CH], F32)) for b in range(2)]
        block = ctx.enter_context(nc.Block())

        @block.tensor
        def _(pe):
            def sums(i, par):
                pe.wait_ge(s.u_in0, 2 * i + 2)
                at_least(pe, s.sp_ready, i - 1)
                for q in range(2):
                    ins = nc.tensor.matmul(pr[par][0:1, 0:CT], W["ones"][:, 0:1], W["x"][:, q, bass.ds(CT * i, CT)],
                                           start=(q == 0), stop=(q == 1))
                ins.then_inc(s.fx_done, 1)

            def body(i, par, r, last):
                pe.wait_ge(s.a_ready, i + 1)
                at_least(pe, s.vt_ready, i - 1)
                pe.nop(nofuse=True)
                for b in range(4):
                    ins = nc.tensor.transpose(pt[par][:, T * b:T * b + T], eb[:, par, b, :], W["eye"][0:T, 0:T])
                ins.then_inc(s.tr_done, 1)
                if not (isinstance(i, int) and i == 0):
                    sums(i - 1, 1 - par)
                pe.wait_ge(s.vt_ready, i + 1)
                at_least(pe, s.u_in0, 2 * (i - 1))
                for q in range(2):
                    ins = nc.tensor.matmul(pu[2 * par + q][:, 0:CT], W["DxT"][:, P * q:P * q + P], et[:, par, :],
                                           start=True, stop=True)
                ins.then_inc(s.fy_done, 1)
                if last:
                    sums(i, par)

            walk(pe, n, body)

        @block.gpsimd
        def _(pool):
            def body(i, par, r, last):
                at_least(pool, s.tr_done, i - 1)
                nc.gpsimd.tensor_copy(eb[:, par, :, :], W["e"][:, bass.ds(4 * i, 4), :]).then_inc(s.a_ready, 1)

            walk(pool, n, body)

        @block.scalar
        def _(act):
            def body(i, par, r, last):
                act.wait_ge(s.fy_done, i + 1)
                for q in range(2):
                    nc.scalar.activation(W["x"][:, q, bass.ds(CT * i, CT)], pu[2 * par + q][:, 0:CT], ACT.Relu)\
                        .then_inc(s.u_in0, 1)

            walk(act, n, body)

        @block.vector
        def _(dve):
            def sums_out(i, par):
                dve.wait_ge(s.fx_done, i + 1)
                nc.vector.tensor_copy(row[0:1, bass.ds(CT * i, CT)], pr[par][0:1, 0:CT]).then_inc(s.sp_ready, 1)

            def body(i, par, r, last):
                dve.wait_ge(s.tr_done, i + 1)
                at_least(dve, s.fy_done, i - 1)
                nc.vector.tensor_copy(et[:, par, :], pt[par][:, 0:CT]).then_inc(s.vt_ready, 1)
                if not (isinstance(i, int) and i == 0):
                    sums_out(i - 1, 1 - par)
                if last:
                    sums_out(i, par)

            walk(dve, n, body)

        @block.sync
        def _(eng):
            eng.wait_ge(s.sp_ready, n)
            eng.dma_start(usum.rearrange("(o b) t -> o (b t)", o=1), row[:, :]).then_inc(s.y_out0, 16)
            eng.wait_ge(s.y_out0, 16)


def decay_phase(nc, sems, usum, coef):
    s = sems
    B, T = usum.shape
    with ExitStack() as ctx:
        us = ctx.enter_context(nc.sbuf_tensor("d_us", [B, T], F32))
        sg = ctx.enter_context(nc.sbuf_tensor("d_sg", [B, T], F32))
        sm = ctx.enter_context(nc.sbuf_tensor("d_sm", [B, T], F32))
        cf = ctx.enter_context(nc.sbuf_tensor("d_cf", [B, 2, T], F32))
        block = ctx.enter_context(nc.Block())

        @block.sync
        def _(eng):
            eng.dma_start(us[:, :], usum).then_inc(s.in_a, 16)
            eng.wait_ge(s.aggr, 1)
            eng.dma_start(coef.rearrange("q b t -> b q t"), cf[:, :, :]).then_inc(s.y_out0, 16)
            eng.wait_ge(s.y_out0, 16)

        @block.vector
        def _(dve):
            ve = nc.vector
            c = Chain(dve, s.step)
            dve.wait_ge(s.in_a, 16)
            c.then(ve.tensor_tensor_scan(sg[:, :], us[:, :], us[:, :], 0.0, ALU.max, ALU.max))
            c.then(ve.tensor_scalar(sg[:, :], sg[:, :], 0.0, None, ALU.is_gt))
            c.then(ve.tensor_copy(sm[:, 0:1], us[:, 0:1]))
            for sweep in range(5):
                c.then(ve.scalar_tensor_tensor(out=sm[:, 1:T], in0=sg[:, 0:T - 1], scalar=DECAY, in1=us[:, 1:T],
                                               op0=ALU.mult, op1=ALU.add))
                c.then(ve.tensor_scalar(sg[:, :], sm[:, :], 1e12, 1.0, ALU.mult, ALU.min))
            c.then(ve.scalar_tensor_tensor(out=sm[:, 1:T], in0=sg[:, 0:T - 1], scalar=DECAY, in1=us[:, 1:T],
                                           op0=ALU.mult, op1=ALU.add))
            c.then(ve.tensor_scalar(sm[:, :], sm[:, :], 1e-12, None, ALU.max))
            c.then(ve.reciprocal(cf[:, 0, :], sm[:, :]))
            c.then(ve.tensor_scalar(cf[:, 1, :], cf[:, 0, :], DECAY, None, ALU.mult))
            c.then(ve.memset(cf[:, 1, 0:1], 0.0))
            dve.sem_inc(s.aggr, 1)


def attention_phase(nc, sems, W, h_img, txt, coef, le_dram, e2t_dram):
    s = sems
    T, B, D = W["e"].shape
    NB = 8
    n, HT, CT = B // NB, 4 * T, NB * T
    with ExitStack() as ctx:
        def sb(name, shape):
            return ctx.enter_context(nc.sbuf_tensor("at_" + name, shape, F32))

        cf = sb("cf", [P, 2, 2, CT])
        x = sb("x", [P, 2, 2, CT])
        hb = sb("h", [T, 2, NB, D])
        sc = sb("sc", [T, CT])
        la = sb("la", [T, NB, D])
        lat = sb("lat", [D, CT])
        y = sb("y", [P, 2, CT])
        e2 = sb("e2", [T, NB, D])
        e2t = sb("e2t", [D, 2, CT])
        le = sb("le", [T, 2, NB, D])
        st = sb("st", [T, NB, 6])
        w = sb("w", [T, 6, NB])
        ps_s = [ctx.enter_context(nc.psum_tensor(f"at_ps{b}", [T, CH], F32)) for b in range(2)]
        ps_a = ctx.enter_context(nc.psum_tensor("at_pa", [T, CH], F32))
        ps_t = [ctx.enter_context(nc.psum_tensor(f"at_pt{b}", [D, CH], F32)) for b in range(2)]
        ps_y = [ctx.enter_context(nc.psum_tensor(f"at_py{b}", [P, CH], F32)) for b in range(2)]
        ps_v = ctx.enter_context(nc.psum_tensor("at_pv", [T, CH], F32))
        cf_in, h_in, le_in, e_out = [s.u_in0, s.u_in1], [s.y_in0, s.y_in1], [s.sp_out0, s.sp_out1], [s.u_out0, s.u_out1]
        block = ctx.enter_context(nc.Block())

        @block.sync
        def _(eng):
            def store(i, par):
                eng.wait_ge(s.t_ready, 2 * i + 2)
                eng.dma_start(e2t_dram[:, bass.ds(CT * i, CT)], e2t[:, par, :]).then_inc(e_out[par], 16)

            def body(i, par, r, last):
                at_least(eng, s.bn_done, 2 * (i - 1))
                for q in range(2):
                    eng.dma_start(cf[:, par, q, :], coef[q].rearrange("(n o b) t -> n o (b t)", o=1, b=NB)[i]
                                  .broadcast_to([P, CT])).then_inc(cf_in[par], 16)
                at_least(eng, s.fx_done, i - 1)
                eng.dma_start(le[:, par], le_dram[:, bass.ds(NB * i, NB), :]).then_inc(le_in[par], 16)
                at_least(eng, s.uo_ready, i - 1)
                hv = h_img.rearrange("(n a) g (t d) -> n t (a g) d", a=NB // G, d=D)
                eng.dma_start(hb[0:S, par], hv[i]).then_inc(h_in[par], 16)
                eng.dma_start(hb[S:T, par], txt.rearrange("(n b) t d -> n t b d", b=NB)[i]).then_inc(h_in[par], 16)
                if not (isinstance(i, int) and i < 2):
                    store(i - 2, par)

            walk(eng, n, body)
            store(n - 2, 0)
            store(n - 1, 1)
            eng.wait_ge(s.u_out0, 8 * n)
            eng.wait_ge(s.u_out1, 8 * n)

        @block.gpsimd
        def _(pool):
            def body(i, par, r, last):
                pool.wait_ge(cf_in[par], 32 * r + 32)
                for q in range(2):
                    xq = W["x"][:, q, bass.ds(CT * i, CT)]
                    nc.gpsimd.tensor_tensor(xq, xq, cf[:, par, 0, :], ALU.mult).then_inc(s.a_ready, 1)

            walk(pool, n, body)

        @block.scalar
        def _(act):
            def body(i, par, r, last):
                act.wait_ge(s.aggr, 3 * i + 1)
                nc.scalar.activation(w[:, 4], w[:, 3], ACT.Sqrt).then_inc(s.act_step, 1)
                for q in range(2):
                    act.wait_ge(s.t2_done, 2 * i + q + 1)
                    nc.scalar.copy(lat[:, HT * q:HT * q + HT], ps_t[q][:, 0:HT]).then_inc(s.a2_ready, 1)
                for k in range(2):
                    act.wait_ge(s.aggr, 3 * i + 2 + k)
                    nc.scalar.activation(w[:, 4], w[:, 3], ACT.Sqrt).then_inc(s.act_step, 1)
                if not (isinstance(i, int) and i < 2):
                    act.wait_ge(e_out[par], 16 * r)
                for q in range(2):
                    act.wait_ge(s.tt_done, 2 * i + q + 1)
                    nc.scalar.copy(e2t[:, par, HT * q:HT * q + HT], ps_t[q][:, 0:HT]).then_inc(s.t_ready, 1)
                act.wait_ge(s.um_done, i + 1)
                nc.scalar.copy(W["gate"][:, bass.ds(NB * i, NB), :],
                               ps_a[:, 0:8 * NB].rearrange("p (b e) -> p b e", b=NB)).then_inc(s.sp_ready, 1)

            walk(act, n, body)

        CHAIN = 2 + 10 + 4 + 10 + 1 + 10 + 1

        @block.vector
        def _(dve):
            ve = nc.vector

            def norm(c, src, out, i, k):
                for b in range(NB):
                    ve.bn_stats(st[:, b, :], src[:, b, :]).then_inc(s.st_done, 1)
                dve.wait_ge(s.st_done, NB * (3 * i + k + 1))
                norm_statistics(nc, c, st, w)
                dve.sem_inc(s.aggr, 1)
                dve.wait_ge(s.act_step, 3 * i + k + 1)
                c.then(ve.reciprocal(w[:, 5], w[:, 4]))
                c.then(ve.tensor_tensor(out[:, :, :], src, spread_over(w[:, 0], D), ALU.subtract))
                c.then(ve.tensor_tensor(out[:, :, :], out[:, :, :], spread_over(w[:, 5], D), ALU.mult))

            def body(i, par, r, last):
                c = Chain(dve, s.step, CHAIN * i)
                for q in range(2):
                    dve.wait_ge(s.a_ready, 2 * i + q + 1)
                    at_least(dve, s.ix_done, i - 1)
                    ve.tensor_tensor_scan(x[:, par, q, :], cf[:, par, 1, :], W["x"][:, q, bass.ds(CT * i, CT)], 0.0,
                                          ALU.mult, ALU.add).then_inc(s.bn_done, 1)
                decay = W["decay"][:, :].rearrange("s (o t) -> s o t", o=1).broadcast_to([T, 4, T])
                for q in range(2):
                    dve.wait_ge(s.fy_done, 2 * i + q + 1)
                    c.then(ve.tensor_tensor(sc[:, HT * q:HT * q + HT].rearrange("s (b t) -> s b t", b=4),
                                            ps_s[q][:, 0:HT].rearrange("s (b t) -> s b t", b=4), decay, ALU.mult))
                dve.wait_ge(s.fx_done, i + 1)
                norm(c, ps_a[:, :].rearrange("t (b d) -> t b d", b=NB), la, i, 0)
                dve.sem_inc(s.pw_ready, 1)
                for q in range(2):
                    for hh in range(2):
                        dve.wait_ge(s.mix_done, 4 * i + 2 * q + hh + 1)
                        c.then(ve.scalar_tensor_tensor(out=y[:, q, HT * hh:HT * hh + HT], in0=ps_y[hh][:, 0:HT], scalar=0.0,
                                                       in1=x[:, par, q, HT * hh:HT * hh + HT], op0=ALU.max, op1=ALU.mult))
                        dve.sem_inc(s.mix_low, 1)
                dve.wait_ge(s.ix_done, i + 1)
                norm(c, ps_v[:, :].rearrange("t (b d) -> t b d", b=NB), e2, i, 1)
                dve.wait_ge(h_in[par], 32 * r + 32)
                c.then(ve.tensor_tensor(hb[:, par], hb[:, par], e2[:, :, :], ALU.add))
                norm(c, hb[:, par], e2, i, 2)
                c.then(ve.tensor_copy(W["h2"][:, bass.ds(NB * i, NB), :], hb[:, par]))
                dve.sem_inc(s.uo_ready, 1)
                assert c.n == CHAIN

            walk(dve, n, body)

        @block.tensor
        def _(pe):
            def body(i, par, r, last):
                pe.wait_ge(s.bn_done, 2 * i + 2)
                for q in range(2):
                    for b in range(4):
                        t = HT * q + T * b
                        for half in range(2):
                            xb = x[:, par, half, t:t + T]
                            ins = nc.tensor.matmul(ps_s[q][:, T * b:T * b + T], xb, xb, start=(half == 0), stop=(half == 1))
                    ins.then_inc(s.fy_done, 1)
                pe.wait_ge(s.step, CHAIN * i + 2)
                pe.wait_ge(le_in[par], 16 * r + 16)
                at_least(pe, s.sp_ready, i)
                for b in range(NB):
                    ins = nc.tensor.matmul(ps_a[:, D * b:D * b + D], sc[:, T * b:T * b + T],
                                           le[:, par, b, :], start=True, stop=True)
                ins.then_inc(s.fx_done, 1)
                pe.wait_ge(s.pw_ready, i + 1)
                pe.nop(nofuse=True)
                for q in range(2):
                    for b in range(4):
                        ins = nc.tensor.transpose(ps_t[q][:, T * b:T * b + T], la[:, 4 * q + b, :], W["eye"][0:T, 0:T])
                    ins.then_inc(s.t2_done, 1)
                for q in range(2):
                    for hh in range(2):
                        if q == 0:
                            pe.wait_ge(s.a2_ready, 2 * i + hh + 1)
                            at_least(pe, s.mix_low, 4 * i + hh - 1)
                        else:
                            pe.wait_ge(s.mix_low, 4 * i + hh + 1)
                        nc.tensor.matmul(ps_y[hh][:, 0:HT], W["DyT"][:, P * q:P * q + P], lat[:, HT * hh:HT * hh + HT],
                                         start=True, stop=True).then_inc(s.mix_done, 1)
                pe.wait_ge(s.mix_low, 4 * i + 4)
                for b in range(NB):
                    for q in range(2):
                        ins = nc.tensor.matmul(ps_v[:, D * b:D * b + D], y[:, q, T * b:T * b + T], W["ET"][:, q, :],
                                               start=(q == 0), stop=(q == 1))
                ins.then_inc(s.ix_done, 1)
                pe.wait_ge(s.uo_ready, i + 1)
                pe.nop(nofuse=True)
                for q in range(2):
                    for b in range(4):
                        ins = nc.tensor.transpose(ps_t[q][:, T * b:T * b + T], e2[:, 4 * q + b, :], W["eye"][0:T, 0:T])
                    ins.then_inc(s.tt_done, 1)
                pe.wait_ge(s.t_ready, 2 * i + 2)
                for b in range(NB):
                    ins = nc.tensor.matmul(ps_a[:, 8 * b:8 * b + 8], e2t[:, par, T * b:T * b + T], W["Wr"][:, :],
                                           start=True, stop=True)
                ins.then_inc(s.um_done, 1)

            walk(pe, n, body)


def gate_phase(nc, sems, W, d):
    s = sems
    T, B, D = W["e"].shape
    E = 8
    with ExitStack() as ctx:
        def sb(name, shape):
            return ctx.enter_context(nc.sbuf_tensor("g_" + name, shape, F32))

        p, q, first, tmp = (sb(x, [T, B, E]) for x in ("p", "q", "first", "tmp"))
        m = sb("m", [T, 4, B])
        b2 = sb("b2", [P, 16, D])
        b2s = sb("b2s", [T, D])
        mt = sb("mt", [P, 2, T])
        rank = sb("rank", [T, E])
        pt = [ctx.enter_context(nc.psum_tensor(f"g_pt{b}", [P, CH], F32)) for b in range(2)]
        pb = [ctx.enter_context(nc.psum_tensor(f"g_pb{b}", [T, CH], F32)) for b in range(4)]
        gate = W["gate"]
        block = ctx.enter_context(nc.Block())

        def per_token(j):
            return m[:, j, :].rearrange("p (n o) -> p n o", o=1).broadcast_to([T, B, E])

        @block.sync
        def _(eng):
            eng.dma_start(b2s[:, :], d["b2s"].rearrange("(o d) -> o d", o=1).broadcast_to([T, D])).then_inc(s.in_a, 16)
            eng.wait_ge(s.w_fix, 1)
            for b in range(16):
                eng.dma_start(b2[E * b:E * b + E, b, :], d["b2p"]).then_inc(s.w_in, 16)

        @block.gpsimd
        def _(pool):
            nc.gpsimd.memset(b2[:, :, :], 0.0).then_inc(s.w_fix, 1)

        @block.scalar
        def _(act):
            act.wait_ge(s.aggr, 1)
            nc.scalar.activation(p[:, :, :], q[:, :, :], ACT.Exp).then_inc(s.act_step, 1)

        @block.tensor
        def _(pe):
            pe.wait_ge(s.w_in, 256)
            pe.wait_ge(s.aggr, 2)
            for t in range(B // 16):
                at_least(pe, s.vt_ready, t - 1)
                nc.tensor.transpose(pt[t % 2][:, 0:T], gate[:, 16 * t:16 * t + 16, :].rearrange("p b e -> p (b e)"),
                                    W["eye"][0:T, 0:T]).then_inc(s.tr_done, 1)
                pe.wait_ge(s.vt_ready, t + 1)
                at_least(pe, s.st_done, 2 * t - 2)
                for hh in range(2):
                    ins = nc.tensor.matmul(pb[2 * (t % 2) + hh][:, :], mt[:, t % 2, :],
                                           b2[:, 8 * hh:8 * hh + 8, :].rearrange("p b d -> p (b d)"), start=True, stop=True)
                ins.then_inc(s.fx_done, 1)

        @block.vector
        def _(dve):
            ve = nc.vector
            c = Chain(dve, s.step)
            for e in range(E):
                c.then(ve.memset(rank[:, e:e + 1], float(E - e)))
            ranks = rank[:, :].rearrange("p (o e) -> p o e", o=1).broadcast_to([T, B, E])
            c.then(ve.tensor_reduce(m[:, 0, :], gate[:, :, :], AX.X, ALU.max))
            c.then(ve.tensor_tensor(q[:, :, :], gate[:, :, :], per_token(0), ALU.subtract))
            dve.sem_inc(s.aggr, 1)
            dve.wait_ge(s.act_step, 1)
            c.then(ve.tensor_reduce(m[:, 0, :], p[:, :, :], AX.X, ALU.add))
            c.then(ve.reciprocal(m[:, 1, :], m[:, 0, :]))
            c.then(ve.tensor_tensor(p[:, :, :], p[:, :, :], per_token(1), ALU.mult))
            for k in range(2):
                c.then(ve.tensor_reduce(m[:, 2 + k, :], p[:, :, :], AX.X, ALU.max))
                c.then(ve.tensor_tensor(q[:, :, :], p[:, :, :], per_token(2 + k), ALU.is_equal))
                c.then(ve.tensor_tensor(q[:, :, :], q[:, :, :], ranks, ALU.mult))
                c.then(ve.tensor_reduce(m[:, 0, :], q[:, :, :], AX.X, ALU.max))
                c.then(ve.tensor_tensor(q[:, :, :], ranks, per_token(0), ALU.is_equal))
                c.then(ve.tensor_tensor(tmp[:, :, :], q[:, :, :], per_token(2 + k), ALU.mult))
                if k == 0:
                    c.then(ve.tensor_copy(first[:, :, :], tmp[:, :, :]))
                    c.then(ve.scalar_tensor_tensor(out=p[:, :, :], in0=q[:, :, :], scalar=-2.0, in1=p[:, :, :],
                                                   op0=ALU.mult, op1=ALU.add))
            c.then(ve.tensor_tensor(tmp[:, :, :], tmp[:, :, :], first[:, :, :], ALU.add))
            c.then(ve.tensor_tensor(m[:, 0, :], m[:, 2, :], m[:, 3, :], ALU.add))
            c.then(ve.reciprocal(m[:, 1, :], m[:, 0, :]))
            c.then(ve.tensor_tensor(gate[:, :, :], tmp[:, :, :], per_token(1), ALU.mult))
            dve.sem_inc(s.aggr, 1)
            dve.wait_ge(s.in_a, 16)
            h2 = W["h2"]
            c.then(ve.tensor_tensor(h2[:, :, :], h2[:, :, :],
                                    b2s[:, :].rearrange("p (o d) -> p o d", o=1).broadcast_to([T, B, D]), ALU.add))
            for t in range(B // 16):
                dve.wait_ge(s.tr_done, t + 1)
                at_least(dve, s.fx_done, t - 1)
                ve.tensor_copy(mt[:, t % 2, :], pt[t % 2][:, 0:T]).then_inc(s.vt_ready, 1)
                dve.wait_ge(s.fx_done, t + 1)
                for hh in range(2):
                    rows = h2[:, 16 * t + 8 * hh:16 * t + 8 * hh + 8, :]
                    ve.tensor_tensor(rows, rows, pb[2 * (t % 2) + hh][:, :].rearrange("p (b d) -> p b d", b=8), ALU.add)\
                        .then_inc(s.st_done, 1)


def expert_phase(nc, sems, W, d, out, e2t_dram):
    s = sems
    T, B, D = W["e"].shape
    E, NB = 8, 4
    n, CT = B // NB, NB * T
    F = 2 * P
    TILES = 2 * (E + 1)
    SPLITS = 6
    with ExitStack() as ctx:
        def sb(name, shape, dt=F32):
            return ctx.enter_context(nc.sbuf_tensor("x_" + name, shape, dt))

        w1 = sb("w1", [P, E + 1, F])
        w11, w22, w31 = (sb(x, [P, E + 1, F], BF16) for x in ("w11", "w22", "w31"))
        w2 = sb("w2", [P, E + 1, 2, D])
        b1 = sb("b1", [P, E + 1, 2])
        et = sb("et", [P, 2, CT])
        x12, x13 = (sb(x, [P, 2, CT], BF16) for x in ("x12", "x13"))
        ht = sb("ht", [P, 4, CT])
        prod = sb("prod", [T, NB, E, D])
        part = sb("part", [T, NB, D])
        res = sb("res", [T, 2, NB, D])
        ps_h = [ctx.enter_context(nc.psum_tensor(f"x_ph{b}", [P, CH], F32)) for b in range(3)]
        ps_e = [ctx.enter_context(nc.psum_tensor(f"x_pe{b}", [T, CH], F32)) for b in range(4)]
        ps_s = ctx.enter_context(nc.psum_tensor("x_ps", [T, CH], F32))
        o_out, e_in = [s.u_out0, s.u_out1], [s.u_in0, s.u_in1]
        block = ctx.enter_context(nc.Block())

        @block.sync
        def _(eng):
            for half in range(2):
                rows = slice(D * half, D * half + D)
                eng.dma_start(w1[rows, 0, :], d["W1s"]).then_inc(s.w_in, 16)
                eng.dma_start(w1[rows, 1:, :], d["W1p"].rearrange("e d f -> d e f")).then_inc(s.w_in, 16)
            ov = out.rearrange("(n b) t d -> n t b d", b=NB)

            def store(i, par):
                eng.wait_ge(s.uo_ready, i + 1)
                eng.dma_start(ov[i], res[:, par]).then_inc(o_out[par], 16)

            def body(i, par, r, last):
                at_least(eng, s.bn_done, SPLITS * (i - 1))
                for half in range(2):
                    eng.dma_start(et[D * half:D * half + D, par, :], e2t_dram[:, bass.ds(CT * i, CT)])\
                        .then_inc(e_in[par], 16)
                if not (isinstance(i, int) and i < 2):
                    store(i - 2, par)

            walk(eng, n, body)
            store(n - 2, 0)
            store(n - 1, 1)
            eng.wait_ge(s.u_out0, 8 * n)
            eng.wait_ge(s.u_out1, 8 * n)

        @block.gpsimd
        def _(pool):
            def body(i, par, r, last):
                pool.wait_ge(e_in[par], 32 * r + 32)
                at_least(pool, s.fy_done, TILES * (i - 1))
                x, a12, a13, gp = et[:, par, :], x12[:, par, :], x13[:, par, :], nc.gpsimd
                c = Chain(pool, s.bn_done, SPLITS * i)
                pool.nop(nofuse=True)
                c.then(gp.tensor_copy(a12, x))
                pool.nop(nofuse=True)
                c.then(gp.tensor_copy(a13[0:D], a12[0:D]))
                c.then(gp.tensor_tensor(x[D:P], x[D:P], a12[D:P], ALU.subtract))
                pool.nop(nofuse=True)
                c.then(gp.tensor_copy(a12[D:P], x[D:P]))
                c.then(gp.tensor_tensor(x[D:P], x[D:P], a12[D:P], ALU.subtract))
                pool.nop(nofuse=True)
                c.then(gp.tensor_copy(a13[D:P], x[D:P]))
                assert c.n == SPLITS

            walk(pool, n, body)

        @block.scalar
        def _(act):
            act.dma_start(w2[:, 0], d["W2s"].rearrange("(t p) d -> p t d", p=P)).then_inc(s.w_tmp, 16)
            for e in range(E):
                act.dma_start(w2[:, 1 + e], d["W2p"][e].rearrange("(t p) d -> p t d", p=P)).then_inc(s.w_tmp, 16)
            with nc.allow_non_contiguous_dma("biases to partitions"):
                act.dma_start(b1[:, 0, :], d["b1s"].rearrange("(t p) -> p t", p=P)).then_inc(s.w_tmp, 16)
                act.dma_start(b1[:, 1:, :].rearrange("p e t -> p (e t)"),
                              d["b1p"].rearrange("e (t p) -> p (e t)", p=P)).then_inc(s.w_tmp, 16)
            act.wait_ge(s.w_tmp, 16 * 11)

            def body(i, par, r, last):
                for j in range(TILES):
                    t = TILES * i + j
                    act.wait_ge(s.fy_done, t + 1)
                    if not (isinstance(i, int) and i == 0 and j < 4):
                        act.wait_ge(s.fx_done, t - 3)
                    nc.scalar.activation(ht[:, (TILES * par + j) % 4, :], ps_h[j % 3][:, 0:CT], ACT.Gelu,
                                         bias=b1[:, j // 2, j % 2:j % 2 + 1]).then_inc(s.a_ready, 1)

            walk(act, n, body)

        @block.vector
        def _(dve):
            ve = nc.vector
            dve.wait_ge(s.w_in, 64)
            for e in range(E + 1):
                wx, b1x, b2x, b3x = w1[:, e, :], w11[:, e, :], w22[:, e, :], w31[:, e, :]
                c = Chain(dve, s.step, 6 * e)
                c.then(ve.tensor_copy(b1x, wx))
                c.then(ve.tensor_tensor(wx, wx, b1x, ALU.subtract))
                c.then(ve.tensor_copy(b2x, wx))
                c.then(ve.tensor_tensor(wx[0:D], wx[0:D], b2x[0:D], ALU.subtract))
                c.then(ve.tensor_copy(b3x[0:D], wx[0:D]))
                c.then(ve.tensor_copy(b3x[D:P], b1x[D:P]))

            def body(i, par, r, last):
                if not (isinstance(i, int) and i < 2):
                    dve.wait_ge(o_out[par], 16 * r)
                dve.wait_ge(s.fx_done, TILES * i + 2)
                ve.tensor_tensor(res[:, par], W["h2"][:, bass.ds(NB * i, NB), :],
                                 ps_s[:, 0:NB * D].rearrange("p (b d) -> p b d", b=NB), ALU.add).then_inc(s.s_ready, 1)
                dve.wait_ge(s.fx_done, TILES * i + TILES)
                for b in range(NB):
                    g = W["gate"][:, bass.ds(NB * i + b, 1), :].rearrange("p o e -> p (o e)")
                    ve.tensor_tensor(prod[:, b], ps_e[b][:, :].rearrange("p (e d) -> p e d", e=E),
                                     spread_over(g, D), ALU.mult).then_inc(s.t_ready, 1)
                for b in range(NB):
                    dve.wait_ge(s.t_ready, NB * i + b + 1)
                    ve.tensor_reduce(part[:, b, :], prod[:, b].rearrange("p e d -> p d e"), AX.X, ALU.add)\
                        .then_inc(s.st_done, 1)
                dve.wait_ge(s.st_done, NB * i + NB)
                dve.wait_ge(s.s_ready, i + 1)
                ve.tensor_tensor(res[:, par], res[:, par], part[:, :, :], ALU.add).then_inc(s.uo_ready, 1)
                dve.wait_ge(s.uo_ready, i + 1)

            walk(dve, n, body)

        @block.tensor
        def _(pe):
            def hidden(i, par, r, j):
                t, e = TILES * i + j, j // 2
                first = isinstance(i, int) and i == 0
                if j == 0:
                    pe.wait_ge(s.bn_done, SPLITS * (i + 1))
                if first and j % 2 == 0:
                    pe.wait_ge(s.step, 6 * (e + 1))
                if not (first and j < 3):
                    pe.wait_ge(s.a_ready, t - 2)
                cols = slice(P * (j % 2), P * (j % 2) + P)
                o = ps_h[j % 3][:, 0:CT]
                nc.tensor.matmul(o, w31[:, e, cols], x13[:, par, :], start=True, stop=False)
                nc.tensor.matmul(o, w22[:, e, cols], x12[:, par, :], start=False, stop=False)
                nc.tensor.matmul(o, w11[:, e, cols], x12[:, par, :], start=False, stop=True).then_inc(s.fy_done, 1)

            def outputs(i, par, j):
                pe.wait_ge(s.a_ready, TILES * i + j + 1)
                e, half = j // 2, j % 2
                if j == 0:
                    at_least(pe, s.s_ready, i)
                for b in range(NB):
                    if j == 2:
                        at_least(pe, s.t_ready, NB * (i - 1) + b + 1)
                    if e == 0:
                        o, start = ps_s[:, D * b:D * b + D], half == 0 and b == 0
                    else:
                        o, start = ps_e[b][:, D * (e - 1):D * e], half == 0
                    ins = nc.tensor.matmul(o, ht[:, (TILES * par + j) % 4, T * b:T * b + T], w2[:, e, half, :],
                                           start=start, stop=(half == 1), skip_group_check=True)
                ins.then_inc(s.fx_done, 1)

            def body(i, par, r, last):
                for j in range(TILES):
                    hidden(i, par, r, j)
                    if j >= 2:
                        outputs(i, par, j - 2)
                    elif not (isinstance(i, int) and i == 0):
                        outputs(i - 1, 1 - par, TILES + j - 2)
                if last:
                    outputs(i, par, TILES - 2)
                    outputs(i, par, TILES - 1)

            pe.wait_ge(s.w_tmp, 16 * 11)
            walk(pe, n, body)


def tokens(nc, ctx, sems, d, h_img, out):
    B, L, D = d["txt"].shape
    T = S + L

    def sb(name, shape, c=ctx):
        return c.enter_context(nc.sbuf_tensor("w_" + name, shape, F32))

    usum = nc.dram_tensor("update_sums", (B, T), F32).ap()
    coef = nc.dram_tensor("state_coefficients", (2, B, T), F32).ap()
    le_dram = nc.dram_tensor("normed_rows", (T, B, D), F32).ap()
    e2t_dram = nc.dram_tensor("expert_inputs", (D, B * T), F32).ap()
    W = {"gate": sb("gate", [T, B, 8]), "Wr": sb("Wr", [D, 8]), "eye": sb("eye", [P, P]), "h2": sb("h2", [T, B, D])}
    W["e"] = W["h2"]
    with nc.Block() as block:
        @block.sync
        def _(eng):
            eng.dma_start(W["Wr"][:, :], d["Wr"]).then_inc(sems.const_in, 16)
            eng.dma_start(W["eye"][:, :], d["eye"]).then_inc(sems.const_in, 16)
            eng.wait_ge(sems.const_in, 32)
    end_phase(nc, sems)
    with ExitStack() as c:
        for name, shape in (("DxT", [D, 2 * P]), ("DyT", [D, 2 * P]), ("ET", [P, 2, D]), ("decay", [T, T]), ("ones", [P, 1])):
            W[name] = sb(name, shape, c)
        token_norm_phase(nc, sems, W, h_img, d["txt"], d, le_dram)
        end_phase(nc, sems)
        W["x"] = sb("x", [P, 2, B * T], c)
        update_phase(nc, sems, W, usum)
        end_phase(nc, sems)
        decay_phase(nc, sems, usum, coef)
        end_phase(nc, sems)
        attention_phase(nc, sems, W, h_img, d["txt"], coef, le_dram, e2t_dram)
        end_phase(nc, sems)
    gate_phase(nc, sems, W, d)
    end_phase(nc, sems)
    expert_phase(nc, sems, W, d, out, e2t_dram)
    end_phase(nc, sems)

def program(nc, d, out):
    B = d["x"].shape[0]
    h_img = nc.dram_tensor("image_rows", (B // G, G, PX), F32).ap()
    with ExitStack() as ctx:
        sems = Semaphores(ctx, nc)
        with ExitStack() as c:
            operator(nc, c, sems, d, h_img)
        tokens(nc, ctx, sems, d, h_img, out)


INPUTS = ("x", "txt", "L0_tok_p_w", "L0_tok_p_b", "L0_tok_fw1", "L0_tok_fw2", "L0_tok_w_w", "L0_tok_w_b", "L0_tok_bn_g",
          "L0_tok_bn_b", "L0_tok_q_w", "L0_tok_q_b", "L0_attn_E", "L0_attn_Dx", "L0_attn_Dy", "L0_ffn_Wr", "L0_ffn_W1s",
          "L0_ffn_b1s", "L0_ffn_W2s", "L0_ffn_b2s", "L0_ffn_W1p", "L0_ffn_b1p", "L0_ffn_W2p", "L0_ffn_b2p")


def kernel(**inputs):
    from concourse import bacc
    from concourse.bass_utils import run_bass_kernel_spmd

    nc = bacc.Bacc("TRN2", target_bir_lowering=False, num_devices=1)
    arrays, d = {}, {}
    named = [(n, n.split("_", 2)[2] if n.startswith("L0_") else n, inputs[n]) for n in INPUTS]
    B, L, D = inputs["txt"].shape
    consts = {**shape_constants(), **token_constants(S + L, D)}
    named += [("const_" + n, n, a) for n, a in consts.items()]
    for full, short, a in named:
        a = np.ascontiguousarray(a)
        arrays[f"in_{full}_dram"] = a
        d[short] = nc.dram_tensor(f"in_{full}_dram", a.shape, mybir.dt.from_np(a.dtype), kind="ExternalInput").ap()
    out = nc.dram_tensor("out_0_dram", (B, S + L, D), F32, kind="ExternalOutput").ap()
    program(nc, d, out)
    r = run_bass_kernel_spmd(nc, [arrays], core_ids=[0])
    return r.results[0]["out_0_dram"]
```

```python
from contextlib import ExitStack

import numpy as np

import concourse.bass as bass
from concourse import mybir

F32 = mybir.dt.float32
BF16 = mybir.dt.bfloat16
ALU = mybir.AluOpType
ACT = mybir.ActivationFunctionType
AX = mybir.AxisListType

P = 128
S = 64
C = 32
G = P // C
PX = S * S
M1 = M2 = 12
KX = 2 * M1
MODES = M1 * M2
SPEC = KX * M2
ROW = M2 * C
CH = 512
NCH = PX // CH
EPS = 1e-5
DECAY = 0.97


def shape_constants():
    f = np.float64
    ang = 2 * np.pi / S
    y = np.arange(S, dtype=f)
    ky = np.arange(M2, dtype=f)
    kx = np.concatenate([np.arange(M1), np.arange(S - M1, S)]).astype(f)
    eye4 = np.eye(4)
    row = np.zeros((S, 32))
    row[:, 0:2 * M2:2] = np.cos(ang * np.outer(y, ky))
    row[:, 1:2 * M2:2] = -np.sin(ang * np.outer(y, ky))
    dfty = np.stack([np.kron(eye4, row[32 * t:32 * t + 32]) for t in range(2)], 1)
    wt = np.where(ky == 0, 1.0, 2.0)[:, None] / S
    inv = np.zeros((32, S))
    inv[0:2 * M2:2] = wt * np.cos(ang * np.outer(ky, y))
    inv[3:2 * M2:2] = (-wt * np.sin(ang * np.outer(ky, y)))[1:]
    idfty = np.kron(eye4, inv)
    r, a_, b_ = (t.reshape(-1) for t in np.meshgrid(range(4), range(4), range(4), indexing="ij"))
    x = 16 * r + 4 * a_ + b_
    c, sn = np.cos(ang * np.outer(x, kx)), np.sin(ang * np.outer(x, kx))
    dftx = np.zeros((P, 2, 2, 2, 32))
    idftx = np.zeros((2, 2, 32, 2, P))
    for h in range(2):
        p = 32 * a_ + 16 * h + 4 * r + b_
        dftx[p, 0, 0, h, :KX], dftx[p, 1, 0, h, :KX] = c, sn
        dftx[p, 0, 1, h, :KX], dftx[p, 1, 1, h, :KX] = -sn, c
        p = 32 * b_ + 16 * h + 4 * a_ + r
        for k in range(KX):
            idftx[0, h, k, 0, p], idftx[1, h, k, 0, p] = c[:, k] / S, -sn[:, k] / S
            idftx[0, h, k, 1, p], idftx[1, h, k, 1, p] = sn[:, k] / S, c[:, k] / S
    lin = np.linspace(0.0, 1.0, S, dtype=np.float32)
    planes = np.stack([np.broadcast_to(lin[:, None], (S, S)), np.broadcast_to(lin[None], (S, S)), np.ones((S, S))])
    px = planes.reshape(3, 4, 4, 4, S).transpose(0, 2, 1, 3, 4)
    px = np.broadcast_to(px[:, :, None], (3, 4, G, 4, 4, S)).reshape(12, PX)
    ft = np.fft.fft2(planes.astype(f))[:, kx.astype(int)][..., :M2]
    ft = np.stack([ft.real, ft.imag], 0)
    out = {
        "dfty": dfty, "dftx": dftx.reshape(P, 2, P), "idftx": idftx.reshape(P, 2, P), "idfty": idfty,
        "eye": np.eye(P), "groupmean": np.tile(np.eye(C), (4, 4)) / 4, "grid_px": px, "grid_ft": ft.reshape(2, 3, 2 * MODES),
    }
    return {k: np.ascontiguousarray(v, dtype=np.float32) for k, v in out.items()}


def at_least(eng, sem, value):
    if isinstance(value, int) and value <= 0:
        return
    eng.wait_ge(sem, value)


def walk(eng, n, body, head=2):
    if n == 1:
        body(0, 0, 0, True)
        return
    for i in range(min(head, n) if n <= 2 else min(head, n - 2)):
        body(i, i % 2, i // 2, i == n - 1)
    if n > head + 2:
        with eng.Fori(head // 2, n // 2 - 1) as m:
            body(2 * m, 0, m, False)
            body(2 * m + 1, 1, m, False)
    if n > 2:
        body(n - 2, 0, n // 2 - 1, False)
        body(n - 1, 1, n // 2 - 1, True)


class Semaphores:

    def __init__(self, ctx, nc):
        def sem(name):
            return ctx.enter_context(nc.semaphore(name))

        self.in_a = sem("in_a")
        self.in_b = sem("in_b")
        self.par_in = sem("par_in")
        self.const_in = sem("const_in")
        self.u_in0 = sem("u_in0")
        self.u_in1 = sem("u_in1")
        self.y_in0 = sem("y_in0")
        self.y_in1 = sem("y_in1")
        self.bn_done = sem("bn_done")
        self.tr_done = sem("tr_done")
        self.vt_ready = sem("vt_ready")
        self.fy_done = sem("fy_done")
        self.a_ready = sem("a_ready")
        self.t2_done = sem("t2_done")
        self.a2_ready = sem("a2_ready")
        self.fx_done = sem("fx_done")
        self.sp_ready = sem("sp_ready")
        self.sp_out0 = sem("sp_out0")
        self.sp_out1 = sem("sp_out1")
        self.w_in = sem("w_in")
        self.w_tmp = sem("w_tmp")
        self.w_fix = sem("w_fix")
        self.mix_done = sem("mix_done")
        self.mix_low = sem("mix_low")
        self.mix_high = sem("mix_high")
        self.y_out0 = sem("y_out0")
        self.y_out1 = sem("y_out1")
        self.ix_done = sem("ix_done")
        self.s_ready = sem("s_ready")
        self.tt_done = sem("tt_done")
        self.t_ready = sem("t_ready")
        self.um_done = sem("um_done")
        self.uo_ready = sem("uo_ready")
        self.st_done = sem("st_done")
        self.u_out0 = sem("u_out0")
        self.u_out1 = sem("u_out1")
        self.step = sem("step")
        self.aggr = sem("aggr")
        self.pe_step = sem("pe_step")
        self.act_step = sem("act_step")
        self.hq_done = sem("hq_done")
        self.hq_ready = sem("hq_ready")
        self.hq_out0 = sem("hq_out0")
        self.hq_out1 = sem("hq_out1")
        self.pw_done = sem("pw_done")
        self.pw_ready = sem("pw_ready")
        self.range = range(self.in_a.num, self.pw_ready.num + 1)


def end_phase(nc, sems):
    nc.gpsimd.sem_clear(sems.range)
    nc.all_engine_barrier()


def forward_phase(nc, sems, tag, K, load, n, spectrum, scale_bias, load_weights):
    s = sems
    with ExitStack() as ctx:
        u = ctx.enter_context(nc.sbuf_tensor(f"f_u{tag}", [P, 2, PX], F32))
        vt = ctx.enter_context(nc.sbuf_tensor(f"f_vt{tag}", [P, 2, 1024], F32))
        at = ctx.enter_context(nc.sbuf_tensor(f"f_at{tag}", [P, 2, 2, C, 32], F32))
        sp = ctx.enter_context(nc.sbuf_tensor(f"f_sp{tag}", [P, 2, 2, 32, M2], F32))
        pf = ctx.enter_context(nc.psum_tensor(f"f_pf{tag}", [P, 2, 2, CH], F32))
        px = ctx.enter_context(nc.psum_tensor(f"f_px{tag}", [P, 2, CH], F32))
        u_in, sp_out = [s.u_in0, s.u_in1], [s.sp_out0, s.sp_out1]
        block = ctx.enter_context(nc.Block())

        @block.sync
        def _(eng):
            def store(i, par):
                eng.wait_ge(s.sp_ready, 2 * i + 2)
                eng.dma_start(spectrum(i).rearrange("q p m -> p q m"),
                              sp[:, par].rearrange("p q x k -> p q (x k)")[:, :, 0:SPEC]).then_inc(sp_out[par], 16)

            def body(i, par, r, last):
                at_least(eng, s.vt_ready, 4 * (i - 1))
                load(eng, u[:, par], i, u_in[par])
                if isinstance(i, int) and i < 10:
                    load_weights(eng, i, n)
                if not (isinstance(i, int) and i < 2):
                    store(i - 2, par)

            walk(eng, n, body, head=10)
            for i in range(max(n - 2, 0), n):
                store(i, i % 2)
            eng.wait_ge(s.sp_out0, 16 * ((n + 1) // 2))
            if n > 1:
                eng.wait_ge(s.sp_out1, 16 * (n // 2))

        @block.gpsimd
        def _(pool):
            if n > 1:
                for h in range(2):
                    turn_weights(pool, s.w_in, s.w_fix, K, h)

        @block.scalar
        def _(act):
            def body(i, par, r, last):
                act.wait_ge(u_in[par], 16 * load.count * (r + 1))
                for k in range(4):
                    t = u[:, par, 1024 * k:1024 * k + 1024]
                    nc.scalar.activation(t, t, ACT.Relu, bias=scale_bias[1], scale=scale_bias[0]).then_inc(s.bn_done, 1)

            if scale_bias is not None:
                walk(act, n, body)

        @block.vector
        def _(dve):
            ve = nc.vector

            def pixels_turn(i, par, g):
                if scale_bias is not None:
                    dve.wait_ge(s.bn_done, 4 * i + g + 1)
                elif g == 0:
                    dve.wait_ge(u_in[par], 16 * load.count)
                at_least(dve, s.fy_done, 4 * i + g - 1)
                ve.transpose(vt[:, g % 2, :], u[:, par, 1024 * g:1024 * g + 1024]).then_inc(s.vt_ready, 1)

            def rows_turn(i, par, q):
                dve.wait_ge(s.fy_done, 4 * i + 2 * q + 2)
                at_least(dve, s.fx_done, 2 * (i - 1))
                ve.transpose(at[:, par, q], pf[:, q].rearrange("p h (x c) -> p c h x", c=C)).then_inc(s.a2_ready, 1)

            def modes_turn(i, par, q, r):
                dve.wait_ge(s.fx_done, 2 * i + q + 1)
                if q == 0 and not (isinstance(i, int) and i < 2):
                    dve.wait_ge(sp_out[par], 16 * r)
                ve.transpose(sp[:, par, q].rearrange("p x k -> p k x"),
                             px[:, q, 0:ROW].rearrange("p (k c) -> p k c", c=C)).then_inc(s.sp_ready, 1)

            def body(i, par, r, last):
                later = not (isinstance(i, int) and i == 0)
                pixels_turn(i, par, 0)
                if later:
                    rows_turn(i - 1, 1 - par, 1)
                pixels_turn(i, par, 1)
                if later:
                    modes_turn(i - 1, 1 - par, 1, 0)
                pixels_turn(i, par, 2)
                rows_turn(i, par, 0)
                pixels_turn(i, par, 3)
                modes_turn(i, par, 0, r)
                if last:
                    rows_turn(i, par, 1)
                    modes_turn(i, par, 1, r)

            walk(dve, n, body)
            if n == 1:
                for h in range(2):
                    turn_weights(dve, s.w_in, s.w_fix, K, h)

        @block.tensor
        def _(pe):
            def transform_y(i, g):
                pe.wait_ge(s.vt_ready, 4 * i + g + 1)
                if g % 2 == 0:
                    at_least(pe, s.a2_ready, 2 * (i - 1) + g // 2 + 1)
                rhs = vt[:, g % 2, :].rearrange("p (x t c) -> p t x c", t=2, c=C)
                for t in range(2):
                    ins = nc.tensor.matmul(pf[:, g // 2, g % 2, :], K["dfty"][:, t, :], rhs[:, t],
                                           start=(t == 0), stop=(t == 1))
                ins.then_inc(s.fy_done, 1)

            def transform_x(i, par, q):
                pe.wait_ge(s.a2_ready, 2 * i + q + 1)
                at_least(pe, s.sp_ready, 2 * (i - 1) + q + 1)
                rhs = at[:, par, q].rearrange("p c (k r) -> p r k c", r=2)
                for t in range(2):
                    ins = nc.tensor.matmul(px[:, q, 0:ROW], K["dftx"][:, t, :], rhs[:, t, 0:M2],
                                           start=(t == 0), stop=(t == 1))
                ins.then_inc(s.fx_done, 1)

            def body(i, par, r, last):
                transform_y(i, 0)
                if not (isinstance(i, int) and i == 0):
                    transform_x(i - 1, 1 - par, 1)
                transform_y(i, 1)
                transform_y(i, 2)
                transform_x(i, par, 0)
                transform_y(i, 3)
                if last:
                    transform_x(i, par, 1)

            walk(pe, n, body)


PIECES = 4


def turn_weights(eng, w_in, done, K, h):
    w, tmp, base = K["mixw"], K["mixtmp"], 3 * PIECES * h
    eng.wait_ge(w_in, 128)
    rows = slice(2 * h * C + C, 2 * h * C + 2 * C)
    size = 2 * C * MODES // PIECES
    flat = w[rows].rearrange("p k m r -> p (k m) r")
    for t in range(PIECES):
        re, im = (flat[:, size * t:size * t + size, j] for j in range(2))
        at_least(eng, done, base + 3 * t)
        eng.tensor_copy(tmp[rows, :], re).then_inc(done, 1)
        eng.wait_ge(done, base + 3 * t + 1)
        eng.tensor_scalar(re, im, -1.0, None, ALU.mult).then_inc(done, 1)
        eng.wait_ge(done, base + 3 * t + 2)
        eng.tensor_copy(im, tmp[rows, :]).then_inc(done, 1)
    eng.wait_ge(done, base + 3 * PIECES)


def weight_loader(s, K, fw1, fw2, layer):
    def load(eng, i, n):
        for j in range(8):
            if n == 1 or j == i - 1:
                k, block = j // 4, j % 4
                src = (fw1, fw2)[k][layer].rearrange("i o x y r -> i (o x y) r")
                eng.dma_start(K["mixw"][C * block:C * block + C, k], src).then_inc(s.w_in, 16)
    return load


def mix_phase(nc, sems, tag, K, B, xsp, ysp, par, layer, first, consts):
    s = sems
    HB = B // 2
    with ExitStack() as ctx:
        xm = ctx.enter_context(nc.sbuf_tensor(f"m_x{tag}", [P, 2, HB, MODES], F32))
        ys = ctx.enter_context(nc.sbuf_tensor(f"m_y{tag}", [P, 2, 2, ROW], F32))
        bank = [ctx.enter_context(nc.psum_tensor(f"m_p{tag}{b}", [P, CH], F32)) for b in range(4)]
        pp = [ctx.enter_context(nc.psum_tensor(f"m_pp{tag}{b}", [P, CH], F32)) for b in range(2)]
        wv = K["mixw"][:, :, :, :].rearrange("p k (o x y) r -> p k o x y r", o=C, x=M1)
        wflat = K["mixw"][:, :, :, :].rearrange("p k m r -> p (k m r)")
        folds = 4 * C * MODES // CH
        x_in, y_out = [s.in_a, s.in_b], [s.y_out0, s.y_out1]
        block = ctx.enter_context(nc.Block())

        @block.sync
        def _(eng):
            for k in range(2):
                cut = slice(MODES * k, MODES * k + MODES)
                for h in range(2):
                    for ri in range(2):
                        if first:
                            a = 64 * h + 4 * ri
                            eng.dma_start(xm[a:a + 1, k].rearrange("o (n q) m -> o n q m", q=2),
                                          xsp.rearrange("q (r h o n) m -> r h o n q m", r=2, h=2, o=1)[ri, h][:, :, :, cut])\
                                .then_inc(x_in[k], 16)
                            eng.dma_start(xm[a + 1:a + 4, k], consts["grid_ft"][ri][:, cut].rearrange("j (o m) -> j o m", o=1)
                                          .broadcast_to([3, HB, MODES])).then_inc(x_in[k], 16)
                        else:
                            a = 64 * h + 32 * ri
                            eng.dma_start(xm[a:a + C, k], xsp.rearrange("b (r h c) m -> r h c b m", r=2, h=2)[ri, h][:, :, cut])\
                                .then_inc(x_in[k], 16)
            for q in range(KX):
                eng.wait_ge(s.mix_low, q + 1)
                eng.wait_ge(s.mix_high, q + 1)
                for h in range(2):
                    eng.dma_start(ysp.rearrange("b (r h x) m -> h x b r m", r=2, h=2)[h, q],
                                  ys[64 * h:64 * h + HB, q % 2]).then_inc(y_out[q % 2], 16)
            eng.wait_ge(s.y_out0, 16 * KX)
            eng.wait_ge(s.y_out1, 16 * KX)

        @block.scalar
        def _(act):
            for g in range(4):
                rows = slice(C * g, C * g + C)
                act.dma_start(K["wbd"][rows, rows], par["w_w"][layer]).then_inc(s.par_in, 16)
                for name in ("w_b", "bn_g", "bn_b"):
                    act.dma_start(K[name][rows, :], par[name][layer].rearrange("(c o) -> c o", o=1)).then_inc(s.par_in, 16)
            for q in range(KX):
                act.wait_ge(s.mix_done, 2 * q + 2)
                if q >= 2:
                    act.wait_ge(y_out[q % 2], 32 * (q // 2))
                out = ys[:, q % 2].rearrange("b r (k c) -> b r k c", c=C)[:, :, 6:12, :]
                nc.scalar.copy(out, bank[(2 * q + 1) % 4][:, 0:ROW]).then_inc(s.mix_high, 1)
            act.wait_ge(s.par_in, 16 * 16)

        @block.vector
        def _(dve):
            if first:
                for n in range(folds):
                    dve.wait_ge(s.pw_done, n + 1)
                    nc.vector.tensor_copy(wflat[:, CH * n:CH * n + CH], pp[n % 2][:, :]).then_inc(s.pw_ready, 1)
                dve.wait_ge(s.pw_done, folds + 1)
                nc.vector.tensor_copy(K["pwbd"][:, :], pp[1][0:16, 0:P]).then_inc(s.pw_ready, 1)
            for q in range(KX):
                dve.wait_ge(s.mix_done, 2 * q + 1)
                if q >= 2:
                    dve.wait_ge(y_out[q % 2], 32 * (q // 2))
                out = ys[:, q % 2].rearrange("b r (k c) -> b r k c", c=C)[:, :, 0:6, :]
                nc.vector.tensor_copy(out, bank[2 * q % 4][:, 0:ROW]).then_inc(s.mix_low, 1)

        @block.tensor
        def _(pe):
            if first:
                for n in range(folds):
                    at_least(pe, s.pw_ready, n - 1)
                    nc.tensor.matmul(pp[n % 2][:, :], K["lift_mix"][:, :], wflat[:, CH * n:CH * n + CH],
                                     start=True, stop=True).then_inc(s.pw_done, 1)
                pe.wait_ge(s.par_in, 16 * 16)
                pe.wait_ge(s.pw_ready, folds)
                nc.tensor.matmul(pp[1][0:16, 0:P], K["lift_px"][:, :], K["wbd"][:, :],
                                 start=True, stop=True).then_inc(s.pw_done, 1)
            depth = 8 if first else 2 * C
            for q in range(KX):
                k, x = q // M1, q % M1
                if x == 0:
                    pe.wait_ge(x_in[k], 128 if first else 64)
                for half in range(2):
                    n = 2 * q + half
                    at_least(pe, s.mix_high if half else s.mix_low, q - 1)
                    for t in range(6):
                        y = 6 * half + t
                        for h in range(2):
                            rows = slice(64 * h, 64 * h + depth)
                            out = bank[n % 4][64 * h:64 * h + HB, 0:ROW].rearrange("b (r k c) -> b k c r", r=2, k=6)[:, t]
                            ins = nc.tensor.matmul(out, xm[rows, k, :, M2 * x + y], wv[rows, k, :, x, y, :],
                                                   start=True, stop=True)
                    ins.then_inc(s.mix_done, 1)


def inverse_phase(nc, sems, tag, K, U, ysp, n, images, scale_bias, stats):
    s = sems
    first = images is not None
    with ExitStack() as ctx:
        v = ctx.enter_context(nc.sbuf_tensor(f"i_v{tag}", [16 if first else P, 2, PX], F32))
        ysb = ctx.enter_context(nc.sbuf_tensor(f"i_y{tag}", [P, 2, 2, ROW], F32))
        st = ctx.enter_context(nc.sbuf_tensor(f"i_t{tag}", [P, 2, 2, C, 32], F32))
        uo = ctx.enter_context(nc.sbuf_tensor(f"i_u{tag}", [P, 2, PX], F32))
        ps_x = ctx.enter_context(nc.psum_tensor(f"i_px{tag}", [P, 2, CH], F32))
        ps_u = [ctx.enter_context(nc.psum_tensor(f"i_pu{tag}{b}", [P, CH], F32)) for b in range(4)]
        u_in, y_in, u_out = [s.u_in0, s.u_in1], [s.y_in0, s.y_in1], [s.u_out0, s.u_out1]
        loads = 4 if first else 1
        block = ctx.enter_context(nc.Block())

        @block.sync
        def _(eng):
            if first:
                for par in range(2):
                    eng.dma_start(v[4:16, par], K["grid_px"]).then_inc(s.const_in, 16)

            def store(i, par):
                eng.wait_ge(s.uo_ready, NCH * i + NCH)
                eng.dma_start(U[i], uo[:, par]).then_inc(u_out[par], 16)

            def body(i, par, r, last):
                at_least(eng, s.ix_done, 4 * (i - 1))
                eng.dma_start(ysb[:, par], ysp[bass.ds(2 * i, 2)].rearrange("q p m -> p q m")).then_inc(y_in[par], 16)
                at_least(eng, s.um_done, NCH * (i - 1))
                if first:
                    img = images.rearrange("(n g) (r a b) y -> n a g r (b y)", g=G, r=4, a=4)[i]
                    for a in range(4):
                        eng.dma_start(v[a:a + 1, par].rearrange("o (g r m) -> o g r m", g=G, r=4), img[a:a + 1])\
                            .then_inc(u_in[par], 16)
                else:
                    eng.dma_start(v[:, par], U[i]).then_inc(u_in[par], 16)
                if not (isinstance(i, int) and i < 2):
                    store(i - 2, par)

            walk(eng, n, body)
            store(n - 2, 0)
            store(n - 1, 1)
            eng.wait_ge(s.u_out0, 8 * n)
            eng.wait_ge(s.u_out1, 8 * n)

        @block.scalar
        def _(act):
            def norm(i, par, r):
                act.wait_ge(u_in[par], 16 * r + 16)
                for k in range(4):
                    px = v[:, par, 1024 * k:1024 * k + 1024]
                    nc.scalar.activation(px, px, ACT.Relu, bias=scale_bias[1], scale=scale_bias[0])\
                        .then_inc(s.bn_done, 1)

            def body(i, par, r, last):
                if not first and isinstance(i, int) and i == 0:
                    norm(0, 0, 0)
                for k in range(NCH):
                    c = NCH * i + k
                    act.wait_ge(s.um_done, c + 1)
                    if k == 0 and not (isinstance(i, int) and i < 2):
                        act.wait_ge(u_out[par], 16 * r)
                        act.wait_ge(s.st_done, NCH * (i - 1))
                    nc.scalar.activation(uo[:, par, CH * k:CH * k + CH], ps_u[k % 4][:, :], ACT.Identity,
                                         bias=K["w_b"][:, 0:1]).then_inc(s.uo_ready, 1)
                    if k == 3 and not first and not last:
                        norm(i + 1, 1 - par, r if par == 0 else r + 1)

            walk(act, n, body)

        def turned(dve, i, par, j):
            dve.wait_ge(s.ix_done, 4 * i + j + 1)
            at_least(dve, s.um_done, NCH * (i - 1))
            nc.vector.transpose(st[:, par, j // 2, 16 * (j % 2):16 * (j % 2) + 16, :],
                                ps_x[:, j % 2, :].rearrange("p (c k) -> p c k", k=32)).then_inc(s.t_ready, 1)

        @block.vector
        def _(dve):
            for b in range(2):
                nc.vector.memset(ps_x[:, b, :], 0.0).then_inc(s.s_ready, 1)
            for j in range(4):
                turned(dve, 0, 0, j)

            def body(i, par, r, last):
                for k in range(NCH):
                    c = NCH * i + k
                    dve.wait_ge(s.uo_ready, c + 1)
                    nc.vector.bn_stats(stats[:, bass.ds(6 * c, 6)], uo[:, par, CH * k:CH * k + CH])\
                        .then_inc(s.st_done, 1)
                    if not last and k % 2 == 1:
                        turned(dve, i + 1, 1 - par, k // 2)

            walk(dve, n, body)

        @block.tensor
        def _(pe):
            def inverse_x(i, par, r, j):
                if j == 0:
                    pe.wait_ge(y_in[par], 16 * r + 16)
                at_least(pe, s.t_ready, 4 * i + j - 1)
                rhs = ysb[:, par, j // 2, :].rearrange("p (k c) -> p c k", c=C)[:, 16 * (j % 2):16 * (j % 2) + 16, :]
                out = ps_x[:, j % 2, :].rearrange("p (c k r) -> p r c k", k=16, r=2)
                for t in range(2):
                    ins = nc.tensor.matmul(out[:, t, :, 0:M2], K["idftx"][:, t, :], rhs, start=True, stop=True,
                                           skip_group_check=True)
                ins.then_inc(s.ix_done, 1)

            def pixels(i, par, r, k):
                c = NCH * i + k
                if first:
                    if k == 0:
                        pe.wait_ge(s.const_in, 32)
                        pe.wait_ge(u_in[par], 16 * loads * (r + 1))
                else:
                    pe.wait_ge(s.bn_done, 4 * i + k // 2 + 1)
                pe.wait_ge(s.t_ready, 4 * i + 2 * (k // 4) + 2)
                at_least(pe, s.uo_ready, c - 3)
                weights = K["pwbd"] if first else K["wbd"]
                bank = ps_u[k % 4]
                nc.tensor.matmul(bank[:, :], weights[:, :], v[:, par, CH * k:CH * k + CH], start=True, stop=False,
                                 skip_group_check=True)
                g = k // 2
                for e in range(2):
                    for a in range(4):
                        rr = 2 * (k % 2) + e
                        ins = nc.tensor.matmul(bank[32 * a:32 * a + 32, 256 * e:256 * e + 256],
                                               st[:, par, g // 2, :, 16 * (g % 2) + 4 * a + rr], K["idfty"][:, :],
                                               start=False, stop=True, skip_group_check=True)
                ins.then_inc(s.um_done, 1)

            pe.wait_ge(s.s_ready, 2)
            for j in range(4):
                inverse_x(0, 0, 0, j)

            def body(i, par, r, last):
                for k in range(NCH):
                    pixels(i, par, r, k)
                    if not last and k % 2 == 0:
                        inverse_x(i + 1, 1 - par, r if par == 0 else r + 1, k // 2)

            walk(pe, n, body)


def norm_phase(nc, sems, tag, K, n, stats, scale_bias):
    s = sems
    scale, bias = scale_bias
    with ExitStack() as ctx:
        mv = ctx.enter_context(nc.sbuf_tensor(f"n_mv{tag}", [P, 2], F32))
        avg = ctx.enter_context(nc.sbuf_tensor(f"n_avg{tag}", [P, 2], F32))
        dm = ctx.enter_context(nc.sbuf_tensor(f"n_dm{tag}", [P, 2], F32))
        sd = ctx.enter_context(nc.sbuf_tensor(f"n_sd{tag}", [P, 4], F32))
        ps = ctx.enter_context(nc.psum_tensor(f"n_ps{tag}", [P, CH], F32))
        block = ctx.enter_context(nc.Block())

        @block.vector
        def _(dve):
            count = 0

            def then(ins):
                nonlocal count
                count += 1
                ins.then_inc(s.step, 1)
                dve.wait_ge(s.step, count)

            then(nc.vector.bn_aggr(mv[:, :], stats[:, 0:6 * NCH * n]))
            dve.sem_inc(s.aggr, 1)
            dve.wait_ge(s.pe_step, 1)
            then(nc.vector.tensor_copy(avg[:, :], ps[:, 0:2]))
            then(nc.vector.tensor_tensor(dm[:, 0:1], mv[:, 0:1], avg[:, 0:1], ALU.subtract))
            then(nc.vector.tensor_tensor(dm[:, 1:2], dm[:, 0:1], dm[:, 0:1], ALU.mult))
            dve.sem_inc(s.aggr, 1)
            dve.wait_ge(s.pe_step, 2)
            then(nc.vector.tensor_tensor(sd[:, 0:1], avg[:, 1:2], ps[:, 2:3], ALU.add))
            then(nc.vector.tensor_scalar(sd[:, 1:2], sd[:, 0:1], EPS, None, ALU.add))
            dve.sem_inc(s.aggr, 1)
            dve.wait_ge(s.act_step, 1)
            then(nc.vector.reciprocal(sd[:, 3:4], sd[:, 2:3]))
            then(nc.vector.tensor_tensor(scale, sd[:, 3:4], K["bn_g"][:, 0:1], ALU.mult))
            then(nc.vector.tensor_tensor(sd[:, 0:1], avg[:, 0:1], scale, ALU.mult))
            then(nc.vector.tensor_tensor(bias, K["bn_b"][:, 0:1], sd[:, 0:1], ALU.subtract))

        @block.scalar
        def _(act):
            act.wait_ge(s.aggr, 3)
            nc.scalar.activation(sd[:, 2:3], sd[:, 1:2], ACT.Sqrt).then_inc(s.act_step, 1)

        @block.tensor
        def _(pe):
            pe.wait_ge(s.aggr, 1)
            nc.tensor.matmul(ps[:, 0:2], K["groupmean"][:, :], mv[:, :], start=True, stop=True).then_inc(s.pe_step, 1)
            pe.wait_ge(s.aggr, 2)
            nc.tensor.matmul(ps[:, 2:3], K["groupmean"][:, :], dm[:, 1:2], start=True, stop=True).then_inc(s.pe_step, 1)


def project_phase(nc, sems, K, U, n, h_img, scale_bias, q_w, q_b):
    s = sems
    scale, bias = scale_bias
    with ExitStack() as ctx:
        u = ctx.enter_context(nc.sbuf_tensor("proj_u", [P, 2, PX], F32))
        hb = ctx.enter_context(nc.sbuf_tensor("proj_h", [P, 2, 2, CH], F32))
        qbd = ctx.enter_context(nc.sbuf_tensor("proj_w", [P, P], F32))
        qc = ctx.enter_context(nc.sbuf_tensor("proj_c", [P, 4], F32))
        qbias = ctx.enter_context(nc.sbuf_tensor("proj_b", [P, 1], F32))
        ones = ctx.enter_context(nc.sbuf_tensor("proj_1", [P, P], F32))
        bank = [ctx.enter_context(nc.psum_tensor(f"proj_p{b}", [P, CH], F32)) for b in range(4)]
        pc = ctx.enter_context(nc.psum_tensor("proj_pc", [P, CH], F32))
        u_in, out = [s.u_in0, s.u_in1], [s.hq_out0, s.hq_out1]
        block = ctx.enter_context(nc.Block())

        @block.sync
        def _(eng):
            for g in range(G):
                eng.dma_start(qc[C * g:C * g + C, 0:1], q_w).then_inc(s.const_in, 16)
            eng.dma_start(qc[:, 1:2], q_b.rearrange("(a o) -> a o", o=1).broadcast_to([P, 1])).then_inc(s.const_in, 16)

            def store(i, par):
                eng.wait_ge(s.hq_ready, 2 * i + 2)
                for j in range(4):
                    for kk in range(2):
                        eng.dma_start(h_img[i, 2 * kk + j // 2].rearrange("(t r a m) -> t a r m", t=2, r=2, a=4)[j % 2],
                                      hb[32 * j:32 * j + 4, par, kk].rearrange("p (r m) -> p r m", r=2))\
                            .then_inc(out[par], 16)

            def body(i, par, r, last):
                at_least(eng, s.hq_done, 2 * (i - 1))
                eng.dma_start(u[:, par], U[i]).then_inc(u_in[par], 16)
                if not (isinstance(i, int) and i < 2):
                    store(i - 2, par)

            walk(eng, n, body)
            store(n - 2, 0)
            store(n - 1, 1)
            eng.wait_ge(s.hq_out0, 64 * n)
            eng.wait_ge(s.hq_out1, 64 * n)

        @block.vector
        def _(dve):
            nc.vector.memset(qbd[:, :], 0.0).then_inc(s.step, 1)
            nc.vector.memset(ones[:, :], 1.0 / G).then_inc(s.step, 1)
            for b in range(4):
                nc.vector.memset(bank[b][:, :], 0.0).then_inc(s.step, 1)
            dve.wait_ge(s.const_in, 16 * (G + 1))
            dve.wait_ge(s.step, 6)
            for g in range(G):
                rows = slice(C * g, C * g + C)
                nc.vector.tensor_tensor(qbd[rows, g:g + 1], qc[rows, 0:1], scale[rows, :], ALU.mult).then_inc(s.step, 1)
            nc.vector.tensor_tensor(qc[:, 2:3], qc[:, 0:1], bias, ALU.mult).then_inc(s.step, 1)
            dve.wait_ge(s.pe_step, 1)
            nc.vector.tensor_tensor(qbias[:, :], pc[:, 0:1], qc[:, 1:2], ALU.add).then_inc(s.step, 1)

        @block.scalar
        def _(act):
            act.wait_ge(s.step, 12)

            def body(i, par, r, last):
                for kk in range(2):
                    act.wait_ge(s.hq_done, 2 * i + kk + 1)
                    if kk == 0 and not (isinstance(i, int) and i < 2):
                        act.wait_ge(out[par], 128 * r)
                    nc.scalar.activation(hb[:, par, kk, :], bank[2 * par + kk][:, :], ACT.Identity,
                                         bias=qbias[:, 0:1]).then_inc(s.hq_ready, 1)

            walk(act, n, body)

        @block.tensor
        def _(pe):
            pe.wait_ge(s.step, 11)
            nc.tensor.matmul(pc[:, 0:1], ones[:, :], qc[:, 2:3], start=True, stop=True).then_inc(s.pe_step, 1)

            def body(i, par, r, last):
                pe.wait_ge(u_in[par], 16 * r + 16)
                for kk in range(2):
                    at_least(pe, s.hq_ready, 2 * i + kk - 3)
                    for j in range(4):
                        k = 4 * kk + j
                        ins = nc.tensor.matmul(bank[2 * par + kk][32 * j:32 * j + G, :], qbd[:, 0:G],
                                               u[:, par, CH * k:CH * k + CH], start=True, stop=True)
                    ins.then_inc(s.hq_done, 1)

            walk(pe, n, body)


def operator(nc, ctx, sems, d, h_img):
    B = d["x"].shape[0]
    n = B // G
    layers = d["w_w"].shape[0]

    def sb(name, shape):
        return ctx.enter_context(nc.sbuf_tensor("k_" + name, shape, F32))

    K = {
        "mixw": sb("mixw", [P, 2, C * MODES, 2]), "mixtmp": sb("mixtmp", [P, 2 * C * MODES // PIECES]),
        "wbd": sb("wbd", [P, P]), "pwbd": sb("pwbd", [16, P]), "lift_mix": sb("lift_mix", [P, P]),
        "lift_px": sb("lift_px", [P, 4 * G]), "w_b": sb("w_b", [P, 1]), "bn_g": sb("bn_g", [P, 1]), "bn_b": sb("bn_b", [P, 1]),
    }
    for name in ("dfty", "dftx", "idftx", "idfty", "eye", "groupmean"):
        K[name] = sb(name, list(d[name].shape))
    K["grid_px"] = d["grid_px"]
    stats = sb("stats", [P, 6 * NCH * n])
    sb_t = sb("scale_bias", [P, 2])
    scale_bias = (sb_t[:, 0:1], sb_t[:, 1:2])
    U = nc.dram_tensor("u_scratch", (n, P, PX), F32).ap()
    xsp = nc.dram_tensor("x_spectrum", (2 * n, P, SPEC), F32).ap()
    isp = nc.dram_tensor("image_spectrum", (2, P, SPEC), F32).ap()
    ysp = nc.dram_tensor("y_spectrum", (2 * n, P, ROW), F32).ap()
    par = {"w_w": d["w_w"], "w_b": d["w_b"], "bn_g": d["bn_g"], "bn_b": d["bn_b"]}
    images = d["x"].rearrange("b x y o -> b x (y o)")

    def load_images(eng, buf, i, sem):
        img = images.rearrange("(n g) (r a b) y -> a n g r (b y)", g=G, r=4, a=4)
        for a in range(4):
            eng.dma_start(buf[C * a:C * a + C].rearrange("p (g r m) -> p g r m", g=G, r=4), img[a]).then_inc(sem, 16)

    load_images.count = 4

    def load_group(eng, buf, i, sem):
        eng.dma_start(buf, U[i]).then_inc(sem, 16)

    load_group.count = 1
    s = sems

    with nc.sbuf_tensor("zero", [P, 8 * ROW], F32) as zero, nc.Block() as block:
        names = ("dfty", "dftx", "idftx", "idfty", "eye", "groupmean")

        @block.vector
        def _(dve):
            for t in ("wbd", "lift_mix", "lift_px"):
                nc.vector.memset(K[t][:, :], 0.0).then_inc(s.step, 1)
            nc.vector.memset(zero[:, :], 0.0).then_inc(s.step, 1)

        @block.sync
        def _(eng):
            for name in names:
                eng.dma_start(K[name][:], d[name]).then_inc(s.const_in, 16)
            eng.wait_ge(s.step, 4)
            zeros = zero[:, :].rearrange("p (x m) -> p x m", m=ROW)
            for t in range(4 * 2 * n // P):
                eng.dma_start(ysp.rearrange("b (r x) m -> (b r) x m", x=32)[P * t:P * t + P, KX:32], zeros).then_inc(s.in_a, 16)
            eng.wait_ge(s.in_a, 16 * (4 * 2 * n // P))
            with nc.allow_non_contiguous_dma("lifting weights, 128 words a piece"):
                for q in range(4):
                    rows, col = slice(C * q, C * q + C), 64 * (q // 2) + 4 * (q % 2)
                    eng.dma_start(K["lift_mix"][rows, col:col + 3], d["p_w"].rearrange("j c -> c j")).then_inc(s.const_in, 16)
                    eng.dma_start(K["lift_mix"][rows, col + 3:col + 4], d["p_b"].rearrange("(c o) -> c o", o=1)).then_inc(s.const_in, 16)
                    eng.dma_start(K["lift_px"][rows, q:3 * G:G], d["p_w"].rearrange("j c -> c j")).then_inc(s.const_in, 16)
                    eng.dma_start(K["lift_px"][rows, 3 * G + q:3 * G + q + 1], d["p_b"].rearrange("(c o) -> c o", o=1)).then_inc(s.const_in, 16)
            eng.wait_ge(s.const_in, 16 * (len(names) + 16))
    end_phase(nc, s)

    fw1, fw2 = d["fw1"], d["fw2"]
    forward_phase(nc, s, "_0", K, load_images, 1, lambda i: isp, None, weight_loader(s, K, fw1, fw2, 0))
    end_phase(nc, s)
    mix_phase(nc, s, "_0", K, B, isp, ysp, par, 0, True, d)
    end_phase(nc, s)
    inverse_phase(nc, s, "_0", K, U, ysp, n, images, None, stats)
    end_phase(nc, s)
    norm_phase(nc, s, "_0", K, n, stats, scale_bias)
    end_phase(nc, s)
    with nc.Fori(1, layers) as layer:
        forward_phase(nc, s, "", K, load_group, n, lambda i: xsp[bass.ds(2 * i, 2)], scale_bias, weight_loader(s, K, fw1, fw2, layer))
        end_phase(nc, s)
        mix_phase(nc, s, "", K, B, xsp, ysp, par, layer, False, d)
        end_phase(nc, s)
        inverse_phase(nc, s, "", K, U, ysp, n, None, scale_bias, stats)
        end_phase(nc, s)
        norm_phase(nc, s, "", K, n, stats, scale_bias)
        end_phase(nc, s)
    project_phase(nc, s, K, U, n, h_img, scale_bias, d["q_w"], d["q_b"])
    end_phase(nc, s)


def token_constants(T, D):
    t = np.arange(T)
    gap = t[None, :] - 1 - t[:, None]
    decay = np.where(gap >= 0, np.float64(DECAY) ** np.maximum(gap, 0), 0.0)
    return {"decay": decay.astype(np.float32)}


class Chain:

    def __init__(self, eng, sem, base=0):
        self.eng, self.sem, self.base, self.n = eng, sem, base, 0

    def then(self, ins):
        self.n += 1
        ins.then_inc(self.sem, 1)
        self.eng.wait_ge(self.sem, self.base + self.n)


def norm_statistics(nc, chain, st, w):
    ve = nc.vector
    me, se, mo, so = (st[:, :, j] for j in (1, 2, 4, 5))
    chain.then(ve.tensor_tensor(w[:, 0], me, mo, ALU.add))
    chain.then(ve.tensor_tensor(w[:, 1], me, mo, ALU.subtract))
    chain.then(ve.tensor_tensor(w[:, 2], se, so, ALU.add))
    chain.then(ve.tensor_scalar(w[:, 0], w[:, 0], 0.5, None, ALU.mult))
    chain.then(ve.scalar_tensor_tensor(out=w[:, 1], in0=w[:, 1], scalar=0.25, in1=w[:, 1], op0=ALU.mult, op1=ALU.mult))
    chain.then(ve.tensor_scalar(w[:, 2], w[:, 2], 1.0 / S, EPS, ALU.mult, ALU.add))
    chain.then(ve.tensor_tensor(w[:, 3], w[:, 1], w[:, 2], ALU.add))


def spread_over(ap, D):
    return ap.rearrange("p (n o) -> p n o", o=1).broadcast_to([ap.shape[0], ap.shape[1], D])


def token_norm_phase(nc, sems, W, h_img, txt, d, le_dram):
    s = sems
    h = W["e"]
    T, B, D = h.shape
    halves = (slice(0, B // 2), slice(B // 2, B))
    with ExitStack() as ctx:
        le = ctx.enter_context(nc.sbuf_tensor("t_le", [T, B, D], F32))
        w = ctx.enter_context(nc.sbuf_tensor("t_w", [T, 6, B], F32))
        raw = ctx.enter_context(nc.sbuf_tensor("t_raw", [P, 2, 2, D], F32))
        rawe = ctx.enter_context(nc.sbuf_tensor("t_rawe", [D, 2, P], F32))
        ps = ctx.enter_context(nc.psum_tensor("t_ps", [P, 6, P], F32))
        block = ctx.enter_context(nc.Block())

        @block.sync
        def _(eng):
            for half, done in zip(halves, (s.in_a, s.in_b)):
                eng.dma_start(h[0:S, half], h_img.rearrange("n g (t d) -> t (n g) d", d=D)[:, half]).then_inc(done, 16)
                eng.dma_start(h[S:T, half], txt.rearrange("b t d -> t b d")[:, half]).then_inc(done, 16)
            for j, name in enumerate(("Dx", "Dy")):
                eng.dma_start(raw[:, j], d[name].rearrange("(q p) d -> p q d", p=P)).then_inc(s.w_in, 16)
            eng.dma_start(rawe[:, :, :], d["E"].rearrange("d (q n) -> d q n", q=2)).then_inc(s.w_in, 16)
            eng.dma_start(W["decay"][:, :], d["decay"]).then_inc(s.const_in, 16)
            eng.wait_ge(s.const_in, 16)
            for g, half in enumerate(halves):
                eng.wait_ge(s.aggr, 7 + g)
                eng.dma_start(le_dram[:, half], le[:, half, :]).then_inc(s.y_out0, 16)
            eng.wait_ge(s.y_out0, 32)

        @block.tensor
        def _(pe):
            pe.wait_ge(s.w_in, 48)
            for j in range(2):
                for q in range(2):
                    nc.tensor.transpose(ps[0:D, 2 * j + q, :], raw[:, j, q, :], W["eye"][:, :])
            for q in range(2):
                ins = nc.tensor.transpose(ps[:, 4 + q, 0:D], rawe[:, q, :], W["eye"][0:D, 0:D])
            ins.then_inc(s.pe_step, 1)

        @block.scalar
        def _(act):
            for g, half in enumerate(halves):
                act.wait_ge(s.aggr, 1 + g)
                nc.scalar.activation(le[:, half], h[:, half], ACT.Square).then_inc(s.act_step, 1)
            for g, half in enumerate(halves):
                act.wait_ge(s.aggr, 3 + g)
                nc.scalar.activation(w[:, 4, half], w[:, 3, half], ACT.Sqrt).then_inc(s.act_step, 1)
            for g, half in enumerate(halves):
                act.wait_ge(s.aggr, 5 + g)
                nc.scalar.activation(w[:, 5, half], w[:, 2, half], ACT.Sqrt).then_inc(s.act_step, 1)

        @block.vector
        def _(dve):
            ve = nc.vector
            c = Chain(dve, s.step)
            c.then(ve.memset(W["ones"][:, :], 1.0))
            dve.wait_ge(s.pe_step, 1)
            for j, t in enumerate(("DxT", "DyT")):
                c.then(ve.tensor_copy(W[t][:, :], ps[0:D, 2 * j:2 * j + 2, :].rearrange("p q n -> p (q n)")))
            c.then(ve.tensor_copy(W["ET"][:, :, :], ps[:, 4:6, 0:D]))
            for half, done in zip(halves, (s.in_a, s.in_b)):
                dve.wait_ge(done, 32)
                c.then(ve.tensor_reduce(w[:, 0, half], h[:, half], AX.X, ALU.add))
                c.then(ve.tensor_scalar(w[:, 0, half], w[:, 0, half], 1.0 / D, None, ALU.mult))
                c.then(ve.tensor_tensor(h[:, half], h[:, half], spread_over(w[:, 0, half], D), ALU.subtract))
                dve.sem_inc(s.aggr, 1)
            for g, half in enumerate(halves):
                dve.wait_ge(s.act_step, 1 + g)
                c.then(ve.tensor_reduce(w[:, 3, half], le[:, half], AX.X, ALU.add))
                c.then(ve.tensor_scalar(w[:, 3, half], w[:, 3, half], 1.0 / D, EPS, ALU.mult, ALU.add))
                dve.sem_inc(s.aggr, 1)
            for g, half in enumerate(halves):
                w1, w2, w3 = (w[:, j, half] for j in (1, 2, 3))
                dve.wait_ge(s.act_step, 3 + g)
                c.then(ve.reciprocal(w1, w[:, 4, half]))
                c.then(ve.tensor_scalar(w3, w3, EPS, None, ALU.subtract))
                c.then(ve.tensor_tensor(w2, w1, w1, ALU.mult))
                c.then(ve.tensor_tensor(w2, w2, w3, ALU.mult))
                c.then(ve.tensor_scalar(w2, w2, EPS, None, ALU.add))
                dve.sem_inc(s.aggr, 1)
                c.then(ve.tensor_tensor(h[:, half], h[:, half], spread_over(w1, D), ALU.mult))
            for g, half in enumerate(halves):
                dve.wait_ge(s.act_step, 5 + g)
                c.then(ve.reciprocal(w[:, 3, half], w[:, 5, half]))
                c.then(ve.tensor_tensor(le[:, half], h[:, half], spread_over(w[:, 3, half], D), ALU.mult))
                dve.sem_inc(s.aggr, 1)


def update_phase(nc, sems, W, usum):
    s = sems
    T, B, D = W["e"].shape
    n, CT = B // 4, 4 * T
    with ExitStack() as ctx:
        et = ctx.enter_context(nc.sbuf_tensor("up_et", [D, 2, CT], F32))
        eb = ctx.enter_context(nc.sbuf_tensor("up_eb", [T, 2, 4, D], F32))
        row = ctx.enter_context(nc.sbuf_tensor("up_row", [1, B * T], F32))
        pt = [ctx.enter_context(nc.psum_tensor(f"up_t{b}", [D, CH], F32)) for b in range(2)]
        pu = [ctx.enter_context(nc.psum_tensor(f"up_u{b}", [P, CH], F32)) for b in range(4)]
        pr = [ctx.enter_context(nc.psum_tensor(f"up_r{b}", [1, CH], F32)) for b in range(2)]
        block = ctx.enter_context(nc.Block())

        @block.tensor
        def _(pe):
            def sums(i, par):
                pe.wait_ge(s.u_in0, 2 * i + 2)
                at_least(pe, s.sp_ready, i - 1)
                for q in range(2):
                    ins = nc.tensor.matmul(pr[par][0:1, 0:CT], W["ones"][:, 0:1], W["x"][:, q, bass.ds(CT * i, CT)],
                                           start=(q == 0), stop=(q == 1))
                ins.then_inc(s.fx_done, 1)

            def body(i, par, r, last):
                pe.wait_ge(s.a_ready, i + 1)
                at_least(pe, s.vt_ready, i - 1)
                pe.nop(nofuse=True)
                for b in range(4):
                    ins = nc.tensor.transpose(pt[par][:, T * b:T * b + T], eb[:, par, b, :], W["eye"][0:T, 0:T])
                ins.then_inc(s.tr_done, 1)
                if not (isinstance(i, int) and i == 0):
                    sums(i - 1, 1 - par)
                pe.wait_ge(s.vt_ready, i + 1)
                at_least(pe, s.u_in0, 2 * (i - 1))
                for q in range(2):
                    ins = nc.tensor.matmul(pu[2 * par + q][:, 0:CT], W["DxT"][:, P * q:P * q + P], et[:, par, :],
                                           start=True, stop=True)
                ins.then_inc(s.fy_done, 1)
                if last:
                    sums(i, par)

            walk(pe, n, body)

        @block.gpsimd
        def _(pool):
            def body(i, par, r, last):
                at_least(pool, s.tr_done, i - 1)
                nc.gpsimd.tensor_copy(eb[:, par, :, :], W["e"][:, bass.ds(4 * i, 4), :]).then_inc(s.a_ready, 1)

            walk(pool, n, body)

        @block.scalar
        def _(act):
            def body(i, par, r, last):
                act.wait_ge(s.fy_done, i + 1)
                for q in range(2):
                    nc.scalar.activation(W["x"][:, q, bass.ds(CT * i, CT)], pu[2 * par + q][:, 0:CT], ACT.Relu)\
                        .then_inc(s.u_in0, 1)

            walk(act, n, body)

        @block.vector
        def _(dve):
            def sums_out(i, par):
                dve.wait_ge(s.fx_done, i + 1)
                nc.vector.tensor_copy(row[0:1, bass.ds(CT * i, CT)], pr[par][0:1, 0:CT]).then_inc(s.sp_ready, 1)

            def body(i, par, r, last):
                dve.wait_ge(s.tr_done, i + 1)
                at_least(dve, s.fy_done, i - 1)
                nc.vector.tensor_copy(et[:, par, :], pt[par][:, 0:CT]).then_inc(s.vt_ready, 1)
                if not (isinstance(i, int) and i == 0):
                    sums_out(i - 1, 1 - par)
                if last:
                    sums_out(i, par)

            walk(dve, n, body)

        @block.sync
        def _(eng):
            eng.wait_ge(s.sp_ready, n)
            eng.dma_start(usum.rearrange("(o b) t -> o (b t)", o=1), row[:, :]).then_inc(s.y_out0, 16)
            eng.wait_ge(s.y_out0, 16)


def decay_phase(nc, sems, usum, coef):
    s = sems
    B, T = usum.shape
    with ExitStack() as ctx:
        us = ctx.enter_context(nc.sbuf_tensor("d_us", [B, T], F32))
        sg = ctx.enter_context(nc.sbuf_tensor("d_sg", [B, T], F32))
        sm = ctx.enter_context(nc.sbuf_tensor("d_sm", [B, T], F32))
        cf = ctx.enter_context(nc.sbuf_tensor("d_cf", [B, 2, T], F32))
        block = ctx.enter_context(nc.Block())

        @block.sync
        def _(eng):
            eng.dma_start(us[:, :], usum).then_inc(s.in_a, 16)
            eng.wait_ge(s.aggr, 1)
            eng.dma_start(coef.rearrange("q b t -> b q t"), cf[:, :, :]).then_inc(s.y_out0, 16)
            eng.wait_ge(s.y_out0, 16)

        @block.vector
        def _(dve):
            ve = nc.vector
            c = Chain(dve, s.step)
            dve.wait_ge(s.in_a, 16)
            c.then(ve.tensor_tensor_scan(sg[:, :], us[:, :], us[:, :], 0.0, ALU.max, ALU.max))
            c.then(ve.tensor_scalar(sg[:, :], sg[:, :], 0.0, None, ALU.is_gt))
            c.then(ve.tensor_copy(sm[:, 0:1], us[:, 0:1]))
            for sweep in range(5):
                c.then(ve.scalar_tensor_tensor(out=sm[:, 1:T], in0=sg[:, 0:T - 1], scalar=DECAY, in1=us[:, 1:T],
                                               op0=ALU.mult, op1=ALU.add))
                c.then(ve.tensor_scalar(sg[:, :], sm[:, :], 1e12, 1.0, ALU.mult, ALU.min))
            c.then(ve.scalar_tensor_tensor(out=sm[:, 1:T], in0=sg[:, 0:T - 1], scalar=DECAY, in1=us[:, 1:T],
                                           op0=ALU.mult, op1=ALU.add))
            c.then(ve.tensor_scalar(sm[:, :], sm[:, :], 1e-12, None, ALU.max))
            c.then(ve.reciprocal(cf[:, 0, :], sm[:, :]))
            c.then(ve.tensor_scalar(cf[:, 1, :], cf[:, 0, :], DECAY, None, ALU.mult))
            c.then(ve.memset(cf[:, 1, 0:1], 0.0))
            dve.sem_inc(s.aggr, 1)


def ticks(eng, n, body):
    for k in range(4):
        body(k, k % 2, k // 2)
    if n > 6:
        with eng.Fori(2, n // 2 - 1) as m:
            body(2 * m, 0, m)
            body(2 * m + 1, 1, m)
    for k in range(max(4, n - 2), n + 2):
        body(k, k % 2, k // 2)


def attention_phase(nc, sems, W, h_img, txt, coef, le_dram, e2t_dram):
    s = sems
    T, B, D = W["e"].shape
    NB = 8
    n, HT, CT = B // NB, 4 * T, NB * T
    READ, VALUE, ROW = (slice(NB * j, NB * j + NB) for j in range(3))
    NORM = 8
    with ExitStack() as ctx:
        def sb(name, shape):
            return ctx.enter_context(nc.sbuf_tensor("at_" + name, shape, F32))

        cf = sb("cf", [P, 2, 2, CT])
        x = sb("x", [P, 2, 2, CT])
        hb = sb("h", [T, 2, NB, D])
        sc = sb("sc", [T, CT])
        la = sb("la", [T, NB, D])
        lat = sb("lat", [D, CT])
        y = sb("y", [P, 2, CT])
        vn = sb("vn", [T, NB, D])
        e2 = sb("e2", [T, NB, D])
        e2t = sb("e2t", [D, 2, CT])
        le = sb("le", [T, 2, NB, D])
        st = sb("st", [T, 3 * NB, 6])
        w = sb("w", [T, 2, 6, 3 * NB])
        ps_s = [ctx.enter_context(nc.psum_tensor(f"at_ps{b}", [T, CH], F32)) for b in range(2)]
        ps_a = ctx.enter_context(nc.psum_tensor("at_pa", [T, CH], F32))
        ps_t = [ctx.enter_context(nc.psum_tensor(f"at_pt{b}", [T, CH], F32)) for b in range(2)]
        ps_y = [ctx.enter_context(nc.psum_tensor(f"at_py{b}", [P, CH], F32)) for b in range(2)]
        ps_v = ctx.enter_context(nc.psum_tensor("at_pv", [T, CH], F32))
        logits = ps_t[1][:, HT:HT + 8 * NB]
        cf_in, h_in, le_in, e_out = [s.u_in0, s.u_in1], [s.y_in0, s.y_in1], [s.sp_out0, s.sp_out1], [s.u_out0, s.u_out1]
        block = ctx.enter_context(nc.Block())

        def valid(step):
            return not isinstance(step, int) or 0 <= step < n

        @block.sync
        def _(eng):
            hv = h_img.rearrange("(n a) g (t d) -> n t (a g) d", a=NB // G, d=D)
            tv = txt.rearrange("(n b) t d -> n t b d", b=NB)

            def body(k, par, r):
                if valid(k):
                    at_least(eng, s.bn_done, 2 * (k - 1))
                    for q in range(2):
                        eng.dma_start(cf[:, par, q, :], coef[q].rearrange("(n o b) t -> n o (b t)", o=1, b=NB)[k]
                                      .broadcast_to([P, CT])).then_inc(cf_in[par], 16)
                    at_least(eng, s.fx_done, k - 1)
                    eng.dma_start(le[:, par], le_dram[:, bass.ds(NB * k, NB), :]).then_inc(le_in[par], 16)
                j = k - 2
                if valid(j):
                    at_least(eng, s.uo_ready, j - 1)
                    eng.nop(nofuse=True)
                    at_least(eng, s.pw_done, 2 * (j - 1))
                    eng.nop(nofuse=True)
                    eng.dma_start(hb[0:S, par], hv[j]).then_inc(h_in[par], 16)
                    eng.dma_start(hb[S:T, par], tv[j]).then_inc(h_in[par], 16)

            ticks(eng, n, body)

        @block.gpsimd
        def _(pool):
            gp = nc.gpsimd

            def scale(j, par, r):
                pool.wait_ge(cf_in[par], 32 * r + 32)
                for q in range(2):
                    xq = W["x"][:, q, bass.ds(CT * j, CT)]
                    gp.tensor_tensor(xq, xq, cf[:, par, 0, :], ALU.mult).then_inc(s.a_ready, 1)

            def body(k, par, r):
                j = k - 2
                if valid(j):
                    pool.wait_ge(s.step, NORM * (k + 1))
                    at_least(pool, s.tt_done, 2 * j)
                    gp.tensor_tensor(e2[:, :, :], hb[:, par], spread_over(w[:, par, 0, ROW], D), ALU.subtract)\
                        .then_inc(s.pw_done, 1)
                    pool.wait_ge(s.pw_done, 2 * j + 1)
                    gp.tensor_tensor(e2[:, :, :], e2[:, :, :], spread_over(w[:, par, 5, ROW], D), ALU.mult)\
                        .then_inc(s.pw_done, 1)
                j = k - 1
                if valid(j):
                    pool.wait_ge(h_in[1 - par], 32 * (r + par))
                    pool.wait_ge(s.hq_done, 2 * j + 2)
                    gp.tensor_tensor(hb[:, 1 - par], hb[:, 1 - par], vn[:, :, :], ALU.add).then_inc(s.hq_ready, 1)
                if valid(k + 2):
                    scale(k + 2, par, r + 1)

            scale(0, 0, 0)
            scale(1, 1, 0)
            ticks(pool, n, body)

        @block.scalar
        def _(act):
            def body(k, par, r):
                act.wait_ge(s.aggr, k + 1)
                nc.scalar.activation(w[:, par, 4], w[:, par, 3], ACT.Sqrt).then_inc(s.act_step, 1)
                if valid(k):
                    at_least(act, s.mix_done, 4 * k)
                    for q in range(2):
                        act.wait_ge(s.t2_done, 2 * k + q + 1)
                        nc.scalar.copy(lat[:, HT * q:HT * q + HT], ps_t[q][0:D, 0:HT]).then_inc(s.a2_ready, 1)
                j = k - 2
                if valid(j):
                    act.wait_ge(s.hq_ready, j + 1)
                    nc.scalar.copy(W["h2"][:, bass.ds(NB * j, NB), :], hb[:, par]).then_inc(s.uo_ready, 1)
                    at_least(act, e_out[par], 16 * (r - 1))
                    for q in range(2):
                        act.wait_ge(s.tt_done, 2 * j + q + 1)
                        nc.scalar.copy(e2t[:, par, HT * q:HT * q + HT], ps_t[q][0:D, 0:HT]).then_inc(s.t_ready, 1)
                    act.wait_ge(s.t_ready, 2 * j + 2)
                    act.dma_start(e2t_dram[:, bass.ds(CT * j, CT)], e2t[:, par, :]).then_inc(e_out[par], 16)
                    act.wait_ge(s.um_done, j + 1)
                    nc.scalar.copy(W["gate"][:, bass.ds(NB * j, NB), :], logits.rearrange("p (b e) -> p b e", b=NB))\
                        .then_inc(s.sp_ready, 1)

            ticks(act, n, body)
            act.wait_ge(s.u_out0, 8 * n)
            act.wait_ge(s.u_out1, 8 * n)

        @block.vector
        def _(dve):
            ve = nc.vector

            def stats(src, cols):
                for b in range(NB):
                    ve.bn_stats(st[:, cols.start + b, :], src[:, b, :]).then_inc(s.st_done, 1)

            def stats_count(k):
                if isinstance(k, int) and (k == 0 or k >= n):
                    return NB if k == 0 else 3 * NB * n - NB * (n + 1 - k)
                return 3 * NB * k

            def norm(src, out, par, cols, sem, j):
                ve.tensor_tensor(out[:, :, :], src, spread_over(w[:, par, 0, cols], D), ALU.subtract).then_inc(sem, 1)
                dve.wait_ge(sem, 2 * j + 1)
                ve.tensor_tensor(out[:, :, :], out[:, :, :], spread_over(w[:, par, 5, cols], D), ALU.mult)\
                    .then_inc(sem, 1)

            def scan(j, par):
                for q in range(2):
                    dve.wait_ge(s.a_ready, 2 * j + q + 1)
                    at_least(dve, s.ix_done, j - 1)
                    ve.tensor_tensor_scan(x[:, par, q, :], cf[:, par, 1, :], W["x"][:, q, bass.ds(CT * j, CT)], 0.0,
                                          ALU.mult, ALU.add).then_inc(s.bn_done, 1)

            def decay_scores(j):
                decay = W["decay"][:, :].rearrange("s (o t) -> s o t", o=1).broadcast_to([T, 4, T])
                for q in range(2):
                    dve.wait_ge(s.fy_done, 2 * j + q + 1)
                    ve.tensor_tensor(sc[:, HT * q:HT * q + HT].rearrange("s (b t) -> s b t", b=4),
                                     ps_s[q][:, 0:HT].rearrange("s (b t) -> s b t", b=4), decay, ALU.mult)\
                        .then_inc(s.s_ready, 1)

            def outputs(k, par, q):
                for hh in range(2):
                    cols = slice(HT * hh, HT * hh + HT)
                    dve.wait_ge(s.mix_done, 4 * k + 2 * q + hh + 1)
                    ve.scalar_tensor_tensor(out=y[:, q, cols], in0=ps_y[hh][:, 0:HT], scalar=0.0,
                                            in1=x[:, par, q, cols], op0=ALU.max, op1=ALU.mult).then_inc(s.mix_low, 1)

            def body(k, par, r):
                if valid(k - 2):
                    dve.wait_ge(s.hq_ready, k - 1)
                    stats(hb[:, par], ROW)
                if valid(k):
                    dve.wait_ge(s.fx_done, k + 1)
                    stats(ps_a[:, :].rearrange("t (b d) -> t b d", b=NB), READ)
                if valid(k - 1):
                    dve.wait_ge(s.ix_done, k)
                    stats(ps_v[:, :].rearrange("t (b d) -> t b d", b=NB), VALUE)
                dve.wait_ge(s.st_done, stats_count(k))
                at_least(dve, s.pw_done, 2 * (k - 3))
                c = Chain(dve, s.step, NORM * k)
                norm_statistics(nc, c, st, w[:, par])
                dve.sem_inc(s.aggr, 1)
                dve.wait_ge(s.act_step, k + 1)
                c.then(ve.reciprocal(w[:, par, 5], w[:, par, 4]))
                assert c.n == NORM
                if valid(k):
                    norm(ps_a[:, :].rearrange("t (b d) -> t b d", b=NB), la, par, READ, s.vt_ready, k)
                if valid(k + 1):
                    scan(k + 1, 1 - par)
                j = k - 1
                if valid(j):
                    at_least(dve, s.hq_ready, j)
                    norm(ps_v[:, :].rearrange("t (b d) -> t b d", b=NB), vn, par, VALUE, s.hq_done, j)
                if valid(k):
                    outputs(k, par, 0)
                if valid(k + 1):
                    decay_scores(k + 1)
                if valid(k):
                    outputs(k, par, 1)

            ve.memset(st[:, :, :], 0.0).then_inc(s.w_fix, 1)
            ve.memset(w[:, :, :, :], 1.0).then_inc(s.w_fix, 1)
            dve.wait_ge(s.w_fix, 2)
            scan(0, 0)
            decay_scores(0)
            ticks(dve, n, body)

        @block.tensor
        def _(pe):
            def transposes(src, done):
                for q in range(2):
                    for b in range(4):
                        ins = nc.tensor.transpose(ps_t[q][0:D, T * b:T * b + T], src[:, 4 * q + b, :], W["eye"][0:T, 0:T])
                    ins.then_inc(done, 1)

            def scores(j, par):
                pe.wait_ge(s.bn_done, 2 * j + 2)
                at_least(pe, s.s_ready, 2 * j)
                for q in range(2):
                    for b in range(4):
                        t = HT * q + T * b
                        for half in range(2):
                            xb = x[:, par, half, t:t + T]
                            ins = nc.tensor.matmul(ps_s[q][:, T * b:T * b + T], xb, xb, start=(half == 0), stop=(half == 1))
                    ins.then_inc(s.fy_done, 1)

            def reads(j, par, r):
                pe.wait_ge(s.s_ready, 2 * j + 2)
                pe.wait_ge(le_in[par], 16 * r + 16)
                at_least(pe, s.vt_ready, 2 * j - 1)
                for b in range(NB):
                    ins = nc.tensor.matmul(ps_a[:, D * b:D * b + D], sc[:, T * b:T * b + T],
                                           le[:, par, b, :], start=True, stop=True)
                ins.then_inc(s.fx_done, 1)

            def body(k, par, r):
                j = k - 2
                if valid(k):
                    pe.wait_ge(s.vt_ready, 2 * k + 2)
                    at_least(pe, s.t_ready, 2 * (k - 2))
                    pe.nop(nofuse=True)
                    transposes(la, s.t2_done)
                    for hh in range(2):
                        pe.wait_ge(s.a2_ready, 2 * k + hh + 1)
                        at_least(pe, s.mix_low, 4 * k + hh - 1)
                        nc.tensor.matmul(ps_y[hh][:, 0:HT], W["DyT"][:, 0:P], lat[:, HT * hh:HT * hh + HT],
                                         start=True, stop=True).then_inc(s.mix_done, 1)
                if valid(k + 1):
                    scores(k + 1, 1 - par)
                if valid(k):
                    for hh in range(2):
                        pe.wait_ge(s.mix_low, 4 * k + hh + 1)
                        nc.tensor.matmul(ps_y[hh][:, 0:HT], W["DyT"][:, P:2 * P], lat[:, HT * hh:HT * hh + HT],
                                         start=True, stop=True).then_inc(s.mix_done, 1)
                if valid(j):
                    pe.wait_ge(s.pw_done, 2 * j + 2)
                    if valid(k):
                        pe.wait_ge(s.a2_ready, 2 * k + 2)
                    else:
                        at_least(pe, s.t_ready, 2 * j)
                    at_least(pe, s.sp_ready, j)
                    pe.nop(nofuse=True)
                    transposes(e2, s.tt_done)
                if valid(k + 1):
                    reads(k + 1, 1 - par, r + par)
                if valid(k):
                    pe.wait_ge(s.mix_low, 4 * k + 4)
                    at_least(pe, s.hq_done, 2 * k - 1)
                    for b in range(NB):
                        for q in range(2):
                            ins = nc.tensor.matmul(ps_v[:, D * b:D * b + D], y[:, q, T * b:T * b + T], W["ET"][:, q, :],
                                                   start=(q == 0), stop=(q == 1))
                    ins.then_inc(s.ix_done, 1)
                if valid(j):
                    pe.wait_ge(s.t_ready, 2 * j + 2)
                    for b in range(NB):
                        ins = nc.tensor.matmul(logits[:, 8 * b:8 * b + 8], e2t[:, par, T * b:T * b + T], W["Wr"][:, :],
                                               start=True, stop=True)
                    ins.then_inc(s.um_done, 1)

            scores(0, 0)
            reads(0, 0, 0)
            ticks(pe, n, body)


def gate_phase(nc, sems, W, d, gates):
    s = sems
    T, B, D = W["e"].shape
    E = 8
    with ExitStack() as ctx:
        def sb(name, shape):
            return ctx.enter_context(nc.sbuf_tensor("g_" + name, shape, F32))

        p, q, first, tmp = (sb(x, [T, B, E]) for x in ("p", "q", "first", "tmp"))
        m = sb("m", [T, 4, B])
        b2 = sb("b2", [P, 16, D])
        b2s = sb("b2s", [T, D])
        GB = B // 16
        mt = sb("mt", [P, GB, T])
        rank = sb("rank", [T, E])
        pt = [ctx.enter_context(nc.psum_tensor(f"g_pt{b}", [P, CH], F32)) for b in range(2)]
        pb = [ctx.enter_context(nc.psum_tensor(f"g_pb{b}", [T, CH], F32)) for b in range(4)]
        gate = W["gate"]
        block = ctx.enter_context(nc.Block())

        def per_token(j):
            return m[:, j, :].rearrange("p (n o) -> p n o", o=1).broadcast_to([T, B, E])

        def store_gates(eng, odd, done):
            for t in range(GB):
                eng.wait_ge(s.vt_ready, t + 1)
                for e in range(odd, E, 2):
                    eng.dma_start(gates[e, 16 * t:16 * t + 16, :], mt[e::E, t, :]).then_inc(done, 16)
            eng.wait_ge(done, 16 * GB * E // 2)

        @block.sync
        def _(eng):
            eng.dma_start(b2s[:, :], d["b2s"].rearrange("(o d) -> o d", o=1).broadcast_to([T, D])).then_inc(s.in_a, 16)
            eng.wait_ge(s.w_fix, 1)
            for b in range(16):
                eng.dma_start(b2[E * b:E * b + E, b, :], d["b2p"]).then_inc(s.w_in, 16)
            store_gates(eng, 0, s.y_out0)

        @block.gpsimd
        def _(pool):
            nc.gpsimd.memset(b2[:, :, :], 0.0).then_inc(s.w_fix, 1)

        @block.scalar
        def _(act):
            act.wait_ge(s.aggr, 1)
            nc.scalar.activation(p[:, :, :], q[:, :, :], ACT.Exp).then_inc(s.act_step, 1)
            store_gates(act, 1, s.y_out1)

        @block.tensor
        def _(pe):
            pe.wait_ge(s.w_in, 256)
            pe.wait_ge(s.aggr, 2)
            for t in range(B // 16):
                at_least(pe, s.vt_ready, t - 1)
                nc.tensor.transpose(pt[t % 2][:, 0:T], gate[:, 16 * t:16 * t + 16, :].rearrange("p b e -> p (b e)"),
                                    W["eye"][0:T, 0:T]).then_inc(s.tr_done, 1)
                pe.wait_ge(s.vt_ready, t + 1)
                at_least(pe, s.st_done, 2 * t - 2)
                for hh in range(2):
                    ins = nc.tensor.matmul(pb[2 * (t % 2) + hh][:, :], mt[:, t, :],
                                           b2[:, 8 * hh:8 * hh + 8, :].rearrange("p b d -> p (b d)"), start=True, stop=True)
                ins.then_inc(s.fx_done, 1)

        @block.vector
        def _(dve):
            ve = nc.vector
            c = Chain(dve, s.step)
            for e in range(E):
                c.then(ve.memset(rank[:, e:e + 1], float(E - e)))
            ranks = rank[:, :].rearrange("p (o e) -> p o e", o=1).broadcast_to([T, B, E])
            c.then(ve.tensor_reduce(m[:, 0, :], gate[:, :, :], AX.X, ALU.max))
            c.then(ve.tensor_tensor(q[:, :, :], gate[:, :, :], per_token(0), ALU.subtract))
            dve.sem_inc(s.aggr, 1)
            dve.wait_ge(s.act_step, 1)
            c.then(ve.tensor_reduce(m[:, 0, :], p[:, :, :], AX.X, ALU.add))
            c.then(ve.reciprocal(m[:, 1, :], m[:, 0, :]))
            c.then(ve.tensor_tensor(p[:, :, :], p[:, :, :], per_token(1), ALU.mult))
            for k in range(2):
                c.then(ve.tensor_reduce(m[:, 2 + k, :], p[:, :, :], AX.X, ALU.max))
                c.then(ve.tensor_tensor(q[:, :, :], p[:, :, :], per_token(2 + k), ALU.is_equal))
                c.then(ve.tensor_tensor(q[:, :, :], q[:, :, :], ranks, ALU.mult))
                c.then(ve.tensor_reduce(m[:, 0, :], q[:, :, :], AX.X, ALU.max))
                c.then(ve.tensor_tensor(q[:, :, :], ranks, per_token(0), ALU.is_equal))
                c.then(ve.tensor_tensor(tmp[:, :, :], q[:, :, :], per_token(2 + k), ALU.mult))
                if k == 0:
                    c.then(ve.tensor_copy(first[:, :, :], tmp[:, :, :]))
                    c.then(ve.scalar_tensor_tensor(out=p[:, :, :], in0=q[:, :, :], scalar=-2.0, in1=p[:, :, :],
                                                   op0=ALU.mult, op1=ALU.add))
            c.then(ve.tensor_tensor(tmp[:, :, :], tmp[:, :, :], first[:, :, :], ALU.add))
            c.then(ve.tensor_tensor(m[:, 0, :], m[:, 2, :], m[:, 3, :], ALU.add))
            c.then(ve.reciprocal(m[:, 1, :], m[:, 0, :]))
            c.then(ve.tensor_tensor(gate[:, :, :], tmp[:, :, :], per_token(1), ALU.mult))
            dve.sem_inc(s.aggr, 1)
            dve.wait_ge(s.in_a, 16)
            h2 = W["h2"]
            c.then(ve.tensor_tensor(h2[:, :, :], h2[:, :, :],
                                    b2s[:, :].rearrange("p (o d) -> p o d", o=1).broadcast_to([T, B, D]), ALU.add))
            for t in range(B // 16):
                dve.wait_ge(s.tr_done, t + 1)
                at_least(dve, s.fx_done, t - 1)
                ve.tensor_copy(mt[:, t, :], pt[t % 2][:, 0:T]).then_inc(s.vt_ready, 1)
                dve.wait_ge(s.fx_done, t + 1)
                for hh in range(2):
                    rows = h2[:, 16 * t + 8 * hh:16 * t + 8 * hh + 8, :]
                    ve.tensor_tensor(rows, rows, pb[2 * (t % 2) + hh][:, :].rearrange("p (b d) -> p b d", b=8), ALU.add)\
                        .then_inc(s.st_done, 1)


def expert_phase(nc, sems, W, d, out, e2t_dram, gates):
    s = sems
    T, B, D = W["e"].shape
    E, NB = 8, 4
    n, CT = B // NB, NB * T
    F = 2 * P
    TILES = 2 * (E + 1)
    SPLITS = 6
    with ExitStack() as ctx:
        def sb(name, shape, dt=F32):
            return ctx.enter_context(nc.sbuf_tensor("x_" + name, shape, dt))

        w1 = sb("w1", [P, E + 1, F])
        w11, w22, w31 = (sb(x, [P, E + 1, F], BF16) for x in ("w11", "w22", "w31"))
        w2 = sb("w2", [P, E + 1, 2, D])
        b1 = sb("b1", [P, E + 1, 2])
        et = sb("et", [P, 2, CT])
        x12, x13 = (sb(x, [P, 2, CT], BF16) for x in ("x12", "x13"))
        mask = sb("mask", [P, 2, E, CT])
        ht = sb("ht", [P, 6, CT])
        total = sb("total", [P, CT])
        units = sb("units", [P, D])
        res = sb("res", [T, 2, NB, D])
        ps_h = [ctx.enter_context(nc.psum_tensor(f"x_ph{b}", [P, CH], F32)) for b in range(4)]
        ps_e = [ctx.enter_context(nc.psum_tensor(f"x_pe{b}", [P, CH], F32)) for b in range(2)]
        ps_r = ctx.enter_context(nc.psum_tensor("x_pr", [T, CH], F32))
        o_out, e_in, m_in = [s.u_out0, s.u_out1], [s.u_in0, s.u_in1], [s.y_in0, s.y_in1]
        block = ctx.enter_context(nc.Block())

        @block.sync
        def _(eng):
            for half in range(2):
                rows = slice(D * half, D * half + D)
                eng.dma_start(w1[rows, 0, :], d["W1s"]).then_inc(s.w_in, 16)
                eng.dma_start(w1[rows, 1:, :], d["W1p"].rearrange("e d f -> d e f")).then_inc(s.w_in, 16)
            for half in range(2):
                eng.dma_start(units[D * half:D * half + D, :], d["eye"][0:D, 0:D]).then_inc(s.const_in, 16)
            ov = out.rearrange("(n b) t d -> n t b d", b=NB)

            def store(i, par):
                eng.wait_ge(s.uo_ready, i + 1)
                eng.dma_start(ov[i], res[:, par]).then_inc(o_out[par], 16)

            def body(i, par, r, last):
                at_least(eng, s.bn_done, SPLITS * (i - 1))
                for half in range(2):
                    eng.dma_start(et[D * half:D * half + D, par, :], e2t_dram[:, bass.ds(CT * i, CT)])\
                        .then_inc(e_in[par], 16)
                at_least(eng, s.t_ready, 2 * E * (i - 1))
                eng.dma_start(mask[:, par], gates.rearrange("(o e) (n b) t -> n o e (b t)", o=1, b=NB)[i]
                              .broadcast_to([P, E, CT])).then_inc(m_in[par], 16)
                if not (isinstance(i, int) and i < 2):
                    store(i - 2, par)

            walk(eng, n, body)
            store(n - 2, 0)
            store(n - 1, 1)
            eng.wait_ge(s.u_out0, 8 * n)
            eng.wait_ge(s.u_out1, 8 * n)

        @block.gpsimd
        def _(pool):
            def body(i, par, r, last):
                pool.wait_ge(e_in[par], 32 * r + 32)
                at_least(pool, s.fy_done, TILES * (i - 1))
                x, a12, a13, gp = et[:, par, :], x12[:, par, :], x13[:, par, :], nc.gpsimd
                c = Chain(pool, s.bn_done, SPLITS * i)
                pool.nop(nofuse=True)
                c.then(gp.tensor_copy(a12, x))
                pool.nop(nofuse=True)
                c.then(gp.tensor_copy(a13[0:D], a12[0:D]))
                c.then(gp.tensor_tensor(x[D:P], x[D:P], a12[D:P], ALU.subtract))
                pool.nop(nofuse=True)
                c.then(gp.tensor_copy(a12[D:P], x[D:P]))
                c.then(gp.tensor_tensor(x[D:P], x[D:P], a12[D:P], ALU.subtract))
                pool.nop(nofuse=True)
                c.then(gp.tensor_copy(a13[D:P], x[D:P]))
                assert c.n == SPLITS

            walk(pool, n, body)

        @block.scalar
        def _(act):
            act.dma_start(w2[:, 0], d["W2s"].rearrange("(t p) d -> p t d", p=P)).then_inc(s.w_tmp, 16)
            for e in range(E):
                act.dma_start(w2[:, 1 + e], d["W2p"][e].rearrange("(t p) d -> p t d", p=P)).then_inc(s.w_tmp, 16)
            with nc.allow_non_contiguous_dma("biases to partitions"):
                act.dma_start(b1[:, 0, :], d["b1s"].rearrange("(t p) -> p t", p=P)).then_inc(s.w_tmp, 16)
                act.dma_start(b1[:, 1:, :].rearrange("p e t -> p (e t)"),
                              d["b1p"].rearrange("e (t p) -> p (e t)", p=P)).then_inc(s.w_tmp, 16)
            act.wait_ge(s.w_tmp, 16 * 11)

            def body(i, par, r, last):
                for j in range(TILES):
                    t = TILES * i + j
                    act.wait_ge(s.fy_done, t + 1)
                    if j % 2 == 0 and not (isinstance(i, int) and i == 0 and j < 6):
                        act.wait_ge(s.fx_done, (E + 1) * i + j // 2 - 2)
                    nc.scalar.activation(ht[:, j % 6, :], ps_h[(2 * par + j) % 4][:, 0:CT], ACT.Gelu,
                                         bias=b1[:, j // 2, j % 2:j % 2 + 1]).then_inc(s.a_ready, 1)

            walk(act, n, body)

        @block.vector
        def _(dve):
            ve = nc.vector
            dve.wait_ge(s.w_in, 64)
            for e in range(E + 1):
                wx, b1x, b2x, b3x = w1[:, e, :], w11[:, e, :], w22[:, e, :], w31[:, e, :]
                c = Chain(dve, s.step, 6 * e)
                c.then(ve.tensor_copy(b1x, wx))
                c.then(ve.tensor_tensor(wx, wx, b1x, ALU.subtract))
                c.then(ve.tensor_copy(b2x, wx))
                c.then(ve.tensor_tensor(wx[0:D], wx[0:D], b2x[0:D], ALU.subtract))
                c.then(ve.tensor_copy(b3x[0:D], wx[0:D]))
                c.then(ve.tensor_copy(b3x[D:P], b1x[D:P]))

            def totals(i, par):
                dve.wait_ge(s.fx_done, (E + 1) * (i + 1))
                at_least(dve, s.um_done, i)
                ve.tensor_copy(total[:, :], ps_e[par][:, 0:CT]).then_inc(s.s_ready, 1)

            def rows(i, par, r):
                dve.wait_ge(s.um_done, i + 1)
                if not (isinstance(i, int) and i < 2):
                    dve.wait_ge(o_out[par], 16 * r)
                ve.tensor_tensor(res[:, par], W["h2"][:, bass.ds(NB * i, NB), :],
                                 ps_r[:, 0:NB * D].rearrange("p (b d) -> p b d", b=NB), ALU.add).then_inc(s.uo_ready, 1)

            def body(i, par, r, last):
                dve.wait_ge(m_in[par], 16 * r + 16)
                later = not (isinstance(i, int) and i == 0)
                for j in range(2, TILES):
                    dve.wait_ge(s.a_ready, TILES * i + j + 1)
                    h = ht[:, j % 6, :]
                    ve.tensor_tensor(h, h, mask[:, par, j // 2 - 1, :], ALU.mult).then_inc(s.t_ready, 1)
                    if j == 6 and later:
                        totals(i - 1, 1 - par)
                    if j == 10 and later:
                        rows(i - 1, 1 - par, r - 1 + par)
                if last:
                    totals(i, par)
                    rows(i, par, r)

            walk(dve, n, body)

        @block.tensor
        def _(pe):
            def hidden(i, par, r, j):
                t, e = TILES * i + j, j // 2
                first = isinstance(i, int) and i == 0
                if j == 0:
                    pe.wait_ge(s.bn_done, SPLITS * (i + 1))
                if first and j % 2 == 0:
                    pe.wait_ge(s.step, 6 * (e + 1))
                if not (first and j < 4):
                    pe.wait_ge(s.a_ready, t - 3)
                cols = slice(P * (j % 2), P * (j % 2) + P)
                o = ps_h[(2 * par + j) % 4][:, 0:CT]
                nc.tensor.matmul(o, w31[:, e, cols], x13[:, par, :], start=True, stop=False)
                nc.tensor.matmul(o, w22[:, e, cols], x12[:, par, :], start=False, stop=False)
                nc.tensor.matmul(o, w11[:, e, cols], x12[:, par, :], start=False, stop=True).then_inc(s.fy_done, 1)

            def outputs(i, par, e):
                if e == 0:
                    pe.wait_ge(s.a_ready, TILES * i + 2)
                    at_least(pe, s.s_ready, i - 1)
                else:
                    pe.wait_ge(s.t_ready, 2 * E * i + 2 * e)
                for half in range(2):
                    ins = nc.tensor.matmul(ps_e[par][D * half:D * half + D, 0:CT], w2[:, e, half, :],
                                           ht[:, (2 * e + half) % 6, :], start=(e == 0), stop=(e == E),
                                           skip_group_check=True)
                ins.then_inc(s.fx_done, 1)

            def turn(i):
                pe.wait_ge(s.s_ready, i + 1)
                at_least(pe, s.uo_ready, i)
                for b in range(NB):
                    ins = nc.tensor.matmul(ps_r[:, D * b:D * b + D], total[:, T * b:T * b + T], units[:, :],
                                           start=True, stop=True)
                ins.then_inc(s.um_done, 1)

            def body(i, par, r, last):
                later = not (isinstance(i, int) and i == 0)
                for e in range(E + 1):
                    hidden(i, par, r, 2 * e)
                    hidden(i, par, r, 2 * e + 1)
                    if e >= 2:
                        outputs(i, par, e - 2)
                    elif later:
                        outputs(i - 1, 1 - par, E + e - 1)
                    if e == 4 and later:
                        turn(i - 1)
                if last:
                    outputs(i, par, E - 1)
                    outputs(i, par, E)
                    turn(i)

            pe.wait_ge(s.w_tmp, 16 * 11)
            pe.wait_ge(s.const_in, 32)
            walk(pe, n, body)


def tokens(nc, ctx, sems, d, h_img, out):
    B, L, D = d["txt"].shape
    T = S + L

    def sb(name, shape, c=ctx):
        return c.enter_context(nc.sbuf_tensor("w_" + name, shape, F32))

    usum = nc.dram_tensor("update_sums", (B, T), F32).ap()
    coef = nc.dram_tensor("state_coefficients", (2, B, T), F32).ap()
    le_dram = nc.dram_tensor("normed_rows", (T, B, D), F32).ap()
    e2t_dram = nc.dram_tensor("expert_inputs", (D, B * T), F32).ap()
    gates = nc.dram_tensor("expert_weights", (8, B, T), F32).ap()
    W = {"gate": sb("gate", [T, B, 8]), "Wr": sb("Wr", [D, 8]), "eye": sb("eye", [P, P]), "h2": sb("h2", [T, B, D])}
    W["e"] = W["h2"]
    with nc.Block() as block:
        @block.sync
        def _(eng):
            eng.dma_start(W["Wr"][:, :], d["Wr"]).then_inc(sems.const_in, 16)
            eng.dma_start(W["eye"][:, :], d["eye"]).then_inc(sems.const_in, 16)
            eng.wait_ge(sems.const_in, 32)
    end_phase(nc, sems)
    with ExitStack() as c:
        for name, shape in (("DxT", [D, 2 * P]), ("DyT", [D, 2 * P]), ("ET", [P, 2, D]), ("decay", [T, T]), ("ones", [P, 1])):
            W[name] = sb(name, shape, c)
        token_norm_phase(nc, sems, W, h_img, d["txt"], d, le_dram)
        end_phase(nc, sems)
        W["x"] = sb("x", [P, 2, B * T], c)
        update_phase(nc, sems, W, usum)
        end_phase(nc, sems)
        decay_phase(nc, sems, usum, coef)
        end_phase(nc, sems)
        attention_phase(nc, sems, W, h_img, d["txt"], coef, le_dram, e2t_dram)
        end_phase(nc, sems)
    gate_phase(nc, sems, W, d, gates)
    end_phase(nc, sems)
    expert_phase(nc, sems, W, d, out, e2t_dram, gates)
    end_phase(nc, sems)

def program(nc, d, out):
    B = d["x"].shape[0]
    h_img = nc.dram_tensor("image_rows", (B // G, G, PX), F32).ap()
    with ExitStack() as ctx:
        sems = Semaphores(ctx, nc)
        with ExitStack() as c:
            operator(nc, c, sems, d, h_img)
        tokens(nc, ctx, sems, d, h_img, out)


INPUTS = ("x", "txt", "L0_tok_p_w", "L0_tok_p_b", "L0_tok_fw1", "L0_tok_fw2", "L0_tok_w_w", "L0_tok_w_b", "L0_tok_bn_g",
          "L0_tok_bn_b", "L0_tok_q_w", "L0_tok_q_b", "L0_attn_E", "L0_attn_Dx", "L0_attn_Dy", "L0_ffn_Wr", "L0_ffn_W1s",
          "L0_ffn_b1s", "L0_ffn_W2s", "L0_ffn_b2s", "L0_ffn_W1p", "L0_ffn_b1p", "L0_ffn_W2p", "L0_ffn_b2p")


def kernel(**inputs):
    from concourse import bacc
    from concourse.bass_utils import run_bass_kernel_spmd

    nc = bacc.Bacc("TRN2", target_bir_lowering=False, num_devices=1)
    arrays, d = {}, {}
    named = [(n, n.split("_", 2)[2] if n.startswith("L0_") else n, inputs[n]) for n in INPUTS]
    B, L, D = inputs["txt"].shape
    consts = {**shape_constants(), **token_constants(S + L, D)}
    named += [("const_" + n, n, a) for n, a in consts.items()]
    for full, short, a in named:
        a = np.ascontiguousarray(a)
        arrays[f"in_{full}_dram"] = a
        d[short] = nc.dram_tensor(f"in_{full}_dram", a.shape, mybir.dt.from_np(a.dtype), kind="ExternalInput").ap()
    out = nc.dram_tensor("out_0_dram", (B, S + L, D), F32, kind="ExternalOutput").ap()
    program(nc, d, out)
    r = run_bass_kernel_spmd(nc, [arrays], core_ids=[0])
    return r.results[0]["out_0_dram"]
```
